# Optimizing a Trainium2 kernel written in Bass

```python
import numpy as np
import jax
import jax.numpy as jnp

def _softmax(x, axis=-1):
    return jax.nn.softmax(x, axis=axis)

def _gelu(x):
    return jax.nn.gelu(x, approximate=True)

def _silu(x):
    return jax.nn.silu(x)

def _sigmoid(x):
    return jax.nn.sigmoid(x)

def _layernorm(x, axis=-1, eps=1e-05):
    m = jnp.mean(x, axis=axis, keepdims=True)
    v = jnp.var(x, axis=axis, keepdims=True)
    return (x - m) / jnp.sqrt(v + eps)

def _scatter_add(tgt, idx, src, axis=0):
    return tgt.at[idx].add(src)

def _segment_sum(src, seg, n):
    return jax.ops.segment_sum(src, seg, n)
kernel_name = 'mk_gps_d1_gnn_r32_f23dda'

def setup_inputs(seed: int=0):
    np.random.seed(seed)
    _w = jnp.asarray

    def _rec_inputs():
        import jax
        import jax.numpy as jnp
        _gk = jax.random.key(seed)
        x = -3.713e-06 + 0.01 * jax.random.normal(jax.random.fold_in(_gk, 1), (3125, 256), jnp.float32)
        src = jax.random.randint(jax.random.fold_in(_gk, 2), (50000,), 0, 3125, jnp.int32)
        dst = jax.random.randint(jax.random.fold_in(_gk, 3), (50000,), 0, 3125, jnp.int32)
        _o = jnp.argsort(dst, stable=True)
        src = src[_o]
        dst = dst[_o]
        return (x, src, dst)
    x, src, dst = _rec_inputs()

    def _L0_gnn_setup():
        import jax, jax.numpy as jnp
        import numpy as np
        C = 1.0
        SQC = 1.0
        MIN_NORM = 1e-15
        PROJ_EPS = 0.004

        def _norm(x):
            return jnp.clip(jnp.linalg.norm(x, axis=-1, keepdims=True), MIN_NORM)

        def logmap0(x):
            n = _norm(x)
            return jnp.arctanh(jnp.minimum(SQC * n, 1.0 - 1e-07)) * x / (SQC * n)

        def expmap0(u):
            n = _norm(u)
            return jnp.tanh(SQC * n) * u / (SQC * n)

        def proj(x):
            n = _norm(x)
            maxn = (1.0 - PROJ_EPS) / SQC
            return jnp.where(n > maxn, x / n * maxn, x)

        def mobius_add(x, y):
            x2 = jnp.sum(x * x, -1, keepdims=True)
            y2 = jnp.sum(y * y, -1, keepdims=True)
            xy = jnp.sum(x * y, -1, keepdims=True)
            num = (1.0 + 2.0 * C * xy + C * y2) * x + (1.0 - C * x2) * y
            den = 1.0 + 2.0 * C * xy + C * C * x2 * y2
            return num / jnp.clip(den, MIN_NORM)
        N, E, DIN, H, DH = (50000, 25000, 256, 4, 64)
        key = jax.random.key(seed)
        k1, k2, k3, k4, k5, k6, k7 = jax.random.split(key, 7)
        x = proj(0.01 * jax.random.normal(k1, (N, DIN), jnp.float32))
        src = jax.random.randint(k2, (E,), 0, N)
        off = jax.random.randint(k3, (E,), 1, N)
        dst = (src + off) % N
        edge_index = jnp.stack([src, dst]).astype(jnp.int64)
        glorot = float(np.sqrt(2.0 / (DIN + H * DH)))
        W = glorot * jax.random.normal(k4, (H * DH, DIN), jnp.float32)
        b_lin = 0.01 * jax.random.normal(k5, (H * DH,), jnp.float32)
        ga = float(np.sqrt(6.0 / (1 + 2 * DH)))
        att = jax.random.uniform(k6, (H, 2 * DH), jnp.float32, -ga, ga)
        b_conv = jnp.zeros((H * DH,), jnp.float32)
        return {'x': x, 'edge_index': edge_index, 'W': W, 'b_lin': b_lin, 'att': att, 'b_conv': b_conv}
    _L0_gnn_all = _L0_gnn_setup()
    _L0_gnn_in = {k: v for k, v in _L0_gnn_all.items() if k in ('W', 'b_lin', 'att', 'b_conv')}
    del _L0_gnn_all

    def _L0_mix_setup():
        import jax, jax.numpy as jnp
        import numpy as np
        B, S, D = (8, 64, 256)
        H, KD = (8, 256)
        M = 256
        EPS_LN = 1e-06
        EPS_ATT = 1e-06

        def _layernorm(x, g, b):
            mu = jnp.mean(x, axis=-1, keepdims=True)
            var = jnp.mean(jnp.square(x - mu), axis=-1, keepdims=True)
            return (x - mu) * jax.lax.rsqrt(var + EPS_LN) * g + b

        def _phi(x, proj):
            u = jnp.einsum('bshd,md->bshm', x, proj)
            sq = 0.5 * jnp.sum(jnp.square(x), axis=-1, keepdims=True)
            return jnp.exp(u - sq) * (1.0 / np.sqrt(M)) + EPS_ATT
        key = jax.random.key(seed)
        ks = jax.random.split(key, 16)
        sd = lambda *s: 1.0 / np.sqrt(s[0])
        return {'inputs': jax.random.normal(ks[0], (B, S, D), dtype=jnp.float32), 'Wq': jax.random.normal(ks[1], (D, H, KD), jnp.float32) * sd(D), 'bq': jnp.zeros((H, KD), jnp.float32), 'Wk': jax.random.normal(ks[2], (D, H, KD), jnp.float32) * sd(D), 'bk': jnp.zeros((H, KD), jnp.float32), 'Wv': jax.random.normal(ks[3], (D, H, KD), jnp.float32) * sd(D), 'bv': jnp.zeros((H, KD), jnp.float32), 'Wo': jax.random.normal(ks[4], (H, KD, D), jnp.float32) * sd(H * KD), 'bo': jnp.zeros((D,), jnp.float32), 'proj': jax.random.normal(ks[5], (M, KD), jnp.float32), 'W1': jax.random.normal(ks[6], (D, D), jnp.float32) * sd(D), 'bias1': jnp.zeros((D,), jnp.float32), 'W2': jax.random.normal(ks[7], (D, D), jnp.float32) * sd(D), 'bias2': jnp.zeros((D,), jnp.float32), 'g1': jnp.ones((D,), jnp.float32), 'beta1': jnp.zeros((D,), jnp.float32), 'g2': jnp.ones((D,), jnp.float32), 'beta2': jnp.zeros((D,), jnp.float32)}
    _L0_mix_all = _L0_mix_setup()
    _L0_mix_in = {k: v for k, v in _L0_mix_all.items() if k in ('Wq', 'bq', 'Wk', 'bk', 'Wv', 'bv', 'Wo', 'bo', 'proj', 'W1', 'bias1', 'W2', 'bias2', 'g1', 'beta1', 'g2', 'beta2')}
    del _L0_mix_all

    def _L0_ffn_setup():
        import math
        import jax, jax.numpy as jnp
        import numpy as np
        CAPACITY_FACTOR = 1.25
        key = jax.random.key(seed)
        ks = jax.random.split(key, 5)
        B, L, D, F, E = (8, 256, 256, 1024, 8)
        h = jax.random.normal(ks[0], (B, L, D), dtype=jnp.float32)
        gate_w = jax.random.normal(ks[1], (D, E), dtype=jnp.float32) * 0.02
        gate_b = jnp.zeros((E,), dtype=jnp.float32)
        w1 = jax.random.normal(ks[2], (E, D, F), dtype=jnp.float32) * (1.0 / math.sqrt(D))
        b1 = jnp.zeros((E, F), dtype=jnp.float32)
        w2 = jax.random.normal(ks[3], (E, F, D), dtype=jnp.float32) * (1.0 / math.sqrt(F))
        b2 = jnp.zeros((E, D), dtype=jnp.float32)
        return {'h': h, 'gate_w': gate_w, 'gate_b': gate_b, 'w1': w1, 'b1': b1, 'w2': w2, 'b2': b2}
    _L0_ffn_all = _L0_ffn_setup()
    _L0_ffn_in = {k: v for k, v in _L0_ffn_all.items() if k in ('gate_w', 'gate_b', 'w1', 'b1', 'w2', 'b2')}
    del _L0_ffn_all
    return {'x': x, 'src': src, 'dst': dst, 'L0_gnn_W': _L0_gnn_in['W'], 'L0_gnn_b_lin': _L0_gnn_in['b_lin'], 'L0_gnn_att': _L0_gnn_in['att'], 'L0_gnn_b_conv': _L0_gnn_in['b_conv'], 'L0_mix_Wq': _L0_mix_in['Wq'], 'L0_mix_bq': _L0_mix_in['bq'], 'L0_mix_Wk': _L0_mix_in['Wk'], 'L0_mix_bk': _L0_mix_in['bk'], 'L0_mix_Wv': _L0_mix_in['Wv'], 'L0_mix_bv': _L0_mix_in['bv'], 'L0_mix_Wo': _L0_mix_in['Wo'], 'L0_mix_bo': _L0_mix_in['bo'], 'L0_mix_proj': _L0_mix_in['proj'], 'L0_mix_W1': _L0_mix_in['W1'], 'L0_mix_bias1': _L0_mix_in['bias1'], 'L0_mix_W2': _L0_mix_in['W2'], 'L0_mix_bias2': _L0_mix_in['bias2'], 'L0_mix_g1': _L0_mix_in['g1'], 'L0_mix_beta1': _L0_mix_in['beta1'], 'L0_mix_g2': _L0_mix_in['g2'], 'L0_mix_beta2': _L0_mix_in['beta2'], 'L0_ffn_gate_w': _L0_ffn_in['gate_w'], 'L0_ffn_gate_b': _L0_ffn_in['gate_b'], 'L0_ffn_w1': _L0_ffn_in['w1'], 'L0_ffn_b1': _L0_ffn_in['b1'], 'L0_ffn_w2': _L0_ffn_in['w2'], 'L0_ffn_b2': _L0_ffn_in['b2']}

def reference(x, src, dst, L0_gnn_W, L0_gnn_b_lin, L0_gnn_att, L0_gnn_b_conv, L0_mix_Wq, L0_mix_bq, L0_mix_Wk, L0_mix_bk, L0_mix_Wv, L0_mix_bv, L0_mix_Wo, L0_mix_bo, L0_mix_proj, L0_mix_W1, L0_mix_bias1, L0_mix_W2, L0_mix_bias2, L0_mix_g1, L0_mix_beta1, L0_mix_g2, L0_mix_beta2, L0_ffn_gate_w, L0_ffn_gate_b, L0_ffn_w1, L0_ffn_b1, L0_ffn_w2, L0_ffn_b2):
    import jax
    import jax.numpy as jnp

    def _L0_gnn_ref(x, edge_index, W, b_lin, att, b_conv):
        import jax, jax.numpy as jnp
        import numpy as np
        C = 1.0
        SQC = 1.0
        MIN_NORM = 1e-15
        PROJ_EPS = 0.004

        def _norm(x):
            return jnp.clip(jnp.linalg.norm(x, axis=-1, keepdims=True), MIN_NORM)

        def logmap0(x):
            n = _norm(x)
            return jnp.arctanh(jnp.minimum(SQC * n, 1.0 - 1e-07)) * x / (SQC * n)

        def expmap0(u):
            n = _norm(u)
            return jnp.tanh(SQC * n) * u / (SQC * n)

        def proj(x):
            n = _norm(x)
            maxn = (1.0 - PROJ_EPS) / SQC
            return jnp.where(n > maxn, x / n * maxn, x)

        def mobius_add(x, y):
            x2 = jnp.sum(x * x, -1, keepdims=True)
            y2 = jnp.sum(y * y, -1, keepdims=True)
            xy = jnp.sum(x * y, -1, keepdims=True)
            num = (1.0 + 2.0 * C * xy + C * y2) * x + (1.0 - C * x2) * y
            den = 1.0 + 2.0 * C * xy + C * C * x2 * y2
            return num / jnp.clip(den, MIN_NORM)
        N, E, DIN, H, DH = (50000, 25000, 256, 4, 64)
        n = x.shape[0]
        xh = proj(expmap0(logmap0(x) @ W.T))
        hb = proj(expmap0(b_lin[None, :]))
        xh = proj(mobius_add(xh, hb))
        loop = jnp.arange(n)
        src = jnp.concatenate([edge_index[0], loop])
        dst = jnp.concatenate([edge_index[1], loop])
        logx = logmap0(xh).reshape(H, n, DH)
        s_i = jnp.einsum('hnd,hd->nh', logx, att[:, :DH])
        s_j = jnp.einsum('hnd,hd->nh', logx, att[:, DH:])
        alpha = jax.nn.leaky_relu(s_i[dst] + s_j[src], 0.2)
        m = jax.ops.segment_max(alpha, dst, num_segments=n)
        a = jnp.exp(alpha - m[dst])
        ssum = jax.ops.segment_sum(a, dst, num_segments=n)
        a = a / jnp.clip(ssum[dst], MIN_NORM)
        xj = jnp.take(logx, src, axis=1).transpose(1, 0, 2)
        out = jax.ops.segment_sum(xj * a[:, :, None], dst, num_segments=n)
        out = out.transpose(1, 0, 2).reshape(n, H * DH) + b_conv
        out = jax.nn.relu(out)
        return proj(expmap0(out))

    def _L0_mix_ref(inputs, Wq, bq, Wk, bk, Wv, bv, Wo, bo, proj, W1, bias1, W2, bias2, g1, beta1, g2, beta2):
        import jax, jax.numpy as jnp
        import numpy as np
        B, S, D = (8, 64, 256)
        H, KD = (8, 256)
        M = 256
        EPS_LN = 1e-06
        EPS_ATT = 1e-06

        def _layernorm(x, g, b):
            mu = jnp.mean(x, axis=-1, keepdims=True)
            var = jnp.mean(jnp.square(x - mu), axis=-1, keepdims=True)
            return (x - mu) * jax.lax.rsqrt(var + EPS_LN) * g + b

        def _phi(x, proj):
            u = jnp.einsum('bshd,md->bshm', x, proj)
            sq = 0.5 * jnp.sum(jnp.square(x), axis=-1, keepdims=True)
            return jnp.exp(u - sq) * (1.0 / np.sqrt(M)) + EPS_ATT
        scale = KD ** (-0.25)
        q = (jnp.einsum('bsd,dhk->bshk', inputs, Wq) + bq) * scale
        k = (jnp.einsum('bsd,dhk->bshk', inputs, Wk) + bk) * scale
        v = jnp.einsum('bsd,dhk->bshk', inputs, Wv) + bv
        phi_q = _phi(q, proj)
        phi_k = _phi(k, proj)
        kv = jnp.einsum('bshm,bshk->bhmk', phi_k, v)
        z = jnp.einsum('bshm,bhm->bsh', phi_q, phi_k.sum(axis=1))
        attn = jnp.einsum('bshm,bhmk->bshk', phi_q, kv) / z[..., None]
        attn_out = jnp.einsum('bshk,hkd->bsd', attn, Wo) + bo
        out1 = _layernorm(inputs + attn_out, g1, beta1)
        h = jax.nn.relu(out1 @ W1 + bias1)
        ffn_out = h @ W2 + bias2
        return _layernorm(out1 + ffn_out, g2, beta2)

    def _L0_ffn_ref(h, gate_w, gate_b, w1, b1, w2, b2):
        import math
        import jax, jax.numpy as jnp
        import numpy as np
        CAPACITY_FACTOR = 1.25
        B, L, D = h.shape
        E = gate_w.shape[1]
        T = B * L
        C = max(1, math.ceil(CAPACITY_FACTOR * T / E))
        x = h.reshape(T, D)
        logits = x @ gate_w + gate_b
        probs = jax.nn.softmax(logits, axis=-1)
        idx = jnp.argmax(probs, axis=-1)
        prb = jnp.take_along_axis(probs, idx[:, None], axis=1)[:, 0]
        one_hot = jax.nn.one_hot(idx, E, dtype=jnp.float32)
        pos = (jnp.cumsum(one_hot, axis=0) * one_hot).sum(-1).astype(jnp.int32) - 1
        kept = pos < C
        pos_safe = jnp.where(kept, pos, C)
        buf = jnp.zeros((E, C, D), dtype=h.dtype).at[idx, pos_safe].set(x, mode='drop')
        hmid = jax.nn.relu(jnp.einsum('ecd,edf->ecf', buf, w1) + b1[:, None, :])
        ybuf = jnp.einsum('ecf,efd->ecd', hmid, w2) + b2[:, None, :]
        pos_g = jnp.minimum(pos, C - 1)
        y_tok = ybuf[idx, pos_g] * (prb * kept)[:, None]
        y = y_tok.reshape(B, L, D)
        y = jnp.nan_to_num(y, nan=0.0, posinf=10000.0, neginf=-10000.0)
        return y
    edge_index = jnp.stack([src, dst])
    xn = _layernorm(x, axis=-1)
    x = x + _L0_gnn_ref(xn, edge_index, L0_gnn_W, L0_gnn_b_lin, L0_gnn_att, L0_gnn_b_conv) + _L0_mix_ref(xn[None], L0_mix_Wq, L0_mix_bq, L0_mix_Wk, L0_mix_bk, L0_mix_Wv, L0_mix_bv, L0_mix_Wo, L0_mix_bo, L0_mix_proj, L0_mix_W1, L0_mix_bias1, L0_mix_W2, L0_mix_bias2, L0_mix_g1, L0_mix_beta1, L0_mix_g2, L0_mix_beta2)[0]
    x = x + _L0_ffn_ref(_layernorm(x, axis=-1)[None], L0_ffn_gate_w, L0_ffn_gate_b, L0_ffn_w1, L0_ffn_b1, L0_ffn_w2, L0_ffn_b2)[0]
    return x

_drawn_inputs = setup_inputs


def setup_inputs(seed=0):
    import zlib

    import numpy as np

    out = dict(_drawn_inputs(seed))
    spreads = {'L0_gnn_b_conv': (0.0, 0.1),
     'L0_mix_bq': (0.0, 0.1),
     'L0_mix_bk': (0.0, 0.1),
     'L0_mix_bv': (0.0, 0.1),
     'L0_mix_bo': (0.0, 0.1),
     'L0_mix_bias1': (0.0, 0.1),
     'L0_mix_bias2': (0.0, 0.1),
     'L0_mix_g1': (1.0, 0.2),
     'L0_mix_beta1': (0.0, 0.1),
     'L0_mix_g2': (1.0, 0.2),
     'L0_mix_beta2': (0.0, 0.1),
     'L0_ffn_gate_b': (0.0, 0.1),
     'L0_ffn_b1': (0.0, 0.664),
     'L0_ffn_b2': (0.0, 0.48)}
    factors = {'L0_gnn_b_lin': 8.0, 'L0_gnn_att': 5.988}
    for name, (base, spread) in spreads.items():
        noise = np.random.default_rng([zlib.crc32(name.encode()), seed]).standard_normal(out[name].shape)
        drawn = base * np.exp(spread * noise) if base else spread * noise
        out[name] = jnp.asarray(drawn.astype(out[name].dtype))
    for name, factor in factors.items():
        out[name] = (out[name] * factor).astype(out[name].dtype)
    return out
```

```python
from contextlib import ExitStack

import numpy as np
import concourse.bass as bass
from concourse import mybir

ALU = mybir.AluOpType
ACT = mybir.ActivationFunctionType
F32 = mybir.dt.float32
BF16 = mybir.dt.bfloat16
I32 = mybir.dt.int32
AX = mybir.AxisListType

P = 128
N, D, E = 3125, 256, 50000
T, R = 25, 125
DT = D // P
CH = -(-E // P)
STEPS = 416
GS = 8
NG = STEPS // GS
SB = 4
GH = 4
DH = D // GH
MH = 8
PAIRS = MH // 2
PW = 2 * D
BIG = 1.0e30
MIN_NORM = 1e-15
MAXN = 1.0 - 0.004
EPS_ATT = 1e-6
SCALE = float(D) ** -0.25
ATANH_MAX = float(np.float32(1.0 - 1e-7))
XE, FF = 8, 1024
CAP = 489
SLOT = 512


class Chain:

    def __init__(self, eng, sem):
        self.eng, self.sem, self.base, self.n = eng, sem, 0, 0

    def __call__(self, ins):
        ins.then_inc(self.sem, 1)
        self.n += 1
        self.eng.wait_ge(self.sem, self.base + self.n)

    def enter(self, i, k):
        self.outer = (self.base, self.n)
        self.base = i * k + (self.base + self.n)
        self.n, self.k = 0, k

    def leave(self, count):
        assert self.n == self.k, (self.n, self.k)
        base, n = self.outer
        self.base, self.n = base, n + count * self.k


def done(t):
    return t + 3


def bcast(ap, rows, cols, offset=0):
    return bass.AP(ap.tensor, offset, [[0, rows], [1, cols]])


def build(nc, x, src, dst, gW, gb, gatt, gbc, Wq, bq, Wk, bk, Wv, bv, Wo, bo, proj, W1, bias1, W2, bias2,
          g1, beta1, g2, beta2, gate_w, gate_b, w1, b1, w2, b2, out):
    top = ExitStack()
    with top:
        def sb(name, shape, dt=F32, ctx=top):
            return ctx.enter_context(nc.sbuf_tensor(name, shape, dt))

        def pb(name, shape, dt=F32, ctx=top):
            return ctx.enter_context(nc.psum_tensor(name, shape, dt))

        def sem(name):
            return top.enter_context(nc.semaphore(name))

        lx_dram = nc.dram_tensor("lx_dram", (N, D), F32).ap()
        ft_dram = nc.dram_tensor("ft_dram", (N, D), F32).ap()
        sj_dram = nc.dram_tensor("sj_dram", (N, GH), F32).ap()
        er_dram = nc.dram_tensor("er_dram", (CH, 1 + 2 * P), I32).ap()
        rel_dram = nc.dram_tensor("rel_dram", (SB * P, P), BF16).ap()

        XN = sb("XN", [R, T, D + 1])
        XNT = sb("XNT", [P, DT, N])
        ACC = sb("ACC", [R, T, D])
        GACC = sb("GACC", [P, T, 265])
        SIJ = sb("SIJ", [R, T, 2 * GH])
        ident = sb("ident", [P, P])
        ones = sb("ones", [P, P])
        iota_p = sb("iota_p", [P, 1])
        iota_f = sb("iota_f", [P, P])
        CSE = sb("CSE", [P, D + 1])
        idxT = sb("idxT", [P, STEPS], I32)
        relT = sb("relT", [P, STEPS])
        PEN = sb("PEN", [P, SB, P])
        D0 = sb("D0", [P, SB, P])
        tI = sb("tI", [1, STEPS], I32)

        bank = [pb(f"bank{i}", [P, 512]) for i in range(8)]

        x_in = sem("x_in"); w_in = sem("w_in"); e_in = sem("e_in"); er_ready = sem("er_ready")
        v1 = sem("v1"); a1s = sem("a1s"); p1 = sem("p1"); const_ready = sem("const_ready")
        xns_full = sem("xns_full"); xns_kept = sem("xns_kept"); xt_full = sem("xt_full"); xts_full = sem("xts_full")
        xts_kept = sem("xts_kept"); u_full = sem("u_full"); u_kept = sem("u_kept"); sq_done = sem("sq_done")
        hbs_full = sem("hbs_full"); lx_done = sem("lx_done"); sij_done = sem("sij_done")
        stat_n = sem("stat_n"); cs_full = sem("cs_full")
        pre_psum = sem("pre_psum"); pre_used = sem("pre_used"); sc_v = sem("sc_v"); sc_a = sem("sc_a")
        hb2 = sem("hb2"); lx_ready = sem("lx_ready"); lx_out = sem("lx_out"); nt_in = sem("nt_in")
        sij_ready = sem("sij_ready"); tab_out = sem("tab_out"); cf_psum = sem("cf_psum"); cf_used = sem("cf_used")
        ci_ready = sem("ci_ready"); er_rows = sem("er_rows"); rel_ready = sem("rel_ready"); rel_out = sem("rel_out")
        eT_psum = sem("eT_psum"); eT_used = sem("eT_used")

        with ExitStack() as ctx:
            Wn = sb("Wn", [P, DT, D], ctx=ctx)
            WT = sb("WT", [P, DT, D + 1], ctx=ctx)
            bcol = sb("bcol", [P, DT], ctx=ctx)
            hbcol = sb("hbcol", [P, DT], ctx=ctx)
            hbrow = sb("hbrow", [R, D], ctx=ctx)
            attr = sb("attr", [R, 2, GH, DH], ctx=ctx)
            st6 = sb("st6", [R, T, 6], ctx=ctx)
            xns = sb("xns", [R, 2, D + 1], ctx=ctx)
            xts = sb("xts", [P, 2, DT, R], ctx=ctx)
            hbs = sb("hbs", [R, 2, D], ctx=ctx)
            junk = sb("junk", [R, 2, D], ctx=ctx)
            prod = sb("prod", [R, 2, 2, GH, DH], ctx=ctx)
            bsq = sb("bsq", [P, DT], ctx=ctx)
            zrow = sb("zrow", [1, P], ctx=ctx)
            zwide = sb("zwide", [1, D + 1], ctx=ctx)
            hs = sb("hs", [P, 8], ctx=ctx)
            ns = {k: sb("ns_" + k, [R, T], ctx=ctx) for k in (
                "mean", "var", "dm", "std", "rstd", "n0", "nc", "p", "q", "lp", "lq", "at", "ser", "msk", "s1",
                "usq", "uh", "nu", "th", "f1", "x2", "xy", "A", "B", "den", "P", "Q", "nv2", "nv", "g",
                "a1", "a2", "t0", "t1")}
            er = sb("er", [P, SB, 1 + 2 * P], I32, ctx=ctx)
            erf = sb("erf", [P, SB, 1 + 2 * P], ctx=ctx)
            firsts = sb("firsts", [1, CH - 1], I32, ctx=ctx)
            firstf = sb("firstf", [1, CH - 1], ctx=ctx)
            thr = sb("thr", [T - 1, 1], ctx=ctx)
            ge = sb("ge", [T - 1, CH - 1], ctx=ctx)
            iotc = sb("iotc", [P, CH - 1], ctx=ctx)
            stepid = sb("stepid", [P, SB], ctx=ctx)
            cif = sb("cif", [P, SB], ctx=ctx)
            cii = sb("cii", [P, SB], I32, ctx=ctx)
            tf = sb("tf", [P, SB], ctx=ctx)
            t125 = sb("t125", [P, SB], ctx=ctx)
            AC = sb("AC", [P, CH - 1], ctx=ctx)
            ejunk = sb("ejunk", [P, CH - 1], ctx=ctx)
            rel = sb("rel", [P, SB, P], ctx=ctx)
            relb = sb("relb", [P, SB, P], BF16, ctx=ctx)
            m1 = sb("m1", [P, SB, P], ctx=ctx)
            padd = sb("padd", [1, 48], I32, ctx=ctx)
            pads = sb("pads", [1, 48], I32, ctx=ctx)
            X = GACC[0:R, :, 0:D]
            NTs = GACC[0:R, :, 0:D]
            NT = GACC[0:R, :, 0:D].rearrange("r t (h d) -> r t h d", h=GH)
            TAIL = E - (CH - 1) * P
            col = lambda name, t: ns[name][:, bass.ds(t, 1)]

            def row(buf, t):
                return buf[:, bass.ds(t, 1), :].rearrange("r a c -> r (a c)")

            def over_tiles(eng, body, *before_after):
                with eng.Fori(0, T // 2) as i:
                    body(2 * i, 0)
                    body(2 * i + 1, 1)
                body(T - 1, 0)

            block = ctx.enter_context(nc.Block())

            @block.sync
            def _(sp):
                for k in range(5):
                    sp.dma_start(X[:, 5 * k:5 * k + 5, :],
                                 x[5 * k * R:5 * (k + 1) * R, :].rearrange("(t r) d -> r t d", r=R)).then_inc(x_in, 16)
                sp.dma_start(Wn[:], gW.rearrange("(o p) d -> p o d", p=P)).then_inc(w_in, 16)
                with nc.allow_non_contiguous_dma("bias column"):
                    sp.dma_start(bcol[:], gb.rearrange("(o p) -> p o", p=P)).then_inc(w_in, 16)
                sp.dma_start(hbrow[:], bcast(gb, R, D)).then_inc(w_in, 16)
                for s in range(2):
                    sp.dma_start(attr[:, s], bass.AP(gatt.tensor, s * DH, [[0, R], [2 * DH, GH], [1, DH]])).then_inc(w_in, 16)
                full = (CH - 1) * P
                with nc.allow_non_contiguous_dma("chunk edges"):
                    sp.dma_start(er_dram[0:CH - 1, 1:1 + P], dst[0:full].rearrange("(c e) -> c e", e=P)).then_inc(er_ready, 16)
                    sp.dma_start(er_dram[0:CH - 1, 1 + P:], src[0:full].rearrange("(c e) -> c e", e=P)).then_inc(er_ready, 16)
                    sp.dma_start(er_dram[CH - 1:CH, 1:1 + TAIL], dst[full:E].rearrange("(c e) -> c e", c=1)).then_inc(er_ready, 16)
                    sp.dma_start(er_dram[CH - 1:CH, 1 + P:1 + P + TAIL], src[full:E].rearrange("(c e) -> c e", c=1)).then_inc(er_ready, 16)
                    sp.dma_start(er_dram[1:CH, 0:1], bass.AP(dst.tensor, P - 1, [[P, CH - 1], [1, 1]])).then_inc(er_ready, 16)
                    sp.dma_start(firsts[:], bass.AP(dst.tensor, P, [[0, 1], [P, CH - 1]])).then_inc(e_in, 16)
                    sp.wait_ge(const_ready, 1)
                    sp.dma_start(er_dram[CH - 1:CH, 1 + TAIL:1 + P], padd[:, 0:P - TAIL]).then_inc(er_ready, 16)
                    sp.dma_start(er_dram[CH - 1:CH, 1 + P + TAIL:], pads[:, 0:P - TAIL]).then_inc(er_ready, 16)
                    sp.dma_start(er_dram[0:1, 0:1], padd[:, 0:1]).then_inc(er_ready, 16)
                sp.wait_ge(rel_ready, 1)
                for b in range(SB):
                    sp.dma_start(rel_dram[b * P:(b + 1) * P, :], relb[:, b, :]).then_inc(rel_out, 16)
                sp.wait_ge(lx_done, done(T - 1))
                sp.dma_start(lx_dram.rearrange("(t r) d -> r t d", r=R), ACC[:]).then_inc(lx_out, 16)
                sp.wait_ge(lx_out, 16)
                for h in range(GH):
                    sp.dma_start(NT[:, :, h, :], bass.AP(lx_dram.tensor, h * N * DH, [[DH, R], [R * DH, T], [1, DH]])).then_inc(nt_in, 16)
                sp.wait_ge(nt_in, 16 * GH)
                sp.dma_start(ft_dram.rearrange("(t r) d -> r t d", r=R), X).then_inc(tab_out, 16)
                sp.wait_ge(sij_ready, T)
                with nc.allow_non_contiguous_dma("source scores"):
                    sp.dma_start(sj_dram.rearrange("(t r) h -> r t h", r=R), SIJ[:, :, GH:]).then_inc(tab_out, 16)
                sp.wait_ge(tab_out, 32)
                sp.wait_ge(rel_out, 16 * SB)

            @block.gpsimd
            def _(pool):
                c = Chain(pool, p1)
                pool.memset(padd[:], 4095)
                pool.memset(pads[:], 0).then_inc(const_ready, 1)
                pool.memset(XN[:, :, D:D + 1], 1.0)
                pool.memset(xns[:, :, D:D + 1], 1.0)
                pool.memset(ones[:], 1.0)
                pool.memset(zrow[:], 0.0)
                pool.memset(zwide[:], 0.0)
                c(pool.memset(ident[:], 0.0))
                c(pool.affine_select(out=ident[:], in_=ident[:], compare_op=ALU.not_equal, fill=1.0, base=0,
                                     pattern=[[-1, P]], channel_multiplier=1))
                kw = dict(allow_small_or_imprecise_dtypes=True)
                pool.iota(iota_p[:], pattern=[[0, 1]], base=0, channel_multiplier=1, **kw)
                pool.iota(iota_f[:], pattern=[[1, P]], base=0, channel_multiplier=0, **kw)
                pool.iota(thr[:], pattern=[[0, 1]], base=R, channel_multiplier=R, **kw)
                pool.iota(iotc[:], pattern=[[1, CH - 1]], base=1, channel_multiplier=0, **kw)
                c(pool.iota(stepid[:], pattern=[[P, SB]], base=0, channel_multiplier=1, **kw))
                pool.engine_nop().then_inc(const_ready, 1)
                def keep_tile(t, par):
                    pool.wait_ge(xns_full, done(t))
                    pool.tensor_copy(row(XN, t)[:, 0:D], xns[:, par, 0:D]).then_inc(xns_kept, 1)

                pool.sem_inc(xns_kept, 2)
                over_tiles(pool, keep_tile)
                pool.wait_ge(ci_ready, 1)
                pool.wait_ge(er_ready, 16 * 8)
                for b in range(SB):
                    pool.indirect_dma_start(out=er[:, b, :], out_offset=None, in_=er_dram,
                                            in_offset=bass.IndirectOffsetOnAxis(ap=cii[:, b:b + 1], axis=0)).then_inc(er_rows, 16)
                pool.wait_ge(er_rows, 16 * SB)

            @block.tensor
            def _(pe):
                pe.sem_inc(xt_full, 2)
                pe.sem_inc(u_full, 2)
                pe.wait_ge(const_ready, 2)
                pe.wait_ge(w_in, 80)
                for o in range(DT):
                    for k in range(DT):
                        last = pe.transpose(bank[0][:, (o * DT + k) * P:(o * DT + k + 1) * P], Wn[:, o, k * P:(k + 1) * P], ident[:])
                last.then_inc(pre_psum, 1)
                pe.wait_ge(hb2, 1)
                for o in range(DT):
                    last = pe.matmul(bank[1][:, 0:1], ones[:], bsq[:, o:o + 1], start=(o == 0), stop=(o == DT - 1))
                last.then_inc(pre_psum, 1)
                pe.wait_ge(hb2, 2)
                for k in range(DT):
                    for o in range(DT):
                        last = pe.matmul(bank[1][:, 8 + k:9 + k], Wn[:, o, k * P:(k + 1) * P], hbcol[:, o:o + 1], start=(o == 0), stop=(o == DT - 1))
                last.then_inc(pre_psum, 1)
                pe.wait_ge(cf_used, 1)
                pe.matmul(bank[2][0:T - 1, 0:CH - 1], ones[0:1, 0:T - 1], firstf[:], start=True, stop=True).then_inc(cf_psum, 1)
                pe.wait_ge(cf_used, 2)
                pe.matmul(bank[3][:, 0:CH - 1], ones[0:T - 1, :], ge[:], start=True, stop=True).then_inc(cf_psum, 1)
                pe.wait_ge(cf_used, 3)
                for b in range(SB):
                    last = pe.transpose(bank[2][0:1, b * P:(b + 1) * P], tf[:, b:b + 1], ident[:])
                last.then_inc(cf_psum, 1)
                pe.wait_ge(pre_used, 3)

                def node_tile(t, par):
                    pe.wait_ge(xns_full, done(t))
                    pe.matmul(bank[7][:, 0:D + 1], ones[0:R, :], xns[:, par, :], start=False, stop=False,
                              skip_group_check=True)
                    pe.wait_ge(xts_full, done(t - 1))
                    for k in range(DT):
                        last = pe.transpose(bank[4][:, k * P:k * P + R], xns[:, par, k * P:(k + 1) * P], ident[0:R, 0:R])
                    last.then_inc(xt_full, 1)
                    pe.wait_ge(xts_full, done(t))
                    pe.wait_ge(u_kept, done(t - 1))
                    for k in range(DT):
                        last = pe.matmul(bank[5][0:R, 0:D + 1], xts[:, par, k, :], WT[:, k, :], start=(k == 0), stop=(k == DT - 1))
                    last.then_inc(u_full, 1)

                pe.matmul(bank[7][:, 0:D + 1], zrow[:], zwide[:], start=True, stop=False, skip_group_check=True)
                over_tiles(pe, node_tile)
                pe.matmul(bank[7][:, 0:D + 1], zrow[:], zwide[:], start=False, stop=True, skip_group_check=True).then_inc(cs_full, 1)

                pe.wait_ge(rel_ready, 2)
                for b in range(SB):
                    w = min(P, STEPS - b * P)
                    pe.transpose(bank[0][:, b * P:b * P + w], rel[0:w, b, :], ident[0:w, 0:w])
                    last = pe.transpose(bank[1][:, b * P:b * P + w], erf[0:w, b, 1 + P:], ident[0:w, 0:w])
                last.then_inc(eT_psum, 1)

            @block.scalar
            def _(act):
                c = Chain(act, a1s)
                act.sem_inc(xts_full, 2)
                act.sem_inc(sq_done, 2)
                act.sem_inc(hbs_full, 2)
                act.wait_ge(w_in, 80)
                act.activation(bsq[:], bcol[:], ACT.Square).then_inc(hb2, 1)
                act.wait_ge(sc_v, 1)
                act.activation(ns["std"][:], ns["t1"][:], ACT.Sqrt)
                act.activation(ns["n0"][:], ns["var"][:], ACT.Sqrt).then_inc(sc_a, 1)
                act.wait_ge(sc_v, 2)
                act.activation(hs[:, 1:2], hs[:, 0:1], ACT.Sqrt).then_inc(sc_a, 1)
                act.wait_ge(sc_v, 3)
                act.activation(hs[:, 3:4], hs[:, 2:3], ACT.Tanh).then_inc(sc_a, 1)
                act.wait_ge(sc_v, 4)
                act.activation(ns["lp"][:], ns["p"][:], ACT.Ln)
                act.activation(ns["lq"][:], ns["q"][:], ACT.Ln).then_inc(sc_a, 1)

                def node_tile(t, par):
                    act.wait_ge(xt_full, done(t))
                    act.wait_ge(u_full, done(t - 2))
                    act.wait_ge(xts_kept, done(t - 2))
                    act.activation(xts[:, par, :, :], bank[4][:, 0:D].rearrange("p (k r) -> p k r", k=DT)[:, :, 0:R], ACT.Copy).then_inc(xts_full, 1)
                    act.wait_ge(u_kept, done(t))
                    act.activation(junk[:, par, :], row(ACC, t), ACT.Square, accum_out=col("usq", t)).then_inc(sq_done, 1)
                over_tiles(act, node_tile)
                act.wait_ge(sc_v, 5)
                act.activation(ns["nu"][:], ns["t0"][:], ACT.Sqrt).then_inc(sc_a, 1)
                act.wait_ge(sc_v, 6)
                act.activation(ns["th"][:], ns["t1"][:], ACT.Tanh).then_inc(sc_a, 1)
                act.wait_ge(sc_v, 7)
                act.activation(ns["nv"][:], ns["nv2"][:], ACT.Sqrt).then_inc(sc_a, 1)
                act.wait_ge(sc_v, 8)
                act.activation(ns["lp"][:], ns["p"][:], ACT.Ln)
                act.activation(ns["lq"][:], ns["q"][:], ACT.Ln).then_inc(sc_a, 1)
                act.wait_ge(sc_v, 9)

                def hb_tile(t, par):
                    act.wait_ge(lx_done, done(t - 2))
                    act.activation(hbs[:, par, :], hbrow[:], ACT.Copy, scale=col("a2", t)).then_inc(hbs_full, 1)
                over_tiles(act, hb_tile)

            @block.vector
            def _(v):
                c = Chain(v, v1)

                def stats(t, par):
                    v.bn_stats(row(st6, t), row(X, t)).then_inc(stat_n, 1)
                v.wait_ge(x_in, 80)
                over_tiles(v, stats)
                v.wait_ge(stat_n, T)
                s = [st6[:, :, k] for k in range(6)]
                n = {k: b[:] for k, b in ns.items()}
                c(v.tensor_tensor(n["mean"], s[1], s[4], ALU.add))
                c(v.tensor_scalar(n["mean"], n["mean"], 0.5, None, ALU.mult))
                c(v.tensor_tensor(n["dm"], s[1], s[4], ALU.subtract))
                c(v.tensor_tensor(n["dm"], n["dm"], n["dm"], ALU.mult))
                c(v.tensor_tensor(n["var"], s[2], s[5], ALU.add))
                c(v.tensor_scalar(n["var"], n["var"], 1.0 / D, None, ALU.mult))
                c(v.scalar_tensor_tensor(out=n["var"], in0=n["dm"], scalar=0.25, in1=n["var"], op0=ALU.mult, op1=ALU.add))
                v.tensor_scalar(n["t1"], n["var"], 1e-5, None, ALU.add).then_inc(sc_v, 1)
                v.wait_ge(sc_a, 1)
                c(v.reciprocal(n["rstd"], n["std"]))

                v.wait_ge(pre_psum, 2)
                v.tensor_copy(hs[:, 0:1], bank[1][:, 0:1]).then_inc(sc_v, 1)
                v.wait_ge(sc_a, 2)
                v.tensor_scalar(hs[:, 2:3], hs[:, 1:2], MIN_NORM, None, ALU.max).then_inc(sc_v, 1)
                v.wait_ge(sc_a, 3)
                c(v.tensor_scalar(hs[:, 3:4], hs[:, 3:4], MAXN, None, ALU.min))
                c(v.tensor_tensor(hs[:, 5:6], hs[:, 3:4], hs[:, 3:4], ALU.mult))
                c(v.reciprocal(hs[:, 4:5], hs[:, 2:3]))
                c(v.tensor_tensor(hs[:, 6:7], hs[:, 3:4], hs[:, 4:5], ALU.mult))
                c(v.tensor_scalar(hbrow[:], hbrow[:], hs[0:R, 6:7], None, ALU.mult))
                v.tensor_scalar(hbcol[:], bcol[:], hs[:, 6:7], None, ALU.mult).then_inc(hb2, 1)
                v.wait_ge(pre_psum, 3)
                for o in range(DT):
                    for k in range(DT):
                        v.tensor_copy(WT[:, k, o * P:(o + 1) * P], bank[0][:, (o * DT + k) * P:(o * DT + k + 1) * P]).then_inc(pre_used, 1)
                v.tensor_copy(WT[:, :, D:D + 1], bank[1][:, 8:8 + DT]).then_inc(pre_used, 1)

                def atanh(norm, extra):
                    c(v.tensor_scalar(n["p"], norm, 1.0, None, ALU.add))
                    v.tensor_scalar(n["q"], norm, -1.0, 1.0, ALU.mult, ALU.add).then_inc(sc_v, 1)
                    c(v.tensor_tensor(n["t0"], norm, norm, ALU.mult))
                    c(v.tensor_scalar(n["ser"], n["t0"], 1.0 / 7, 1.0 / 5, ALU.mult, ALU.add))
                    c(v.tensor_tensor(n["ser"], n["ser"], n["t0"], ALU.mult))
                    c(v.tensor_scalar(n["ser"], n["ser"], 1.0 / 3, None, ALU.add))
                    c(v.tensor_tensor(n["ser"], n["ser"], n["t0"], ALU.mult))
                    c(v.scalar_tensor_tensor(out=n["ser"], in0=n["ser"], scalar=1.0, in1=norm, op0=ALU.add, op1=ALU.mult))
                    c(v.tensor_scalar(n["msk"], norm, 0.1, None, ALU.is_lt))
                    v.wait_ge(sc_a, extra)
                    c(v.tensor_tensor(n["at"], n["lp"], n["lq"], ALU.subtract))
                    c(v.tensor_scalar(n["at"], n["at"], 0.5, None, ALU.mult))
                    c(v.tensor_tensor(n["ser"], n["ser"], n["at"], ALU.subtract))
                    c(v.tensor_tensor(n["ser"], n["ser"], n["msk"], ALU.mult))
                    c(v.tensor_tensor(n["at"], n["at"], n["ser"], ALU.add))

                c(v.scalar_tensor_tensor(out=n["n0"], in0=n["n0"], scalar=float(D) ** 0.5, in1=n["rstd"], op0=ALU.mult, op1=ALU.mult))
                c(v.tensor_scalar(n["n0"], n["n0"], MIN_NORM, None, ALU.max))
                c(v.tensor_scalar(n["nc"], n["n0"], ATANH_MAX, None, ALU.min))
                atanh(n["nc"], 4)
                c(v.reciprocal(n["t0"], n["n0"]))
                c(v.tensor_tensor(n["s1"], n["at"], n["t0"], ALU.mult))

                v.wait_ge(e_in, 16)
                v.wait_ge(const_ready, 2)
                v.tensor_copy(firstf[:], firsts[:]).then_inc(cf_used, 1)
                v.wait_ge(cf_psum, 1)
                v.tensor_scalar(ge[:], bank[2][0:T - 1, 0:CH - 1], thr[:], None, ALU.is_ge).then_inc(cf_used, 1)
                v.wait_ge(cf_psum, 2)
                c(v.tensor_tensor(AC[:], bank[3][:, 0:CH - 1], iotc[:], ALU.add))
                for b in range(SB):
                    c(v.tensor_scalar(ejunk[:], AC[:], stepid[:, b:b + 1], 0.0, ALU.is_le, ALU.add, accum_out=cif[:, b:b + 1]))
                c(v.tensor_tensor(tf[:], stepid[:], cif[:], ALU.subtract))
                c(v.tensor_scalar(t125[:], tf[:], float(R), None, ALU.mult))
                v.tensor_copy(cii[:], cif[:]).then_inc(ci_ready, 1)
                c(v.tensor_scalar(tf[:], tf[:], 0.0, float(T - 1), ALU.max, ALU.min))
                v.sem_inc(cf_used, 1)
                v.wait_ge(cf_psum, 3)
                c(v.tensor_copy(tI[:], bank[2][0:1, 0:STEPS]))

                def norm_tile(t, par):
                    v.wait_ge(xt_full, done(t - 2))
                    v.wait_ge(xns_kept, done(t - 2))
                    v.tensor_scalar(xns[:, par, 0:D], row(X, t), col("mean", t), col("rstd", t), ALU.subtract, ALU.mult).then_inc(xns_full, 1)

                v.sem_inc(u_kept, 2)
                v.sem_inc(xns_full, 2)
                v.sem_inc(xts_kept, 2)
                norm_tile(0, 0)

                def node_tile(t, par):
                    if not isinstance(t, int):
                        norm_tile(t + 1, 1 - par)
                    v.wait_ge(xts_full, done(t))
                    v.tensor_copy(XNT[:, :, bass.ds(t * R, R)], xts[:, par]).then_inc(xts_kept, 1)
                    v.wait_ge(u_full, done(t))
                    v.tensor_copy(row(ACC, t), bank[5][0:R, 0:D])
                    v.tensor_copy(col("uh", t), bank[5][0:R, D:D + 1]).then_inc(u_kept, 1)
                over_tiles(v, node_tile)
                v.wait_ge(cs_full, 1)
                c(v.tensor_scalar(CSE[:], bank[7][:, 0:D + 1], EPS_ATT, None, ALU.mult))

                v.wait_ge(u_kept, done(T - 1))
                v.wait_ge(sq_done, done(T - 1))
                v.tensor_scalar(n["t0"], n["usq"], 0.0, None, ALU.max).then_inc(sc_v, 1)
                v.wait_ge(sc_a, 5)
                c(v.tensor_tensor(n["nu"], n["nu"], n["s1"], ALU.mult))
                v.tensor_scalar(n["t1"], n["nu"], MIN_NORM, None, ALU.max).then_inc(sc_v, 1)
                v.wait_ge(sc_v, 6)
                c(v.reciprocal(n["f1"], n["t1"]))
                c(v.tensor_tensor(n["f1"], n["f1"], n["s1"], ALU.mult))
                v.wait_ge(sc_a, 6)
                c(v.tensor_scalar(n["th"], n["th"], MAXN, None, ALU.min))
                c(v.tensor_tensor(n["f1"], n["f1"], n["th"], ALU.mult))
                c(v.tensor_tensor(n["x2"], n["th"], n["th"], ALU.mult))
                c(v.tensor_tensor(n["xy"], n["uh"], n["f1"], ALU.mult))
                y2 = hs[0:R, 5:6]
                c(v.tensor_scalar(n["A"], n["xy"], 2.0, 1.0, ALU.mult, ALU.add))
                c(v.scalar_tensor_tensor(out=n["den"], in0=n["x2"], scalar=y2, in1=n["A"], op0=ALU.mult, op1=ALU.add))
                c(v.tensor_scalar(n["A"], n["A"], y2, None, ALU.add))
                c(v.tensor_scalar(n["B"], n["x2"], -1.0, 1.0, ALU.mult, ALU.add))
                c(v.tensor_scalar(n["den"], n["den"], MIN_NORM, None, ALU.max))
                c(v.reciprocal(n["den"], n["den"]))
                c(v.tensor_tensor(n["P"], n["A"], n["f1"], ALU.mult))
                c(v.tensor_tensor(n["P"], n["P"], n["den"], ALU.mult))
                c(v.tensor_tensor(n["Q"], n["B"], n["den"], ALU.mult))
                c(v.tensor_tensor(n["t0"], n["P"], n["usq"], ALU.mult))
                c(v.scalar_tensor_tensor(out=n["t1"], in0=n["Q"], scalar=2.0, in1=n["uh"], op0=ALU.mult, op1=ALU.mult))
                c(v.tensor_tensor(n["t0"], n["t0"], n["t1"], ALU.add))
                c(v.tensor_tensor(n["t0"], n["t0"], n["P"], ALU.mult))
                c(v.tensor_tensor(n["t1"], n["Q"], n["Q"], ALU.mult))
                c(v.scalar_tensor_tensor(out=n["t0"], in0=n["t1"], scalar=y2, in1=n["t0"], op0=ALU.mult, op1=ALU.add))
                v.tensor_scalar(n["nv2"], n["t0"], 0.0, None, ALU.max).then_inc(sc_v, 1)
                v.wait_ge(sc_a, 7)
                c(v.tensor_scalar(n["nv"], n["nv"], MIN_NORM, None, ALU.max))
                c(v.tensor_scalar(n["nc"], n["nv"], MAXN, ATANH_MAX, ALU.min, ALU.min))
                atanh(n["nc"], 8)
                c(v.reciprocal(n["t0"], n["nv"]))
                c(v.tensor_tensor(n["g"], n["at"], n["t0"], ALU.mult))
                c(v.tensor_tensor(n["a1"], n["g"], n["P"], ALU.mult))
                v.tensor_tensor(n["a2"], n["g"], n["Q"], ALU.mult).then_inc(sc_v, 1)
                v.sem_inc(lx_done, 2)

                def lx_tile(t, par):
                    v.wait_ge(hbs_full, done(t))
                    v.scalar_tensor_tensor(out=row(ACC, t), in0=row(ACC, t), scalar=col("a1", t), in1=hbs[:, par, :],
                                           op0=ALU.mult, op1=ALU.add).then_inc(lx_done, 1)
                over_tiles(v, lx_tile)

                v.wait_ge(er_rows, 16 * SB)
                c(v.tensor_copy(erf[:], er[:]))
                de = erf[:, :, 1:1 + P]
                for b in range(SB):
                    c(v.tensor_scalar(rel[:, b, :], de[:, b, :], t125[:, b:b + 1], -1.0, ALU.subtract, ALU.max))
                c(v.tensor_scalar(rel[:], rel[:], float(R), None, ALU.min))
                c(v.tensor_copy(relb[:], rel[:]))
                c(v.tensor_tensor(m1[:], de, erf[:, :, 0:P], ALU.not_equal))
                c(v.tensor_scalar(PEN[:], rel[:], 0.0, None, ALU.is_ge))
                c(v.scalar_tensor_tensor(out=PEN[:], in0=rel[:], scalar=float(R) - 0.5, in1=PEN[:], op0=ALU.is_lt, op1=ALU.mult))
                c(v.scalar_tensor_tensor(out=D0[:], in0=m1[:], scalar=-BIG, in1=PEN[:], op0=ALU.mult, op1=ALU.mult))
                c(v.tensor_scalar(PEN[:], PEN[:], -1.0, BIG, ALU.add, ALU.mult))
                v.sem_inc(rel_ready, 2)
                v.wait_ge(eT_psum, 1)
                c(v.tensor_copy(relT[:], bank[0][:, 0:STEPS]))
                c(v.tensor_copy(idxT[:], bank[1][:, 0:STEPS]))

                v.wait_ge(nt_in, 16 * GH)

                def score_tile(t, par):
                    nt = row(NTs, t).rearrange("r (h d) -> r h d", h=GH)
                    for s_ in range(2):
                        last = v.tensor_tensor(prod[:, par, s_], nt, attr[:, s_], ALU.mult)
                    c(last)
                    v.tensor_reduce(row(SIJ, t), prod[:, par].rearrange("r s h d -> r (s h) d"), AX.X, ALU.add).then_inc(sij_ready, 1)
                with v.Fori(0, T // 2) as i:
                    c.enter(i, 2)
                    score_tile(2 * i, 0)
                    score_tile(2 * i + 1, 1)
                c.leave(T // 2)
                score_tile(T - 1, 0)


        wp_in = sem("wp_in"); set_pe = sem("set_pe"); set_v = sem("set_v"); set_a = sem("set_a")
        fin_v = sem("fin_v"); fin_pe = sem("fin_pe"); v2 = sem("v2")
        xtm_full = sem("xtm_full"); pj_full = sem("pj_full"); pj_used = sem("pj_used"); nsq_full = sem("nsq_full")
        u2_full = sem("u2_full"); e_full = sem("e_full"); e_used = sem("e_used")
        phi_full = sem("phi_full"); att_full = sem("att_full"); rz_full = sem("rz_full"); acc_half = sem("acc_half")
        att_used = sem("att_used")
        oht_done = sem("oht_done"); sd_full = sem("sd_full"); sd_kept = sem("sd_kept"); r_full = sem("r_full")
        c_in = sem("c_in"); p_ready = sem("p_ready"); rb_in = sem("rb_in"); stg = sem("stg"); sj_in = sem("sj_in")
        sj_kept = sem("sj_kept"); p2 = sem("p2"); stg_seen = sem("stg_seen"); g_in = [sem("g_in0"), sem("g_in1")]; o_full = sem("o_full"); o_used = sem("o_used")
        v3 = sem("v3")
        HB = T + 1
        HALVES = STEPS // 4
        flat = GACC[:, :, :].rearrange("p t c -> p (t c)")
        SJ = flat[:, 0:SB * P * GH].rearrange("p (s h) -> p s h", h=GH)
        SD = flat[:, SB * P * GH:3 * SB * P * GH].rearrange("p (s h) -> p s h", h=2 * GH)
        projT = sb("projT", [P, DT, D])
        zr = sb("zr", [1, P]); zw = sb("zw", [1, D + 1])

        def row(buf, t):
            return buf[:, bass.ds(t, 1), :].rearrange("r a c -> r (a c)")

        def steps_tiles(eng_type, u):
            _, regs = nc.values_load_multi_w_load_instructions(tI[0:1, bass.ds(4 * u, 4)], engines=[eng_type],
                                                               min_val=0, max_val=T - 1)
            return regs

        def mixer_block(first):
            ctx = ExitStack()
            with ctx:
                n_ = "A" if first else "B"
                mk = lambda name, shape, dt=F32: sb(name + n_, shape, dt, ctx=ctx)
                WS = {k: mk(f"W{k}S", [P, DT, PW]) for k in "kqv"}
                WoS = mk("WoS", [P, 4, D])
                WTs = {k: mk(f"W{k}T", [P, 4, D]) for k in "kqv"}
                MS = {k: mk(f"M{k}S", [P, DT, PW]) for k in "kq"}
                WVO = mk("WVO", [P, 4, D])
                BVWO = mk("BVWO", [P, PW])
                KVX = mk("KVX", [P, 4, D + 1])
                KVXT = WTs["k"]
                KVO = mk("KVO", [P, 4, D + 1])
                bc = mk("bc", [P, 3, 16])
                bcp = mk("bcp", [P, 3, 4])
                brow = KVX[0:1, :, :].rearrange("p b c -> p (b c)")[:, 0:2 * PW].rearrange("p (i k) -> p i k", i=2)
                kvo_flat = KVO[:].rearrange("p b c -> p (b c)")
                BVB = kvo_flat[:, 0:PW].rearrange("p (c k) -> p c k", c=4)
                rr = kvo_flat[0:1, PW:2 * PW]
                mid = mk("mid", [1, PW], BF16)
                b3 = {k: mk(f"b3{k}", [65, PW], BF16) for k in ("k", "q", "ck", "cq")}
                ones3 = mk("ones3", [65, R], BF16)
                spare = WTs["v"][:].rearrange("p c d -> p (c d)")
                xtm = spare[:, 0:2 * DT * R].rearrange("p (a k r) -> p a k r", a=2, k=DT)
                PT = spare[:, 2 * D:2 * D + 4 * R].rearrange("p (b r) -> p b r", b=4)
                EB = WTs["q"][0:R].rearrange("p c d -> p (c d)").rearrange("p (a k) -> p a k", a=2)
                sq = mk("sq", [R, 2, 2])
                nsq = mk("nsq", [R, 2, 2])
                rz = mk("rz", [R, 2])
                sidx = mk("sidx", [P, 4], I32)
                if first:
                    pn = mk("pn", [P, DT, D])
                    RB = mk("RB", [R, 4 * P], BF16)
                    OHT = mk("OHT", [R, 4 * P])
                    sjst = mk("sjst", [P, 4, GH])
                else:
                    G = [mk(f"G{i}", [P, 4, D]) for i in range(2)]
                    RS = mk("RS", [P, 2, 4, 265])
                    OH = mk("OH", [P, 2, 4, R])
                g0 = 0 if first else 2
                block = ctx.enter_context(nc.Block())

                def loops(g, ph, tile):
                    B0, Q0, u0 = (2 * g + ph) * T, g * T, (2 * (g - g0) + ph) * HB
                    tile(0, 0, B0, Q0, u0)
                    with_loop = lambda i, k: tile(2 * i + k, k % 2, B0 + 2 * i + k, Q0 + 2 * i + k, u0 + 2 * i + k)
                    return B0, with_loop, (T, 1, B0 + T, Q0 + T, u0 + T)

                def run(eng, g, ph, tile):
                    _, inner, last = loops(g, ph, tile)
                    with eng.Fori(0, T // 2) as i:
                        inner(i, 1)
                        inner(i, 2)
                    tile(*last)

                zero = lambda t: isinstance(t, int) and t == 0
                last_ = lambda t: isinstance(t, int) and t == T
                SV, SA, SPE = 6, 2, 7

                @block.sync
                def _(sp):
                    if first:
                        sp.dma_start(pn[:], proj.rearrange("(o p) k -> p o k", p=P)).then_inc(c_in, 16)
                    with nc.allow_non_contiguous_dma("bias columns"):
                        for i_, b_ in enumerate((bk, bq, bv)):
                            sp.dma_start(bc[:, i_, :], b_.rearrange("h k -> (h k)").rearrange("(c p) -> p c", p=P)).then_inc(c_in, 16)
                    for g in (g0, g0 + 1):
                        if g > g0:
                            sp.wait_ge(u2_full, done(2 * g * T - 1))
                        for k, w_ in (("k", Wk), ("q", Wq), ("v", Wv)):
                            sp.dma_start(WS[k][:], w_.rearrange("(o p) h k -> p o (h k)", p=P)[:, :, PW * g:PW * (g + 1)]).then_inc(wp_in, 16)
                        sp.dma_start(WoS[:], Wo.rearrange("h k d -> (h k) d").rearrange("(c p) d -> p c d", p=P)[:, 4 * g:4 * g + 4, :]).then_inc(wp_in, 16)
                        for i_, b_ in enumerate((bk, bq)):
                            sp.dma_start(brow[:, i_, :], b_.rearrange("h k -> (h k)")[PW * g:PW * (g + 1)].rearrange("(a k) -> a k", a=1)).then_inc(wp_in, 16)
                        if first:
                            with sp.Fori(0, 2 * HB) as i:
                                u = 2 * HB * (g - g0) + i
                                sp.wait_ge(oht_done, done(u - 1))
                                sp.dma_start(RB[:], bass.AP(rel_dram.tensor, u * 4 * P, [[0, R], [1, 4 * P]])).then_inc(rb_in, 16)

                @block.gpsimd
                def _(pool):
                    if first:
                        pool.memset(zr[:], 0.0)
                        pool.memset(zw[:], 0.0)
                        pool.sem_inc(sj_kept, 2)
                        pool.memset(ACC[:], 0.0).then_inc(p_ready, 1)
                    else:
                        pool.memset(GACC[:], 0.0).then_inc(p_ready, 1)
                    if first:
                        pool.memset(SJ[:, STEPS:, :], 0.0)
                        pool.memset(SD[:, STEPS:, :], 0.0)
                        with pool.Fori(0, HALVES) as u:
                            pool.tensor_copy(sidx[:], idxT[:, bass.ds(4 * u, 4)]).then_inc(stg, 1)
                            pool.wait_ge(sj_kept, done(u - 1))
                            pool.sem_inc(stg_seen, 1)
                            pool.wait_ge(stg, u + 1)
                            pool.sem_inc(stg_seen, 1)
                            for k in range(4):
                                pool.indirect_dma_start(out=sjst[:, k, :], out_offset=None, in_=sj_dram,
                                                        in_offset=bass.IndirectOffsetOnAxis(ap=sidx[:, k:k + 1], axis=0)).then_inc(sj_in, 16)
                            pool.wait_ge(sj_in, 64 * (u + 1))
                            pool.tensor_copy(SJ[:, bass.ds(4 * u, 4), :], sjst[:]).then_inc(sj_kept, 1)
                    else:
                        with pool.Fori(0, HALVES // 2) as j:
                            for h in range(2):
                                u = 2 * j + h
                                pool.wait_ge(r_full, done(u - 2))
                                if h == 1:
                                    pool.wait_ge(g_in[0], 64 * (j + 1))
                                pool.tensor_copy(sidx[:], idxT[:, bass.ds(4 * u, 4)]).then_inc(stg, 1)
                                pool.wait_ge(stg, HALVES + u + 1)
                                pool.sem_inc(stg_seen, 1)
                                for k in range(4):
                                    pool.indirect_dma_start(out=G[h][:, k, :], out_offset=None, in_=ft_dram,
                                                            in_offset=bass.IndirectOffsetOnAxis(ap=sidx[:, k:k + 1], axis=0)).then_inc(g_in[h], 16)
                            pool.wait_ge(g_in[1], 64 * (j + 1))

                @block.tensor
                def _(pe):
                    pe.wait_ge(p_ready, 1 if first else 2)
                    if first:
                        pe.sem_inc(pj_full, 2); pe.sem_inc(u2_full, 2); pe.sem_inc(e_used, 2)
                        pe.sem_inc(att_full, 2); pe.sem_inc(sd_full, 2)
                        pe.wait_ge(c_in, 64)
                        for o in range(DT):
                            for k in range(DT):
                                last = pe.transpose(bank[5][:, k * D + o * P:k * D + (o + 1) * P], pn[:, o, k * P:(k + 1) * P], ident[:])
                        last.then_inc(fin_pe, 1)
                        pe.wait_ge(fin_v, 1)

                    def setup(g):
                        pe.wait_ge(wp_in, 96 * (g + 1))
                        pe.wait_ge(pj_used, done(2 * g * T - 1))
                        pe.wait_ge(e_full, done(2 * g * T - 1))
                        pe.wait_ge(att_used, done(g * T - 1))
                        for i_, k in enumerate("kqv"):
                            for h in range(2):
                                for c_ in range(2):
                                    for o in range(DT):
                                        last = pe.transpose(bank[2 * i_ + h][:, c_ * D + o * P:c_ * D + (o + 1) * P],
                                                            WS[k][:, o, h * D + c_ * P:h * D + (c_ + 1) * P], ident[:])
                            last.then_inc(set_pe, 1)
                        for i_, (k, s_, n) in enumerate((("k", set_v, SV * g + 2), ("q", set_a, SA * g + 1))):
                            pe.wait_ge(s_, n)
                            for o in range(DT):
                                for h in range(2):
                                    for c_ in range(2):
                                        last = pe.matmul(bank[2 * i_ + o][:, h * D:(h + 1) * D], WTs[k][:, 2 * h + c_, o * P:(o + 1) * P],
                                                         projT[:, c_, :], start=(c_ == 0), stop=(c_ == 1))
                            last.then_inc(set_pe, 1)
                        pe.wait_ge(set_v, SV * g + 3)
                        for h in range(2):
                            for o in range(DT):
                                for c_ in range(2):
                                    last = pe.matmul(bank[4 + h][:, o * D:(o + 1) * D], WTs["v"][:, 2 * h + c_, o * P:(o + 1) * P],
                                                     WoS[:, 2 * h + c_, :], start=(c_ == 0), stop=(c_ == 1))
                        last.then_inc(set_pe, 1)
                        pe.wait_ge(set_v, SV * g + 5)
                        pe.wait_ge(set_a, SA * g + 2)
                        for h in range(2):
                            for c_ in range(2):
                                kw = dict(start=(c_ == 0), stop=(c_ == 1))
                                for i_ in range(2):
                                    pe.matmul(bank[2 * i_][0:1, h * D:(h + 1) * D], bcp[:, i_, 2 * h + c_:2 * h + c_ + 1], projT[:, c_, :], **kw)
                                last = pe.matmul(bank[4][:, h * D:(h + 1) * D], BVB[:, 2 * h + c_, :], WoS[:, 2 * h + c_, :], **kw)
                        last.then_inc(set_pe, 1)
                        pe.wait_ge(set_v, SV * g + 6)

                    def finish_keys(g):
                        pe.wait_ge(fin_v, 1 + 3 * g + 1)
                        for h in range(2):
                            for mb in range(2):
                                for o in range(DT):
                                    last = pe.transpose(bank[h][:, o * D + mb * P:o * D + (mb + 1) * P], KVX[:, 2 * h + mb, o * P:(o + 1) * P], ident[:])
                        last.then_inc(fin_pe, 1)
                        pe.wait_ge(fin_v, 1 + 3 * g + 2)
                        for h in range(2):
                            for mb in range(2):
                                for o in range(DT):
                                    last = pe.matmul(bank[2 + 2 * h + mb][:, 0:D], KVXT[:, 2 * h + o, mb * P:(mb + 1) * P], WVO[:, 2 * h + o, :],
                                                     start=(o == 0), stop=(o == DT - 1))
                        last.then_inc(fin_pe, 1)
                        pe.wait_ge(fin_v, 1 + 3 * g + 3)

                    def edges(u, k0, k1, regs):
                        for k in range(k0, k1):
                            if first:
                                last = pe.matmul(bank[6][:, 8 * k:8 * k + 8], OHT[:, k * P:(k + 1) * P],
                                                 SIJ[:, bass.ds(regs[k], 1), :].rearrange("r a c -> r (a c)"), start=True, stop=True)
                                if k == 3:
                                    last.then_inc(sd_full, 1)
                            else:
                                par, n = edges.par, 4 * u + k
                                pe.wait_ge(o_used, done(n - 2))
                                pe.matmul(bank[6 + k % 2][0:R, 0:265], OH[:, par, k, :], RS[:, par, k, :], start=True, stop=True).then_inc(o_full, 1)

                    def make(ph):
                        kq = "kq"[ph]

                        def tile(t, par, B, Q, u):
                            if ph == 0 and zero(t):
                                for b in range(4):
                                    pe.matmul(bank[2 + b][:, 0:D + 1], zr[:], zw[:], start=True, stop=False, skip_group_check=True)
                            if ph == 1 and not zero(t):
                                pe.wait_ge(e_full, done(B - 1))
                                pe.wait_ge(phi_full, done(Q - 2))
                                for b in range(4):
                                    last = pe.transpose(bank[2][:, b * R:(b + 1) * R], EB[:, 1 - par, b * P:(b + 1) * P], ident[0:R, 0:R])
                                last.then_inc(e_used, 1)
                            regs = None
                            if first:
                                pe.wait_ge(oht_done, done(u))
                                pe.wait_ge(sd_kept, done(u - 1))
                                regs = steps_tiles(mybir.EngineType.PE, u)
                            elif not (isinstance(u, int) and u == 0):
                                pe.wait_ge(r_full, done(u - 1))
                            work = first or not (isinstance(u, int) and u == 0)
                            ue = u if first else u - 1
                            edges.par = 1 - par
                            if not last_(t):
                                pe.wait_ge(xtm_full, done(B))
                                pe.wait_ge(pj_used, done(B - 1))
                                for k in range(DT):
                                    pe.matmul(bank[0][0:R, :], xtm[:, par, k, :], WS[kq][:, k, :], start=(k == 0), stop=False)
                                pe.matmul(bank[0][0:R, :], ones3[:], b3[kq][:], start=False, stop=True).then_inc(pj_full, 1)
                            if work:
                                edges(ue, 0, 2, regs)
                            if not last_(t):
                                pe.wait_ge(e_full, done(B - 1))
                                for k in range(DT):
                                    pe.matmul(bank[1][0:R, :], xtm[:, par, k, :], MS[kq][:, k, :], start=(k == 0), stop=False)
                                pe.matmul(bank[1][0:R, :], ones3[:], b3["c" + kq][:], start=False, stop=True).then_inc(u2_full, 1)
                            if work:
                                edges(ue, 2, 4, regs)
                            if ph == 0 and not zero(t):
                                pe.wait_ge(e_full, done(B - 1))
                                for b in range(4):
                                    last = pe.matmul(bank[2 + b][:, 0:D + 1], EB[:, 1 - par, b * P:(b + 1) * P], row(XN, t - 1),
                                                     start=False, stop=last_(t), skip_group_check=True)
                                last.then_inc(e_used, 1)
                            if ph == 1 and not zero(t):
                                pe.wait_ge(phi_full, done(Q - 1))
                                pe.wait_ge(att_used, done(Q - 2))
                                for h in range(2):
                                    for mb in range(2):
                                        last = pe.matmul(bank[3 + h][0:R, 0:D + 1], PT[:, 2 * h + mb, :], KVO[:, 2 * h + mb, :],
                                                         start=(mb == 0), stop=(mb == 1))
                                last.then_inc(att_full, 1)
                        return tile

                    for g in (g0, g0 + 1):
                        setup(g)
                        run(pe, g, 0, make(0))
                        finish_keys(g)
                        run(pe, g, 1, make(1))
                    if not first:
                        pe.wait_ge(r_full, done(HALVES - 1))
                        edges.par = 1
                        edges(HALVES - 1, 0, 4, None)

                @block.scalar
                def _(act):
                    if first:
                        for s_ in (xtm_full, pj_used, nsq_full, e_full, phi_full):
                            act.sem_inc(s_, 2)

                    def setup(g):
                        act.wait_ge(set_pe, SPE * g + 2)
                        for h in range(2):
                            last = act.activation(WTs["q"][:, 2 * h:2 * h + 2, :], bank[2 + h][:].rearrange("p (c d) -> p c d", c=2), ACT.Copy)
                        last.then_inc(set_a, 1)
                        act.wait_ge(set_pe, SPE * g + 5)
                        for o in range(DT):
                            last = act.activation(MS["q"][:, o, :], bank[2 + o][:], ACT.Copy, scale=SCALE)
                        last.then_inc(set_a, 1)
                        act.wait_ge(set_pe, SPE * g + 7)

                    def make(ph):
                        def tile(t, par, B, Q, u):
                            if not last_(t):
                                act.wait_ge(u2_full, done(B - (1 if zero(t) else 2)))
                                act.activation(xtm[:, par], XNT[:, :, bass.ds(t * R, R)], ACT.Copy).then_inc(xtm_full, 1)
                            if ph == 1 and not zero(t):
                                act.wait_ge(e_used, done(B - 1))
                                act.wait_ge(att_full, done(Q - 2))
                                act.activation(PT[:], bank[2][:, 0:4 * R].rearrange("p (b r) -> p b r", b=4), ACT.Copy,
                                               scale=1.0 / 16, bias=EPS_ATT).then_inc(phi_full, 1)
                            if not last_(t):
                                act.wait_ge(pj_full, done(B))
                                act.wait_ge(e_used, done(B - (1 if zero(t) else 2)))
                                for h in range(2):
                                    last = act.activation(EB[:, par, h * D:(h + 1) * D], bank[0][0:R, h * D:(h + 1) * D], ACT.Square, scale=SCALE * 0.5 ** 0.5,
                                                          accum_out=sq[:, par, h:h + 1])
                                last.then_inc(pj_used, 1)
                                act.wait_ge(pj_used, done(B))
                                act.mul(nsq[:, par, :], sq[:, par, :], -1.0).then_inc(nsq_full, 1)
                                act.wait_ge(nsq_full, done(B))
                                act.wait_ge(u2_full, done(B))
                                for h in range(2):
                                    last = act.activation(EB[:, par, h * D:(h + 1) * D], bank[1][0:R, h * D:(h + 1) * D], ACT.Exp,
                                                          bias=nsq[:, par, h:h + 1])
                                last.then_inc(e_full, 1)
                        return tile

                    for g in (g0, g0 + 1):
                        setup(g)
                        run(act, g, 0, make(0))
                        run(act, g, 1, make(1))

                @block.vector
                def _(v):
                    c = Chain(v, v2 if first else v3)
                    if first:
                        for s_ in (oht_done, sd_kept, r_full, att_used, rz_full, acc_half, o_used):
                            v.sem_inc(s_, 2)
                        v.wait_ge(fin_pe, 1)
                        v.tensor_copy(projT[:], bank[5][:].rearrange("p (k m) -> p k m", k=DT)).then_inc(fin_v, 1)
                    for k in b3:
                        v.memset(b3[k][:], 0.0)
                    c(v.memset(ones3[:], 0.0))
                    for p_ in (0, 32, 64):
                        v.memset(ones3[p_:p_ + 1, :], 1.0)
                    v.wait_ge(p_ready, 1 if first else 2)
                    v.wait_ge(c_in, 64 if first else 112)

                    def three(name, src_):
                        c(v.tensor_copy(b3[name][0:1, :], src_))
                        c(v.tensor_tensor(rr, src_, b3[name][0:1, :], ALU.subtract))
                        c(v.tensor_copy(mid[:], rr))
                        c(v.tensor_copy(b3[name][32:33, :], mid[:]))
                        c(v.tensor_tensor(rr, rr, mid[:], ALU.subtract))
                        c(v.tensor_copy(b3[name][64:65, :], rr))

                    def setup(g):
                        c(v.tensor_copy(bcp[:], bc[:, :, 4 * g:4 * g + 4]))
                        v.tensor_copy(BVB, bcp[:, 2, :].unsqueeze(2).to_broadcast([P, 4, P])).then_inc(set_v, 1)
                        for k, n, s_ in (("k", 1, 0), ("v", 3, 4)):
                            v.wait_ge(set_pe, SPE * g + n)
                            for h in range(2):
                                last = v.tensor_copy(WTs[k][:, 2 * h:2 * h + 2, :], bank[s_ + h][:].rearrange("p (c d) -> p c d", c=2))
                            last.then_inc(set_v, 1)
                        v.wait_ge(set_pe, SPE * g + 4)
                        for o in range(DT):
                            last = v.tensor_scalar(MS["k"][:, o, :], bank[o][:], SCALE, None, ALU.mult)
                        last.then_inc(set_v, 1)
                        v.wait_ge(set_pe, SPE * g + 6)
                        for h in range(2):
                            last = v.tensor_copy(WVO[:, 2 * h:2 * h + 2, :], bank[4 + h][:].rearrange("p (o d) -> p o d", o=2))
                        last.then_inc(set_v, 1)
                        v.wait_ge(set_pe, SPE * g + 7)
                        v.wait_ge(wp_in, 96 * (g + 1))
                        c(v.tensor_copy(BVWO[:], bank[4][:]))
                        for i_, k in enumerate("kq"):
                            three(k, brow[:, i_, :])
                            c(v.tensor_scalar(brow[:, i_, :], bank[2 * i_][0:1, :], SCALE, None, ALU.mult))
                            three("c" + k, brow[:, i_, :])
                        v.sem_inc(set_v, 1)

                    def finish_keys(g):
                        v.wait_ge(e_used, done((2 * g + 1) * T - 1))
                        v.wait_ge(pj_used, done((2 * g + 1) * T - 1))
                        v.wait_ge(e_full, done((2 * g + 1) * T - 1))
                        for b in range(4):
                            last = v.scalar_tensor_tensor(out=KVX[:, b, :], in0=bank[2 + b][:, 0:D + 1], scalar=1.0 / 16, in1=CSE[:],
                                                          op0=ALU.mult, op1=ALU.add)
                        last.then_inc(fin_v, 1)
                        v.wait_ge(fin_pe, 1 + 2 * g + 1)
                        for h in range(2):
                            last = v.tensor_copy(KVXT[:, 2 * h:2 * h + 2, :], bank[h][:].rearrange("p (o m) -> p o m", o=2))
                        last.then_inc(fin_v, 1)
                        v.wait_ge(fin_pe, 1 + 2 * g + 2)
                        for b in range(4):
                            v.scalar_tensor_tensor(out=KVO[:, b, 0:D], in0=BVWO[:, (b // 2) * D:(b // 2 + 1) * D], scalar=KVX[:, b, D:D + 1],
                                                   in1=bank[2 + b][:, 0:D], op0=ALU.mult, op1=ALU.add)
                        v.tensor_copy(KVO[:, :, D:D + 1], KVX[:, :, D:D + 1]).then_inc(fin_v, 1)

                    def sums(u, regs):
                        for k in range(4):
                            v.wait_ge(o_full, 4 * u + k + 1)
                            if k:
                                v.wait_ge(o_used, done(4 * u + k - 1))
                            acc = GACC[0:R, bass.ds(regs[k], 1), :].rearrange("r a c -> r (a c)")
                            v.tensor_tensor(acc, bank[6 + k % 2][0:R, 0:265], acc, ALU.add).then_inc(o_used, 1)

                    def make(ph):
                        def tile(t, par, B, Q, u):
                            if not first and not (isinstance(u, int) and u == 0):
                                sums(u - 1, steps_tiles(mybir.EngineType.DVE, u - 1))
                            if first:
                                v.wait_ge(rb_in, 16 * (u + 1))
                                v.wait_ge(sd_full, done(u - 1))
                                v.tensor_scalar(OHT[:], RB[:], iota_p[0:R, :], None, ALU.is_equal).then_inc(oht_done, 1)
                            if ph == 1 and not zero(t):
                                v.wait_ge(att_full, done(Q - 1))
                                v.reciprocal(rz[:, 0:1], bank[3][0:R, D:D + 1])
                                v.reciprocal(rz[:, 1:2], bank[4][0:R, D:D + 1]).then_inc(rz_full, 1)
                                v.wait_ge(rz_full, done(Q - 1))
                                acc = row(ACC, t - 1)
                                v.scalar_tensor_tensor(out=acc, in0=bank[3][0:R, 0:D], scalar=rz[:, 0:1], in1=acc,
                                                       op0=ALU.mult, op1=ALU.add).then_inc(acc_half, 1)
                                v.wait_ge(acc_half, done(Q - 1))
                                v.scalar_tensor_tensor(out=acc, in0=bank[4][0:R, 0:D], scalar=rz[:, 1:2], in1=acc,
                                                       op0=ALU.mult, op1=ALU.add).then_inc(att_used, 1)
                            if first:
                                v.wait_ge(sd_full, done(u))
                                v.tensor_copy(SD[:, bass.ds(4 * u, 4), :], bank[6][:, 0:32].rearrange("p (s c) -> p s c", c=8)).then_inc(sd_kept, 1)
                            else:
                                if not (isinstance(u, int) and u < 2):
                                    v.wait_ge(o_full, 4 * (u - 1))
                                v.wait_ge(g_in[par], (64 * (u - par) // 2 if isinstance(u, int) else 32 * (u - par)) + 64)
                                rel4 = relT[:, bass.ds(4 * u, 4)].unsqueeze(2).to_broadcast([P, 4, R])
                                v.tensor_tensor(OH[:, par], iota_f[:, 0:R].unsqueeze(1).to_broadcast([P, 4, R]), rel4, ALU.is_equal)
                                at4 = AT[:, bass.ds(4 * u, 4), :]
                                v.tensor_copy(RS[:, par, :, D:], at4)
                                for k in range(4):
                                    last = v.tensor_tensor(RS[:, par, k, 0:D].rearrange("p (h d) -> p h d", h=GH),
                                                           G[par][:, k, :].rearrange("p (h d) -> p h d", h=GH),
                                                           AT[:, bass.ds(4 * u + k, 1), 0:GH].rearrange("p a h -> p (a h)").unsqueeze(2).to_broadcast([P, GH, DH]), ALU.mult)
                                last.then_inc(r_full, 1)
                        return tile

                    for g in (g0, g0 + 1):
                        setup(g)
                        run(v, g, 0, make(0))
                        finish_keys(g)
                        run(v, g, 1, make(1))
                    if not first:
                        sums(HALVES - 1, steps_tiles(mybir.EngineType.DVE, HALVES - 1))

        mixer_block(True)
        AT = sb("AT", [P, STEPS, 9])

        tr = sem("tr"); ev_v = sem("ev_v"); ev_a = sem("ev_a"); v4 = sem("v4"); ex_in = sem("ex_in"); ex_done = sem("ex_done")
        with ExitStack() as ctx:
            big = lambda name: sb(name, [P, GH, SB * P], ctx=ctx)
            XS, SI, SS, M, M2 = big("XS"), big("SI"), big("SS"), big("M"), big("M2")
            D0L = sb("D0L", [P, SB * P + 1], ctx=ctx)
            X0 = sb("X0", [P, GH, SB], ctx=ctx)
            CI = sb("CI", [P, SB, GH], ctx=ctx)
            TL = sb("TL", [P, SB, GH], ctx=ctx)
            AL = sb("AL", [P, SB], ctx=ctx)
            ALB = sb("ALB", [P, SB, GH], ctx=ctx)
            TR = sb("TR", [GH, SB * P], ctx=ctx)
            AR = sb("AR", [GH, SB * P], ctx=ctx)
            CR = sb("CR", [GH, SB * P + 1], ctx=ctx)
            FI = sb("FI", [P, SB * P], ctx=ctx)
            pen = PEN[:].rearrange("p b e -> p (b e)")
            d0 = D0[:].rearrange("p b e -> p (b e)")
            D00 = D0[:, :, 0:1].rearrange("p b e -> p (b e)")
            block = ctx.enter_context(nc.Block())

            @block.tensor
            def _(pe):
                def turn(banks, source):
                    for h in range(GH):
                        for b in range(SB):
                            last = pe.transpose(bank[banks + h][:, b * P:(b + 1) * P], source(b, h), ident[:])
                    last.then_inc(tr, 1)
                turn(0, lambda b, h: SJ[:, b * P:(b + 1) * P, h])
                turn(4, lambda b, h: SD[:, b * P:(b + 1) * P, h])
                pe.wait_ge(ev_v, 1)
                turn(0, lambda b, h: SD[:, b * P:(b + 1) * P, GH + h])
                n = 2
                for k in range(2):
                    pe.wait_ge(ev_v, n + 1)
                    if k == 0:
                        pe.wait_ge(ev_a, 1)
                    for b in range(SB):
                        pe.transpose(bank[4][0:GH, b * P:(b + 1) * P], TL[:, b, :], ident[:])
                        last = pe.transpose(bank[5][0:GH, b * P:(b + 1) * P], ALB[:, b, :], ident[:])
                    last.then_inc(tr, 1)
                    pe.wait_ge(ev_v, n + 2)
                    for b in range(SB):
                        last = pe.transpose(bank[6][:, b * GH:(b + 1) * GH], CR[:, k + b * P:k + (b + 1) * P], ident[0:GH, 0:GH])
                    last.then_inc(tr, 1)
                    n += 2

                def back(bank_, source):
                    for b in range(SB):
                        w = min(P, STEPS - b * P)
                        last = pe.transpose(bank[bank_][:, b * P:b * P + w], source(b)[0:w], ident[0:w, 0:w])
                    return last
                pe.wait_ge(ex_done, 1)
                for h in range(GH):
                    back(h, lambda b: XS[:, h, b * P:(b + 1) * P]).then_inc(tr, 1)
                pe.wait_ge(ev_v, n + 1)
                for h in range(GH):
                    back(4 + h, lambda b: SS[:, h, b * P:(b + 1) * P]).then_inc(tr, 1)
                pe.wait_ge(ev_v, n + 2)
                back(0, lambda b: FI[:, b * P:(b + 1) * P]).then_inc(tr, 1)

            @block.scalar
            def _(act):
                act.wait_ge(tr, 2)
                for h in range(GH):
                    last = act.activation(SI[:, h, :], bank[4 + h][:], ACT.Copy)
                last.then_inc(ev_a, 1)
                act.wait_ge(ex_in, 1)
                act.activation(XS[:], XS[:], ACT.Exp).then_inc(ex_done, 1)
                act.activation(SS[:], SS[:], ACT.Exp).then_inc(ex_done, 1)

            @block.vector
            def _(v):
                c = Chain(v, v4)
                c(v.tensor_copy(D0L[:, 0:SB * P], d0))
                c(v.memset(D0L[:, 0:SB * P].rearrange("p (b e) -> p b e", b=SB)[:, :, 0:1], -BIG))
                v.memset(D0L[:, SB * P:], -BIG)
                v.tensor_reduce(AL[:], D0[:], AX.X, ALU.min)
                c(v.tensor_scalar(FI[:], d0, -1.0, None, ALU.is_lt))
                c(v.tensor_copy(ALB[:], AL[:].unsqueeze(2).to_broadcast([P, SB, GH])))
                v.wait_ge(tr, 1)
                for h in range(GH):
                    last = v.tensor_tensor(XS[:, h, :], bank[h][:], pen, ALU.add)
                last.then_inc(ev_v, 1)
                v.wait_ge(tr, 3)
                for h in range(GH):
                    last = v.tensor_copy(SS[:, h, :], bank[h][:])
                last.then_inc(ev_v, 1)
                v.wait_ge(ev_v, 2)
                c(v.tensor_copy(X0[:], XS[:].rearrange("p h (b e) -> p h b e", b=SB)[:, :, :, 0]))

                def ends(buf, e):
                    return buf[:].rearrange("p h (b e) -> p h b e", b=SB)[:, :, :, e]

                def scan(out_, data, way):
                    for h in range(GH):
                        if way > 0:
                            last = v.tensor_tensor_scan(out_[:, h, :], D0L[:, 0:SB * P], data[:, h, :], -BIG, ALU.add, ALU.max)
                        else:
                            last = v.tensor_tensor_scan(out_[:, h, :][:, ::-1], D0L[:, 1:][:, ::-1], data[:, h, :][:, ::-1], -BIG, ALU.add, ALU.max)
                    c(last)

                bh = lambda ap: ap.rearrange("p h b -> p b h")
                d00 = D00.unsqueeze(2).to_broadcast([P, SB, GH])
                scan(M, XS, 1)
                v.tensor_copy(TL[:], bh(ends(M, P - 1))).then_inc(ev_v, 1)
                v.wait_ge(tr, 4)
                v.tensor_copy(TR[:], bank[4][0:GH, :])
                c(v.tensor_copy(AR[:], bank[5][0:GH, :]))
                c(v.memset(CR[:, 0:1], -BIG))
                v.tensor_tensor_scan(CR[:, 1:], AR[:], TR[:], -BIG, ALU.add, ALU.max).then_inc(ev_v, 1)
                v.wait_ge(tr, 5)
                c(v.tensor_tensor(CI[:], bank[6][:, 0:SB * GH].rearrange("p (b h) -> p b h", b=SB), d00, ALU.add))
                c(v.tensor_tensor(ends(XS, 0), ends(XS, 0), CI[:].rearrange("p b h -> p h b"), ALU.max))
                scan(M, XS, 1)
                c(v.tensor_copy(ends(XS, 0), X0[:]))
                scan(M2, M, -1)
                v.tensor_tensor(TL[:], bh(ends(M2, 0)), d00, ALU.add).then_inc(ev_v, 1)
                v.wait_ge(tr, 6)
                c(v.tensor_copy(TR[:], bank[4][0:GH, :]))
                c(v.memset(CR[:, SB * P:], -BIG))
                v.tensor_tensor_scan(CR[:, 0:SB * P][:, ::-1], AR[:, ::-1], TR[:, ::-1], -BIG, ALU.add, ALU.max).then_inc(ev_v, 1)
                v.wait_ge(tr, 7)
                c(v.tensor_tensor(ends(M, P - 1), ends(M, P - 1), bank[6][:, 0:SB * GH].rearrange("p (b h) -> p h b", b=SB), ALU.max))
                scan(M2, M, -1)
                c(v.tensor_tensor(M2[:], M2[:], SS[:], ALU.max))
                v.wait_ge(ev_a, 1)
                for buf in (XS, M2, SS):
                    last = v.tensor_tensor(buf[:], buf[:], SI[:], ALU.add)
                c(last)
                for buf in (XS, M2, SS):
                    last = v.scalar_tensor_tensor(out=buf[:], in0=buf[:], scalar=0.2, in1=buf[:], op0=ALU.mult, op1=ALU.max)
                c(last)
                for buf in (XS, SS):
                    last = v.tensor_tensor(buf[:], buf[:], M2[:], ALU.subtract)
                last.then_inc(ex_in, 1)
                v.wait_ge(ex_done, 2)
                v.tensor_tensor(SS[:], SS[:], FI[:].unsqueeze(1).to_broadcast([P, GH, SB * P]), ALU.mult).then_inc(ev_v, 1)
                for h in range(GH):
                    v.wait_ge(tr, 8 + h)
                    last = v.tensor_copy(AT[:, :, h], bank[h][:, 0:STEPS])
                last.then_inc(ev_v, 1)
                for h in range(GH):
                    v.wait_ge(tr, 8 + GH + h)
                    v.tensor_copy(AT[:, :, GH + h], bank[4 + h][:, 0:STEPS])
                v.wait_ge(tr, 8 + 2 * GH)
                v.tensor_copy(AT[:, :, 2 * GH], bank[0][:, 0:STEPS])

        mixer_block(False)

        buf_dram = nc.dram_tensor("buf_dram", (XE * SLOT, D), F32).ap()
        y_dram = nc.dram_tensor("y_dram", (XE * SLOT, D), F32).ap()
        g_dram = nc.dram_tensor("g_dram", (N, D), F32).ap()
        sums_ready = sem("sums_ready"); g_out = sem("g_out"); g_in = sem("g_in")
        slot = sb("slot", [R, T], I32)
        wgt = sb("wgt", [R, T])
        f_in = sem("f_in"); x2_in = sem("x2_in"); z_out = sem("z_out"); xn_used = sem("xn_used"); asr_ready = sem("asr_ready")
        nt_done = sem("nt_done"); v5 = sem("v5"); p5 = sem("p5"); st_n = sem("st_n"); sq_v = sem("sq_v"); sq_a = sem("sq_a"); gn_v = sem("gn_v"); gn_a = sem("gn_a")
        zset = sem("zset"); tri_ready = sem("tri_ready"); o1_ready = sem("o1_ready"); lg_done = sem("lg_done"); oh_ready = sem("oh_ready")
        cnt_done = sem("cnt_done"); sc_ready = sem("sc_ready"); sc_out = sem("sc_out")
        s_full = sem("s_full"); t_full = sem("t_full"); tt_full = sem("tt_full"); h_full = sem("h_full"); hr_full = sem("hr_full")
        m_full = sem("m_full"); m_used = sem("m_used")

        def over_tiles(eng, body):
            with eng.Fori(0, T // 2) as i:
                body(2 * i, 0)
                body(2 * i + 1, 1)
            body(T - 1, 0)

        with ExitStack() as ctx:
            mk = lambda name, shape, dt=F32: sb(name, shape, dt, ctx=ctx)
            NTB = mk("NTB", [R, T, D])
            RW = mk("RW", [R, 7, D])
            b1c = mk("b1c", [P, DT])
            W1s = mk("W1s", [P, DT, D]); W2s = mk("W2s", [P, DT, D])
            gw = mk("gw", [P, DT, XE]); gbr = mk("gbr", [R, XE])
            Z = mk("Z", [P, 8 * D])
            TRI = mk("TRI", [R, R])
            stg_ = mk("stg_", [R, 2, D])
            stT = mk("stT", [P, 2, DT, R])
            hT = mk("hT5", [P, 2, DT, R])
            s6 = mk("s6", [R, T, 6])
            sc = {k: mk("f_" + k, [R, T]) for k in ("mean", "dm", "var", "t1", "std", "rstd", "gn", "gr", "th", "gs", "mx", "sm", "prb", "idx", "pos", "kept", "sf", "drop")}
            q4 = {k: mk("q_" + k, [R, T, GH]) for k in ("as", "den", "r", "asr")}
            hm = mk("hm", [R, T])
            e8 = {k: mk("e_" + k, [R, T, XE]) for k in ("lg", "ex", "eq", "oh", "tot", "inc", "po")}
            one_t = mk("one_t", [R, T])
            sidx = mk("scidx", [R, T], I32)
            n = {k: b[:] for k, b in sc.items()}
            GN = GACC[0:R, :, 0:D]
            GN4 = GN.rearrange("r t (h d) -> r t h d", h=GH)
            XX = XN[:, :, 0:D]
            wide = lambda k: RW[:, k, :].unsqueeze(1).to_broadcast([R, T, D])
            over = lambda ap: ap.unsqueeze(2).to_broadcast([R, T, D])
            block = ctx.enter_context(nc.Block())

            @block.sync
            def _(sp):
                sp.dma_start(NTB[:], ft_dram.rearrange("(t r) d -> r t d", r=R)).then_inc(f_in, 16)
                for k, a_ in enumerate((bo, g1, beta1, bias2, g2, beta2, gbc)):
                    sp.dma_start(RW[:, k, :], bcast(a_, R, D)).then_inc(f_in, 16)
                with nc.allow_non_contiguous_dma("bias column"):
                    sp.dma_start(b1c[:], bias1.rearrange("(o p) -> p o", p=P)).then_inc(f_in, 16)
                sp.dma_start(W1s[:], W1.rearrange("(k p) f -> p k f", p=P)).then_inc(f_in, 16)
                sp.dma_start(W2s[:], W2.rearrange("(k p) f -> p k f", p=P)).then_inc(f_in, 16)
                sp.dma_start(gw[:], gate_w.rearrange("(k p) e -> p k e", p=P)).then_inc(f_in, 16)
                sp.dma_start(gbr[:], bcast(gate_b, R, XE)).then_inc(f_in, 16)
                sp.wait_ge(zset, 1)
                for k in range(4):
                    sp.dma_start(buf_dram[k * 1024:(k + 1) * 1024, :].rearrange("(p j) d -> p (j d)", p=P), Z[:]).then_inc(z_out, 16)
                sp.wait_ge(sums_ready, 1)
                for h in range(GH):
                    sp.dma_start(bass.AP(g_dram.tensor, h * N * DH, [[DH, R], [R * DH, T], [1, DH]]), GN4[:, :, h, :]).then_inc(g_out, 16)
                sp.wait_ge(g_out, 16 * GH)
                sp.dma_start(GN, g_dram.rearrange("(t r) d -> r t d", r=R)).then_inc(g_in, 16)
                sp.wait_ge(xn_used, 1)
                sp.dma_start(XX, x.rearrange("(t r) d -> r t d", r=R)).then_inc(x2_in, 16)

            @block.gpsimd
            def _(pool):
                c = Chain(pool, p5)
                pool.memset(Z[:], 0.0).then_inc(zset, 1)
                c(pool.memset(TRI[:], 1.0))
                pool.affine_select(out=TRI[:], in_=TRI[:], compare_op=ALU.is_ge, fill=0.0, base=0, pattern=[[1, R]],
                                   channel_multiplier=-1).then_inc(tri_ready, 1)
                pool.wait_ge(asr_ready, 1)
                pool.wait_ge(f_in, 16 * 13)
                nt4 = NTB[:].rearrange("r t (h d) -> r t h d", h=GH)
                pool.tensor_tensor(nt4, nt4, q4["asr"][:].unsqueeze(3).to_broadcast([R, T, GH, DH]), ALU.mult).then_inc(nt_done, 1)
                pool.wait_ge(sc_ready, 1)
                pool.wait_ge(z_out, 64)
                for t in range(T):
                    pool.indirect_dma_start(out=buf_dram, out_offset=bass.IndirectOffsetOnAxis(ap=sidx[:, t:t + 1], axis=0),
                                            in_=ACC[:, t, :], in_offset=None, bounds_check=XE * SLOT - 1, oob_is_err=False).then_inc(sc_out, 16)
                pool.wait_ge(sc_out, 16 * T)

            @block.tensor
            def _(pe):
                pe.sem_inc(t_full, 2); pe.sem_inc(h_full, 2); pe.sem_inc(m_full, 2)
                pe.wait_ge(f_in, 16 * 13)
                pe.wait_ge(tri_ready, 1)

                def turn(n_, par):
                    pe.wait_ge(s_full, done(n_))
                    pe.wait_ge(tt_full, done(n_ - 1))
                    for k in range(DT):
                        last = pe.transpose(bank[0][:, k * P:k * P + R], stg_[:, par, k * P:(k + 1) * P], ident[0:R, 0:R])
                    last.then_inc(t_full, 1)
                    pe.wait_ge(tt_full, done(n_))

                def mlp(t, par):
                    turn(t, par)
                    pe.wait_ge(hr_full, done(t - 1))
                    for f in range(DT):
                        for k in range(DT):
                            last = pe.matmul(bank[1][:, f * P:f * P + R], W1s[:, k, f * P:(f + 1) * P], stT[:, par, k, :], start=(k == 0), stop=(k == 1))
                    last.then_inc(h_full, 1)
                    pe.wait_ge(hr_full, done(t))
                    pe.wait_ge(m_used, done(t - 1))
                    for f in range(DT):
                        last = pe.matmul(bank[2][0:R, 0:D], hT[:, par, f, :], W2s[:, f, :], start=(f == 0), stop=(f == 1))
                    last.then_inc(m_full, 1)
                over_tiles(pe, mlp)

                def gates(t, par):
                    turn(T + t, par)
                    for k in range(DT):
                        last = pe.matmul(bank[3][0:R, bass.ds(t * XE, XE)], stT[:, par, k, :], gw[:, k, :], start=(k == 0), stop=(k == 1))
                    last.then_inc(lg_done, 1)
                over_tiles(pe, gates)
                pe.wait_ge(oh_ready, 1)
                oh = e8["oh"][:].rearrange("r t e -> r (t e)")
                pe.matmul(bank[4][0:R, 0:T * XE], TRI[:], oh, start=True, stop=True)
                pe.matmul(bank[5][0:R, 0:T * XE], ones[0:R, 0:R], oh, start=True, stop=True).then_inc(cnt_done, 1)

            @block.scalar
            def _(act):
                act.sem_inc(s_full, 2); act.sem_inc(tt_full, 2); act.sem_inc(hr_full, 2)
                act.wait_ge(f_in, 16 * 13)
                act.wait_ge(sq_v, 1)
                act.activation(n["std"], n["t1"], ACT.Sqrt).then_inc(sq_a, 1)
                act.wait_ge(o1_ready, 1)

                def stage(t, n_, par):
                    act.wait_ge(t_full, done(n_ - 2))
                    act.activation(stg_[:, par, :], row(ACC, t), ACT.Copy).then_inc(s_full, 1)
                    act.wait_ge(t_full, done(n_))
                    act.activation(stT[:, par], bank[0][:, 0:D].rearrange("p (k r) -> p k r", k=DT)[:, :, 0:R], ACT.Copy).then_inc(tt_full, 1)

                def mlp(t, par):
                    stage(t, t, par)
                    act.wait_ge(h_full, done(t))
                    for f in range(DT):
                        last = act.activation(hT[:, par, f, :], bank[1][:, f * P:f * P + R], ACT.Relu, bias=b1c[:, f:f + 1])
                    last.then_inc(hr_full, 1)
                over_tiles(act, mlp)
                act.wait_ge(sq_v, 2)
                act.activation(n["std"], n["t1"], ACT.Sqrt).then_inc(sq_a, 1)
                act.wait_ge(gn_v, 1)
                act.activation(GN, GN, ACT.Relu).then_inc(gn_a, 1)
                act.wait_ge(gn_a, 1)
                act.activation(NTB[:], GN, ACT.Square).then_inc(gn_a, 1)
                act.wait_ge(gn_v, 2)
                act.activation(n["gr"], n["gn"], ACT.Sqrt).then_inc(gn_a, 1)
                act.wait_ge(gn_v, 3)
                act.activation(n["th"], n["gr"], ACT.Tanh).then_inc(gn_a, 1)
                act.wait_ge(sq_v, 3)
                act.activation(n["std"], n["t1"], ACT.Sqrt).then_inc(sq_a, 1)
                act.wait_ge(o1_ready, 2)
                over_tiles(act, lambda t, par: stage(t, T + t, par))
                act.wait_ge(gn_v, 4)
                act.activation(e8["ex"][:], e8["lg"][:], ACT.Exp).then_inc(gn_a, 1)

            @block.vector
            def _(v):
                c = Chain(v, v5)
                v.sem_inc(m_used, 2)
                v.memset(one_t[:], 1.0)
                c(v.tensor_scalar(hm[:], GACC[0:R, :, 264], -1.0, 1.0, ALU.mult, ALU.add))
                c(v.tensor_tensor(q4["as"][:], GACC[0:R, :, 260:264], hm[:].unsqueeze(2).to_broadcast([R, T, GH]), ALU.add))
                c(v.tensor_tensor(q4["den"][:], GACC[0:R, :, 256:260], q4["as"][:], ALU.add))
                c(v.tensor_scalar(q4["den"][:], q4["den"][:], MIN_NORM, None, ALU.max))
                c(v.reciprocal(q4["r"][:], q4["den"][:]))
                v.tensor_tensor(q4["asr"][:], q4["as"][:], q4["r"][:], ALU.mult).then_inc(asr_ready, 1)
                c(v.tensor_tensor(ACC[:], ACC[:], XX, ALU.add))
                v.sem_inc(xn_used, 1)
                v.wait_ge(f_in, 16 * 13)
                c(v.tensor_tensor(ACC[:], ACC[:], wide(0), ALU.add))

                def norm(buf, out_, eps, k):
                    with v.Fori(0, T // 2) as i:
                        for p_ in range(2):
                            v.bn_stats(row(s6, 2 * i + p_), row(buf, 2 * i + p_)[:, 0:D]).then_inc(st_n, 1)
                    v.bn_stats(row(s6, T - 1), row(buf, T - 1)[:, 0:D]).then_inc(st_n, 1)
                    v.wait_ge(st_n, k * T)
                    s = [s6[:, :, j] for j in range(6)]
                    c(v.tensor_tensor(n["mean"], s[1], s[4], ALU.add))
                    c(v.tensor_scalar(n["mean"], n["mean"], 0.5, None, ALU.mult))
                    c(v.tensor_tensor(n["dm"], s[1], s[4], ALU.subtract))
                    c(v.tensor_tensor(n["dm"], n["dm"], n["dm"], ALU.mult))
                    c(v.tensor_tensor(n["var"], s[2], s[5], ALU.add))
                    c(v.tensor_scalar(n["var"], n["var"], 1.0 / D, eps, ALU.mult, ALU.add))
                    v.scalar_tensor_tensor(out=n["t1"], in0=n["dm"], scalar=0.25, in1=n["var"], op0=ALU.mult, op1=ALU.add).then_inc(sq_v, 1)
                    v.wait_ge(sq_a, k)
                    c(v.reciprocal(n["rstd"], n["std"]))

                    def one(t, par):
                        return v.tensor_scalar(row(out_, t)[:, 0:D], row(buf, t)[:, 0:D], sc["mean"][:, bass.ds(t, 1)], sc["rstd"][:, bass.ds(t, 1)],
                                               ALU.subtract, ALU.mult)
                    with v.Fori(0, T // 2) as i:
                        one(2 * i, 0)
                        one(2 * i + 1, 1)
                    c(one(T - 1, 0))

                norm(ACC, ACC, 1e-6, 1)
                c(v.tensor_tensor(ACC[:], ACC[:], wide(1), ALU.mult))
                c(v.tensor_tensor(ACC[:], ACC[:], wide(2), ALU.add))
                v.sem_inc(o1_ready, 1)

                c(v.tensor_tensor(GN4, GN4, q4["r"][:].unsqueeze(3).to_broadcast([R, T, GH, DH]), ALU.mult))
                v.wait_ge(nt_done, 1)
                v.tensor_tensor(GN, GN, NTB[:], ALU.add).then_inc(sums_ready, 1)

                def add_mlp(t, par):
                    v.wait_ge(m_full, done(t))
                    v.tensor_tensor(row(ACC, t), bank[2][0:R, 0:D], row(ACC, t), ALU.add).then_inc(m_used, 1)
                over_tiles(v, add_mlp)
                v.wait_ge(m_used, done(T - 1))
                c(v.tensor_tensor(ACC[:], ACC[:], wide(3), ALU.add))
                v.wait_ge(g_in, 16)
                v.tensor_tensor(GN, GN, wide(6), ALU.add).then_inc(gn_v, 1)
                norm(ACC, ACC, 1e-6, 2)
                c(v.tensor_tensor(ACC[:], ACC[:], wide(4), ALU.mult))
                c(v.tensor_tensor(ACC[:], ACC[:], wide(5), ALU.add))
                v.wait_ge(x2_in, 16)
                c(v.tensor_tensor(XX, XX, ACC[:], ALU.add))
                v.wait_ge(gn_a, 2)
                v.tensor_reduce(n["gn"], NTB[:], AX.X, ALU.add).then_inc(gn_v, 1)
                v.wait_ge(gn_a, 3)
                v.tensor_scalar(n["gr"], n["gr"], MIN_NORM, None, ALU.max).then_inc(gn_v, 1)
                v.wait_ge(gn_v, 3)
                c(v.reciprocal(n["gs"], n["gr"]))
                v.wait_ge(gn_a, 4)
                c(v.tensor_scalar(n["th"], n["th"], MAXN, None, ALU.min))
                c(v.tensor_tensor(n["gs"], n["gs"], n["th"], ALU.mult))
                c(v.tensor_tensor(GN, GN, over(n["gs"]), ALU.mult))
                c(v.tensor_tensor(XX, XX, GN, ALU.add))
                norm(XN, ACC, 1e-5, 3)
                v.sem_inc(o1_ready, 1)

                v.wait_ge(lg_done, T)
                lg, oh = e8["lg"][:], e8["oh"][:]
                c(v.tensor_tensor(lg, bank[3][0:R, 0:T * XE].rearrange("r (t e) -> r t e", e=XE), gbr[:].unsqueeze(1).to_broadcast([R, T, XE]), ALU.add))
                c(v.tensor_reduce(n["mx"], lg, AX.X, ALU.max))
                over8 = lambda ap: ap.unsqueeze(2).to_broadcast([R, T, XE])
                v.tensor_tensor(lg, lg, over8(n["mx"]), ALU.subtract).then_inc(gn_v, 1)
                v.wait_ge(gn_v, 4)
                c(v.tensor_scalar(e8["eq"][:], lg, 0.0, None, ALU.is_equal))
                c(v.scalar_tensor_tensor(out=e8["eq"][:], in0=e8["eq"][:], scalar=-float(XE), in1=iota_f[0:R, XE:2 * XE].unsqueeze(1).to_broadcast([R, T, XE]),
                                         op0=ALU.mult, op1=ALU.add))
                c(v.tensor_reduce(n["idx"], e8["eq"][:], AX.X, ALU.min))
                v.tensor_tensor(oh, iota_f[0:R, 0:XE].unsqueeze(1).to_broadcast([R, T, XE]), over8(n["idx"]), ALU.is_equal).then_inc(oh_ready, 1)
                v.wait_ge(gn_a, 5)
                c(v.tensor_reduce(n["sm"], e8["ex"][:], AX.X, ALU.add))
                c(v.reciprocal(n["prb"], n["sm"]))
                v.wait_ge(cnt_done, 1)
                v.wait_ge(oh_ready, 1)
                c(v.tensor_copy(e8["tot"][:], bank[5][0:R, 0:T * XE].rearrange("r (t e) -> r t e", e=XE)))
                for e in range(XE):
                    last = v.tensor_tensor_scan(e8["inc"][:, :, e], one_t[:], e8["tot"][:, :, e], 0.0, ALU.mult, ALU.add)
                c(last)
                c(v.tensor_tensor(e8["inc"][:], e8["inc"][:], e8["tot"][:], ALU.subtract))
                c(v.tensor_tensor(e8["po"][:], bank[4][0:R, 0:T * XE].rearrange("r (t e) -> r t e", e=XE), e8["inc"][:], ALU.add))
                c(v.tensor_tensor(e8["po"][:], e8["po"][:], oh, ALU.mult))
                c(v.tensor_reduce(n["pos"], e8["po"][:], AX.X, ALU.add))
                c(v.tensor_scalar(n["kept"], n["pos"], CAP + 0.5, None, ALU.is_lt))
                c(v.tensor_scalar(n["pos"], n["pos"], float(CAP), -1.0, ALU.min, ALU.add))
                c(v.scalar_tensor_tensor(out=n["sf"], in0=n["idx"], scalar=float(SLOT), in1=n["pos"], op0=ALU.mult, op1=ALU.add))
                c(v.tensor_scalar(n["drop"], n["kept"], -float(XE * SLOT), float(XE * SLOT), ALU.mult, ALU.add))
                c(v.tensor_tensor(n["drop"], n["drop"], n["sf"], ALU.add))
                c(v.tensor_copy(slot[:], n["sf"]))
                c(v.tensor_copy(sidx[:], n["drop"]))
                v.tensor_tensor(wgt[:], n["prb"], n["kept"], ALU.mult).then_inc(sc_ready, 1)

        w_full = [sem("w_full0"), sem("w_full1")]
        bt_full = sem("bt_full"); bT_full = sem("bT_full"); y_full = sem("y_full"); y_out = [sem("y_out0"), sem("y_out1")]; y_free = sem("y_free")
        hp_full = sem("hp_full"); hh_full = sem("hh_full"); yp_full = sem("yp_full"); yy_full = sem("yy_full")
        with ExitStack() as ctx:
            mk = lambda name, shape, dt=F32: sb(name, shape, dt, ctx=ctx)
            W1e = mk("W1e", [P, 2, DT, FF]); W2e = mk("W2e", [P, 2, FF // P, D])
            b1e = mk("b1e", [P, 2, FF // P]); b2e = mk("b2e", [P, 2, D])
            BE = mk("BE", [P, 2, 4, D]); BT = XNT[:, :, 0:SLOT]
            H = mk("H", [P, FF // P, CAP])
            Y = mk("Y", [P, 2, 4, D])
            NF, NQ, LASTQ = FF // P, 4, CAP - 3 * P
            block = ctx.enter_context(nc.Block())

            def experts(eng, body):
                with eng.Fori(0, XE // 2) as i:
                    body(2 * i, 0, i)
                    body(2 * i + 1, 1, i)

            @block.sync
            def _(sp):
                def load(e, par, i):
                    sp.wait_ge(y_full, done(e - 2))
                    one = bass.ds(e, 1)
                    sp.dma_start(BE[:, par], buf_dram.rearrange("(e j p) d -> e p j d", e=XE, p=P)[one].rearrange("e p j d -> (e p) j d")).then_inc(w_full[par], 16)
                    sp.dma_start(W1e[:, par], w1.rearrange("e (k p) f -> e p k f", p=P)[one].rearrange("e p k f -> (e p) k f")).then_inc(w_full[par], 16)
                    sp.dma_start(W2e[:, par], w2.rearrange("e (c p) d -> e p c d", p=P)[one].rearrange("e p c d -> (e p) c d")).then_inc(w_full[par], 16)
                    with nc.allow_non_contiguous_dma("bias column"):
                        sp.dma_start(b1e[:, par], b1.rearrange("e (c p) -> e p c", p=P)[one].rearrange("e p c -> (e p) c")).then_inc(w_full[par], 16)
                    sp.dma_start(b2e[:, par], bass.AP(b2.tensor, e * D, [[0, P], [1, D]])).then_inc(w_full[par], 16)
                experts(sp, load)
                sp.wait_ge(y_out[0], 16 * (XE // 2))
                sp.wait_ge(y_out[1], 16 * (XE // 2))

            @block.gpsimd
            def _(pool):
                def store(e, par, i):
                    pool.wait_ge(y_full, done(e))
                    rows = y_dram.rearrange("(e j p) d -> e p j d", e=XE, p=P)[bass.ds(e, 1)].rearrange("e p j d -> (e p) j d")
                    pool.dma_start(rows, Y[:, par]).then_inc(y_out[par], 16)
                    pool.wait_ge(y_out[par], 16 * (i + 1))
                    pool.sem_inc(y_free, 1)
                pool.memset(Y[:, :, 3, :], 0.0).then_inc(y_free, 2)
                experts(pool, store)

            @block.tensor
            def _(pe):
                pe.sem_inc(bt_full, 2); pe.sem_inc(hp_full, 8); pe.sem_inc(yp_full, 4)

                def expert(e, par, i):
                    pe.wait_ge(w_full[par], 80 * (i + 1))
                    pe.wait_ge(bT_full, done(e - 1))
                    for k in range(DT):
                        for j in range(4):
                            last = pe.transpose(bank[k][:, j * P:(j + 1) * P], BE[:, par, j, k * P:(k + 1) * P], ident[:])
                    last.then_inc(bt_full, 1)
                    pe.wait_ge(bT_full, done(e))
                    for f in range(NF):
                        pe.wait_ge(hh_full, NF * e + f + 8 - 3)
                        for k in range(DT):
                            last = pe.matmul(bank[2 + f % 4][:, 0:CAP], W1e[:, par, k, f * P:(f + 1) * P], BT[:, k, 0:CAP], start=(k == 0), stop=(k == 1))
                        last.then_inc(hp_full, 1)
                    pe.wait_ge(hh_full, NF * e + NF + 8)
                    for j in range(NQ):
                        m = P if j < 3 else LASTQ
                        pe.wait_ge(yy_full, NQ * e + j + 4 - 1)
                        for f in range(NF):
                            last = pe.matmul(bank[6 + j % 2][0:m, 0:D], H[:, f, j * P:j * P + m], W2e[:, par, f, :], start=(f == 0), stop=(f == NF - 1))
                        last.then_inc(yp_full, 1)
                experts(pe, expert)

            @block.scalar
            def _(act):
                act.sem_inc(bT_full, 2); act.sem_inc(hh_full, 8)

                def expert(e, par, i):
                    act.wait_ge(bt_full, done(e))
                    act.wait_ge(yp_full, NQ * e + 4)
                    for k in range(DT):
                        last = act.activation(BT[:, k, :], bank[k][:], ACT.Copy)
                    last.then_inc(bT_full, 1)
                    for f in range(NF):
                        act.wait_ge(hp_full, NF * e + f + 9)
                        act.activation(H[:, f, :], bank[2 + f % 4][:, 0:CAP], ACT.Relu, bias=b1e[:, par, f:f + 1]).then_inc(hh_full, 1)
                experts(act, expert)

            @block.vector
            def _(v):
                v.sem_inc(y_full, 2); v.sem_inc(yy_full, 4)

                def expert(e, par, i):
                    v.wait_ge(y_free, done(e - 2))
                    for j in range(NQ):
                        m = P if j < 3 else LASTQ
                        v.wait_ge(yp_full, NQ * e + j + 5)
                        ins = v.tensor_tensor(Y[0:m, par, j, :], bank[6 + j % 2][0:m, 0:D], b2e[0:m, par, :], ALU.add)
                        ins.then_inc(yy_full, 1)
                    v.wait_ge(yy_full, NQ * e + NQ + 4)
                    v.sem_inc(y_full, 1)
                experts(v, expert)

        yg_in = [sem("yg_in0"), sem("yg_in1")]; ot_done = sem("ot_done"); ot_out = sem("ot_out"); alt_seen = sem("alt_seen"); v7 = sem("v7")
        with ExitStack() as ctx:
            mk = lambda name, shape, dt=F32: sb(name, shape, dt, ctx=ctx)
            YG = GACC[0:R, :, 0:D]
            yw = mk("yw", [R, 2, D]); pos_ = mk("pos_", [R, 2, D]); neg_ = mk("neg_", [R, 2, D]); alt = mk("alt", [R, 2, D])
            fin = mk("fin", [R, 2, D], I32)
            block = ctx.enter_context(nc.Block())

            @block.gpsimd
            def _(pool):
                for t in range(T):
                    pool.indirect_dma_start(out=YG[:, t, :], out_offset=None, in_=y_dram,
                                            in_offset=bass.IndirectOffsetOnAxis(ap=slot[:, t:t + 1], axis=0)).then_inc(yg_in[0], 16)

            @block.vector
            def _(v):
                c = Chain(v, v7)
                v.wait_ge(yg_in[0], 16 * T)

                def tile(t, par):
                    y = yw[:, par, :]
                    c(v.tensor_scalar(y, row(YG, t), wgt[:, bass.ds(t, 1)], None, ALU.mult))
                    v.tensor_scalar(fin[:, par, :], y, 0.0, 0.0, ALU.mult, ALU.is_equal)
                    v.tensor_scalar(pos_[:, par, :], y, 0.0, 1.0e4, ALU.max, ALU.min)
                    c(v.tensor_scalar(neg_[:, par, :], y, 0.0, -1.0e4, ALU.min, ALU.max))
                    c(v.tensor_tensor(alt[:, par, :], pos_[:, par, :], neg_[:, par, :], ALU.add))
                    v.sem_inc(alt_seen, 1)
                    c(v.copy_predicated(alt[:, par, :], fin[:, par, :], y))
                    v.tensor_tensor(row(XN, t)[:, 0:D], row(XN, t)[:, 0:D], alt[:, par, :], ALU.add).then_inc(ot_done, 1)
                with v.Fori(0, T // 2) as i:
                    c.enter(i, 8)
                    tile(2 * i, 0)
                    tile(2 * i + 1, 1)
                c.leave(T // 2)
                tile(T - 1, 0)

            @block.sync
            def _(sp):
                for k in range(5):
                    sp.wait_ge(ot_done, 5 * (k + 1))
                    sp.dma_start(out[5 * k * R:5 * (k + 1) * R, :].rearrange("(t r) d -> r t d", r=R), XN[:, 5 * k:5 * k + 5, 0:D]).then_inc(ot_out, 16)
                sp.wait_ge(ot_out, 80)


_INS = ['x', 'src', 'dst', 'L0_gnn_W', 'L0_gnn_b_lin', 'L0_gnn_att', 'L0_gnn_b_conv', 'L0_mix_Wq', 'L0_mix_bq',
        'L0_mix_Wk', 'L0_mix_bk', 'L0_mix_Wv', 'L0_mix_bv', 'L0_mix_Wo', 'L0_mix_bo', 'L0_mix_proj', 'L0_mix_W1',
        'L0_mix_bias1', 'L0_mix_W2', 'L0_mix_bias2', 'L0_mix_g1', 'L0_mix_beta1', 'L0_mix_g2', 'L0_mix_beta2',
        'L0_ffn_gate_w', 'L0_ffn_gate_b', 'L0_ffn_w1', 'L0_ffn_b1', 'L0_ffn_w2', 'L0_ffn_b2']
_OUTS = [((3125, 256), 'float32')]


def kernel(**inputs):
    import numpy as _np
    import concourse.bacc as _bacc
    from concourse import mybir as _mybir
    from concourse.bass_utils import run_bass_kernel_spmd as _run

    nc = _bacc.Bacc("TRN2", target_bir_lowering=False, num_devices=1)
    arrays, args = {}, []
    for name in _INS:
        a = _np.ascontiguousarray(inputs[name])
        arrays[f"in_{name}_dram"] = a
        args.append(nc.dram_tensor(f"in_{name}_dram", a.shape, _mybir.dt.from_np(a.dtype), kind="ExternalInput").ap())
    for i, (shape, dtype) in enumerate(_OUTS):
        dt = _mybir.dt.from_np(_np.dtype(dtype))
        args.append(nc.dram_tensor(f"out_{i}_dram", shape, dt, kind="ExternalOutput").ap())
    build(nc, *args)
    r = _run(nc, [arrays], core_ids=[0])
    got = tuple(r.results[0][f"out_{i}_dram"] for i in range(len(_OUTS)))
    return got[0]
```

```python
from contextlib import ExitStack

import numpy as np
import concourse.bass as bass
from concourse import mybir

ALU = mybir.AluOpType
ACT = mybir.ActivationFunctionType
F32 = mybir.dt.float32
BF16 = mybir.dt.bfloat16
I32 = mybir.dt.int32
AX = mybir.AxisListType

P = 128
N, D, E = 3125, 256, 50000
T, R = 25, 125
DT = D // P
CH = -(-E // P)
STEPS = 416
GS = 8
NG = STEPS // GS
SB = 4
GH = 4
DH = D // GH
MH = 8
PAIRS = MH // 2
PW = 2 * D
BIG = 1.0e30
MIN_NORM = 1e-15
MAXN = 1.0 - 0.004
EPS_ATT = 1e-6
SCALE = float(D) ** -0.25
ATANH_MAX = float(np.float32(1.0 - 1e-7))
XE, FF = 8, 1024
CAP = 489
SLOT = 512


class Chain:

    def __init__(self, eng, sem):
        self.eng, self.sem, self.base, self.n = eng, sem, 0, 0

    def __call__(self, ins):
        ins.then_inc(self.sem, 1)
        self.n += 1
        self.eng.wait_ge(self.sem, self.base + self.n)

    def enter(self, i, k):
        self.outer = (self.base, self.n)
        self.base = i * k + (self.base + self.n)
        self.n, self.k = 0, k

    def leave(self, count):
        assert self.n == self.k, (self.n, self.k)
        base, n = self.outer
        self.base, self.n = base, n + count * self.k


def done(t):
    return t + 3


def bcast(ap, rows, cols, offset=0):
    return bass.AP(ap.tensor, offset, [[0, rows], [1, cols]])


def build(nc, x, src, dst, gW, gb, gatt, gbc, Wq, bq, Wk, bk, Wv, bv, Wo, bo, proj, W1, bias1, W2, bias2,
          g1, beta1, g2, beta2, gate_w, gate_b, w1, b1, w2, b2, out):
    top = ExitStack()
    with top:
        def sb(name, shape, dt=F32, ctx=top):
            return ctx.enter_context(nc.sbuf_tensor(name, shape, dt))

        def pb(name, shape, dt=F32, ctx=top):
            return ctx.enter_context(nc.psum_tensor(name, shape, dt))

        def sem(name):
            return top.enter_context(nc.semaphore(name))

        lx_dram = nc.dram_tensor("lx_dram", (N, D), F32).ap()
        ft_dram = nc.dram_tensor("ft_dram", (N, D), F32).ap()
        sj_dram = nc.dram_tensor("sj_dram", (N, GH), F32).ap()
        er_dram = nc.dram_tensor("er_dram", (CH, 1 + 2 * P), I32).ap()
        rel_dram = nc.dram_tensor("rel_dram", (SB * P, P), BF16).ap()

        XN = sb("XN", [R, T, D + 1])
        XNT = sb("XNT", [P, DT, N])
        ACC = sb("ACC", [R, T, D])
        GACC = sb("GACC", [P, T, 265])
        SIJ = sb("SIJ", [R, T, 2 * GH])
        ident = sb("ident", [P, P])
        ones = sb("ones", [P, P])
        iota_p = sb("iota_p", [P, 1])
        iota_f = sb("iota_f", [P, P])
        CSE = sb("CSE", [P, D + 1])
        idxT = sb("idxT", [P, STEPS], I32)
        relT = sb("relT", [P, STEPS])
        PEN = sb("PEN", [P, SB, P])
        D0 = sb("D0", [P, SB, P])
        tI = sb("tI", [1, STEPS], I32)

        bank = [pb(f"bank{i}", [P, 512]) for i in range(8)]

        x_in = sem("x_in"); w_in = sem("w_in"); e_in = sem("e_in"); er_ready = sem("er_ready")
        v1 = sem("v1"); a1s = sem("a1s"); p1 = sem("p1"); const_ready = sem("const_ready")
        xns_full = sem("xns_full"); xns_kept = sem("xns_kept"); xt_full = sem("xt_full"); xts_full = sem("xts_full")
        xts_kept = sem("xts_kept"); u_full = sem("u_full"); u_kept = sem("u_kept"); sq_done = sem("sq_done")
        hbs_full = sem("hbs_full"); lx_done = sem("lx_done"); sij_done = sem("sij_done")
        stat_n = sem("stat_n"); cs_full = sem("cs_full")
        pre_psum = sem("pre_psum"); pre_used = sem("pre_used"); sc_v = sem("sc_v"); sc_a = sem("sc_a")
        hb2 = sem("hb2"); lx_ready = sem("lx_ready"); lx_out = sem("lx_out"); nt_in = sem("nt_in")
        sij_ready = sem("sij_ready"); tab_out = sem("tab_out"); cf_psum = sem("cf_psum"); cf_used = sem("cf_used")
        ci_ready = sem("ci_ready"); er_rows = sem("er_rows"); rel_ready = sem("rel_ready"); rel_out = sem("rel_out")
        eT_psum = sem("eT_psum"); eT_used = sem("eT_used")

        with ExitStack() as ctx:
            Wn = sb("Wn", [P, DT, D], ctx=ctx)
            WT = sb("WT", [P, DT, D + 1], ctx=ctx)
            bcol = sb("bcol", [P, DT], ctx=ctx)
            hbcol = sb("hbcol", [P, DT], ctx=ctx)
            hbrow = sb("hbrow", [R, D], ctx=ctx)
            attr = sb("attr", [R, 2, GH, DH], ctx=ctx)
            st6 = sb("st6", [R, T, 6], ctx=ctx)
            xns = sb("xns", [R, 2, D + 1], ctx=ctx)
            xts = sb("xts", [P, 2, DT, R], ctx=ctx)
            hbs = sb("hbs", [R, 2, D], ctx=ctx)
            junk = sb("junk", [R, 2, D], ctx=ctx)
            prod = sb("prod", [R, 2, 2, GH, DH], ctx=ctx)
            bsq = sb("bsq", [P, DT], ctx=ctx)
            zrow = sb("zrow", [1, P], ctx=ctx)
            zwide = sb("zwide", [1, D + 1], ctx=ctx)
            hs = sb("hs", [P, 8], ctx=ctx)
            ns = {k: sb("ns_" + k, [R, T], ctx=ctx) for k in (
                "mean", "var", "dm", "std", "rstd", "n0", "nc", "p", "q", "lp", "lq", "at", "ser", "msk", "s1",
                "usq", "uh", "nu", "th", "f1", "x2", "xy", "A", "B", "den", "P", "Q", "nv2", "nv", "g",
                "a1", "a2", "t0", "t1")}
            er = sb("er", [P, SB, 1 + 2 * P], I32, ctx=ctx)
            erf = sb("erf", [P, SB, 1 + 2 * P], ctx=ctx)
            firsts = sb("firsts", [1, CH - 1], I32, ctx=ctx)
            firstf = sb("firstf", [1, CH - 1], ctx=ctx)
            thr = sb("thr", [T - 1, 1], ctx=ctx)
            ge = sb("ge", [T - 1, CH - 1], ctx=ctx)
            iotc = sb("iotc", [P, CH - 1], ctx=ctx)
            stepid = sb("stepid", [P, SB], ctx=ctx)
            cif = sb("cif", [P, SB], ctx=ctx)
            cii = sb("cii", [P, SB], I32, ctx=ctx)
            tf = sb("tf", [P, SB], ctx=ctx)
            t125 = sb("t125", [P, SB], ctx=ctx)
            AC = sb("AC", [P, CH - 1], ctx=ctx)
            ejunk = sb("ejunk", [P, CH - 1], ctx=ctx)
            rel = sb("rel", [P, SB, P], ctx=ctx)
            relb = sb("relb", [P, SB, P], BF16, ctx=ctx)
            m1 = sb("m1", [P, SB, P], ctx=ctx)
            padd = sb("padd", [1, 48], I32, ctx=ctx)
            pads = sb("pads", [1, 48], I32, ctx=ctx)
            X = GACC[0:R, :, 0:D]
            NTs = GACC[0:R, :, 0:D]
            NT = GACC[0:R, :, 0:D].rearrange("r t (h d) -> r t h d", h=GH)
            TAIL = E - (CH - 1) * P
            col = lambda name, t: ns[name][:, bass.ds(t, 1)]

            def row(buf, t):
                return buf[:, bass.ds(t, 1), :].rearrange("r a c -> r (a c)")

            def over_tiles(eng, body, *before_after):
                with eng.Fori(0, T // 2) as i:
                    body(2 * i, 0)
                    body(2 * i + 1, 1)
                body(T - 1, 0)

            block = ctx.enter_context(nc.Block())

            @block.sync
            def _(sp):
                for k in range(5):
                    sp.dma_start(X[:, 5 * k:5 * k + 5, :],
                                 x[5 * k * R:5 * (k + 1) * R, :].rearrange("(t r) d -> r t d", r=R)).then_inc(x_in, 16)
                sp.dma_start(Wn[:], gW.rearrange("(o p) d -> p o d", p=P)).then_inc(w_in, 16)
                with nc.allow_non_contiguous_dma("bias column"):
                    sp.dma_start(bcol[:], gb.rearrange("(o p) -> p o", p=P)).then_inc(w_in, 16)
                sp.dma_start(hbrow[:], bcast(gb, R, D)).then_inc(w_in, 16)
                for s in range(2):
                    sp.dma_start(attr[:, s], bass.AP(gatt.tensor, s * DH, [[0, R], [2 * DH, GH], [1, DH]])).then_inc(w_in, 16)
                full = (CH - 1) * P
                with nc.allow_non_contiguous_dma("chunk edges"):
                    sp.dma_start(er_dram[0:CH - 1, 1:1 + P], dst[0:full].rearrange("(c e) -> c e", e=P)).then_inc(er_ready, 16)
                    sp.dma_start(er_dram[0:CH - 1, 1 + P:], src[0:full].rearrange("(c e) -> c e", e=P)).then_inc(er_ready, 16)
                    sp.dma_start(er_dram[CH - 1:CH, 1:1 + TAIL], dst[full:E].rearrange("(c e) -> c e", c=1)).then_inc(er_ready, 16)
                    sp.dma_start(er_dram[CH - 1:CH, 1 + P:1 + P + TAIL], src[full:E].rearrange("(c e) -> c e", c=1)).then_inc(er_ready, 16)
                    sp.dma_start(er_dram[1:CH, 0:1], bass.AP(dst.tensor, P - 1, [[P, CH - 1], [1, 1]])).then_inc(er_ready, 16)
                    sp.dma_start(firsts[:], bass.AP(dst.tensor, P, [[0, 1], [P, CH - 1]])).then_inc(e_in, 16)
                    sp.wait_ge(const_ready, 1)
                    sp.dma_start(er_dram[CH - 1:CH, 1 + TAIL:1 + P], padd[:, 0:P - TAIL]).then_inc(er_ready, 16)
                    sp.dma_start(er_dram[CH - 1:CH, 1 + P + TAIL:], pads[:, 0:P - TAIL]).then_inc(er_ready, 16)
                    sp.dma_start(er_dram[0:1, 0:1], padd[:, 0:1]).then_inc(er_ready, 16)
                sp.wait_ge(rel_ready, 1)
                for b in range(SB):
                    sp.dma_start(rel_dram[b * P:(b + 1) * P, :], relb[:, b, :]).then_inc(rel_out, 16)
                sp.wait_ge(lx_done, done(T - 1))
                sp.dma_start(lx_dram.rearrange("(t r) d -> r t d", r=R), ACC[:]).then_inc(lx_out, 16)
                sp.wait_ge(lx_out, 16)
                for h in range(GH):
                    sp.dma_start(NT[:, :, h, :], bass.AP(lx_dram.tensor, h * N * DH, [[DH, R], [R * DH, T], [1, DH]])).then_inc(nt_in, 16)
                sp.wait_ge(nt_in, 16 * GH)
                sp.dma_start(ft_dram.rearrange("(t r) d -> r t d", r=R), X).then_inc(tab_out, 16)
                sp.wait_ge(sij_ready, T)
                with nc.allow_non_contiguous_dma("source scores"):
                    sp.dma_start(sj_dram.rearrange("(t r) h -> r t h", r=R), SIJ[:, :, GH:]).then_inc(tab_out, 16)
                sp.wait_ge(tab_out, 32)
                sp.wait_ge(rel_out, 16 * SB)

            @block.gpsimd
            def _(pool):
                c = Chain(pool, p1)
                pool.memset(padd[:], 4095)
                pool.memset(pads[:], 0).then_inc(const_ready, 1)
                pool.memset(XN[:, :, D:D + 1], 1.0)
                pool.memset(xns[:, :, D:D + 1], 1.0)
                pool.memset(ones[:], 1.0)
                pool.memset(zrow[:], 0.0)
                pool.memset(zwide[:], 0.0)
                c(pool.memset(ident[:], 0.0))
                c(pool.affine_select(out=ident[:], in_=ident[:], compare_op=ALU.not_equal, fill=1.0, base=0,
                                     pattern=[[-1, P]], channel_multiplier=1))
                kw = dict(allow_small_or_imprecise_dtypes=True)
                pool.iota(iota_p[:], pattern=[[0, 1]], base=0, channel_multiplier=1, **kw)
                pool.iota(iota_f[:], pattern=[[1, P]], base=0, channel_multiplier=0, **kw)
                pool.iota(thr[:], pattern=[[0, 1]], base=R, channel_multiplier=R, **kw)
                pool.iota(iotc[:], pattern=[[1, CH - 1]], base=1, channel_multiplier=0, **kw)
                c(pool.iota(stepid[:], pattern=[[P, SB]], base=0, channel_multiplier=1, **kw))
                pool.engine_nop().then_inc(const_ready, 1)
                def keep_tile(t, par):
                    pool.wait_ge(xns_full, done(t))
                    pool.tensor_copy(row(XN, t)[:, 0:D], xns[:, par, 0:D]).then_inc(xns_kept, 1)

                pool.sem_inc(xns_kept, 2)
                over_tiles(pool, keep_tile)
                pool.wait_ge(ci_ready, 1)
                pool.wait_ge(er_ready, 16 * 8)
                for b in range(SB):
                    pool.indirect_dma_start(out=er[:, b, :], out_offset=None, in_=er_dram,
                                            in_offset=bass.IndirectOffsetOnAxis(ap=cii[:, b:b + 1], axis=0)).then_inc(er_rows, 16)
                pool.wait_ge(er_rows, 16 * SB)

            @block.tensor
            def _(pe):
                pe.sem_inc(xt_full, 2)
                pe.sem_inc(u_full, 2)
                pe.wait_ge(const_ready, 2)
                pe.wait_ge(w_in, 80)
                for o in range(DT):
                    for k in range(DT):
                        last = pe.transpose(bank[0][:, (o * DT + k) * P:(o * DT + k + 1) * P], Wn[:, o, k * P:(k + 1) * P], ident[:])
                last.then_inc(pre_psum, 1)
                pe.wait_ge(hb2, 1)
                for o in range(DT):
                    last = pe.matmul(bank[1][:, 0:1], ones[:], bsq[:, o:o + 1], start=(o == 0), stop=(o == DT - 1))
                last.then_inc(pre_psum, 1)
                pe.wait_ge(hb2, 2)
                for k in range(DT):
                    for o in range(DT):
                        last = pe.matmul(bank[1][:, 8 + k:9 + k], Wn[:, o, k * P:(k + 1) * P], hbcol[:, o:o + 1], start=(o == 0), stop=(o == DT - 1))
                last.then_inc(pre_psum, 1)
                pe.wait_ge(cf_used, 1)
                pe.matmul(bank[2][0:T - 1, 0:CH - 1], ones[0:1, 0:T - 1], firstf[:], start=True, stop=True).then_inc(cf_psum, 1)
                pe.wait_ge(cf_used, 2)
                pe.matmul(bank[3][:, 0:CH - 1], ones[0:T - 1, :], ge[:], start=True, stop=True).then_inc(cf_psum, 1)
                pe.wait_ge(cf_used, 3)
                for b in range(SB):
                    last = pe.transpose(bank[2][0:1, b * P:(b + 1) * P], tf[:, b:b + 1], ident[:])
                last.then_inc(cf_psum, 1)
                pe.wait_ge(pre_used, 3)

                def node_tile(t, par):
                    pe.wait_ge(xns_full, done(t))
                    pe.matmul(bank[7][:, 0:D + 1], ones[0:R, :], xns[:, par, :], start=False, stop=False,
                              skip_group_check=True)
                    pe.wait_ge(xts_full, done(t - 1))
                    for k in range(DT):
                        last = pe.transpose(bank[4][:, k * P:k * P + R], xns[:, par, k * P:(k + 1) * P], ident[0:R, 0:R])
                    last.then_inc(xt_full, 1)
                    pe.wait_ge(xts_full, done(t))
                    pe.wait_ge(u_kept, done(t - 1))
                    for k in range(DT):
                        last = pe.matmul(bank[5][0:R, 0:D + 1], xts[:, par, k, :], WT[:, k, :], start=(k == 0), stop=(k == DT - 1))
                    last.then_inc(u_full, 1)

                pe.matmul(bank[7][:, 0:D + 1], zrow[:], zwide[:], start=True, stop=False, skip_group_check=True)
                over_tiles(pe, node_tile)
                pe.matmul(bank[7][:, 0:D + 1], zrow[:], zwide[:], start=False, stop=True, skip_group_check=True).then_inc(cs_full, 1)

                pe.wait_ge(rel_ready, 2)
                for b in range(SB):
                    w = min(P, STEPS - b * P)
                    pe.transpose(bank[0][:, b * P:b * P + w], rel[0:w, b, :], ident[0:w, 0:w])
                    last = pe.transpose(bank[1][:, b * P:b * P + w], erf[0:w, b, 1 + P:], ident[0:w, 0:w])
                last.then_inc(eT_psum, 1)

            @block.scalar
            def _(act):
                c = Chain(act, a1s)
                act.sem_inc(xts_full, 2)
                act.sem_inc(sq_done, 2)
                act.sem_inc(hbs_full, 2)
                act.wait_ge(w_in, 80)
                act.activation(bsq[:], bcol[:], ACT.Square).then_inc(hb2, 1)
                act.wait_ge(sc_v, 1)
                act.activation(ns["std"][:], ns["t1"][:], ACT.Sqrt)
                act.activation(ns["n0"][:], ns["var"][:], ACT.Sqrt).then_inc(sc_a, 1)
                act.wait_ge(sc_v, 2)
                act.activation(hs[:, 1:2], hs[:, 0:1], ACT.Sqrt).then_inc(sc_a, 1)
                act.wait_ge(sc_v, 3)
                act.activation(hs[:, 3:4], hs[:, 2:3], ACT.Tanh).then_inc(sc_a, 1)
                act.wait_ge(sc_v, 4)
                act.activation(ns["lp"][:], ns["p"][:], ACT.Ln)
                act.activation(ns["lq"][:], ns["q"][:], ACT.Ln).then_inc(sc_a, 1)

                def node_tile(t, par):
                    act.wait_ge(xt_full, done(t))
                    act.wait_ge(u_full, done(t - 2))
                    act.wait_ge(xts_kept, done(t - 2))
                    act.activation(xts[:, par, :, :], bank[4][:, 0:D].rearrange("p (k r) -> p k r", k=DT)[:, :, 0:R], ACT.Copy).then_inc(xts_full, 1)
                    act.wait_ge(u_kept, done(t))
                    act.activation(junk[:, par, :], row(ACC, t), ACT.Square, accum_out=col("usq", t)).then_inc(sq_done, 1)
                over_tiles(act, node_tile)
                act.wait_ge(sc_v, 5)
                act.activation(ns["nu"][:], ns["t0"][:], ACT.Sqrt).then_inc(sc_a, 1)
                act.wait_ge(sc_v, 6)
                act.activation(ns["th"][:], ns["t1"][:], ACT.Tanh).then_inc(sc_a, 1)
                act.wait_ge(sc_v, 7)
                act.activation(ns["nv"][:], ns["nv2"][:], ACT.Sqrt).then_inc(sc_a, 1)
                act.wait_ge(sc_v, 8)
                act.activation(ns["lp"][:], ns["p"][:], ACT.Ln)
                act.activation(ns["lq"][:], ns["q"][:], ACT.Ln).then_inc(sc_a, 1)
                act.wait_ge(sc_v, 9)

                def hb_tile(t, par):
                    act.wait_ge(lx_done, done(t - 2))
                    act.activation(hbs[:, par, :], hbrow[:], ACT.Copy, scale=col("a2", t)).then_inc(hbs_full, 1)
                over_tiles(act, hb_tile)

            @block.vector
            def _(v):
                c = Chain(v, v1)

                def stats(t, par):
                    v.bn_stats(row(st6, t), row(X, t)).then_inc(stat_n, 1)
                v.wait_ge(x_in, 80)
                over_tiles(v, stats)
                v.wait_ge(stat_n, T)
                s = [st6[:, :, k] for k in range(6)]
                n = {k: b[:] for k, b in ns.items()}
                c(v.tensor_tensor(n["mean"], s[1], s[4], ALU.add))
                c(v.tensor_scalar(n["mean"], n["mean"], 0.5, None, ALU.mult))
                c(v.tensor_tensor(n["dm"], s[1], s[4], ALU.subtract))
                c(v.tensor_tensor(n["dm"], n["dm"], n["dm"], ALU.mult))
                c(v.tensor_tensor(n["var"], s[2], s[5], ALU.add))
                c(v.tensor_scalar(n["var"], n["var"], 1.0 / D, None, ALU.mult))
                c(v.scalar_tensor_tensor(out=n["var"], in0=n["dm"], scalar=0.25, in1=n["var"], op0=ALU.mult, op1=ALU.add))
                v.tensor_scalar(n["t1"], n["var"], 1e-5, None, ALU.add).then_inc(sc_v, 1)
                v.wait_ge(sc_a, 1)
                c(v.reciprocal(n["rstd"], n["std"]))

                v.wait_ge(pre_psum, 2)
                v.tensor_copy(hs[:, 0:1], bank[1][:, 0:1]).then_inc(sc_v, 1)
                v.wait_ge(sc_a, 2)
                v.tensor_scalar(hs[:, 2:3], hs[:, 1:2], MIN_NORM, None, ALU.max).then_inc(sc_v, 1)
                v.wait_ge(sc_a, 3)
                c(v.tensor_scalar(hs[:, 3:4], hs[:, 3:4], MAXN, None, ALU.min))
                c(v.tensor_tensor(hs[:, 5:6], hs[:, 3:4], hs[:, 3:4], ALU.mult))
                c(v.reciprocal(hs[:, 4:5], hs[:, 2:3]))
                c(v.tensor_tensor(hs[:, 6:7], hs[:, 3:4], hs[:, 4:5], ALU.mult))
                c(v.tensor_scalar(hbrow[:], hbrow[:], hs[0:R, 6:7], None, ALU.mult))
                v.tensor_scalar(hbcol[:], bcol[:], hs[:, 6:7], None, ALU.mult).then_inc(hb2, 1)
                v.wait_ge(pre_psum, 3)
                for o in range(DT):
                    for k in range(DT):
                        v.tensor_copy(WT[:, k, o * P:(o + 1) * P], bank[0][:, (o * DT + k) * P:(o * DT + k + 1) * P]).then_inc(pre_used, 1)
                v.tensor_copy(WT[:, :, D:D + 1], bank[1][:, 8:8 + DT]).then_inc(pre_used, 1)

                def atanh(norm, extra):
                    c(v.tensor_scalar(n["p"], norm, 1.0, None, ALU.add))
                    v.tensor_scalar(n["q"], norm, -1.0, 1.0, ALU.mult, ALU.add).then_inc(sc_v, 1)
                    c(v.tensor_tensor(n["t0"], norm, norm, ALU.mult))
                    c(v.tensor_scalar(n["ser"], n["t0"], 1.0 / 7, 1.0 / 5, ALU.mult, ALU.add))
                    c(v.tensor_tensor(n["ser"], n["ser"], n["t0"], ALU.mult))
                    c(v.tensor_scalar(n["ser"], n["ser"], 1.0 / 3, None, ALU.add))
                    c(v.tensor_tensor(n["ser"], n["ser"], n["t0"], ALU.mult))
                    c(v.scalar_tensor_tensor(out=n["ser"], in0=n["ser"], scalar=1.0, in1=norm, op0=ALU.add, op1=ALU.mult))
                    c(v.tensor_scalar(n["msk"], norm, 0.1, None, ALU.is_lt))
                    v.wait_ge(sc_a, extra)
                    c(v.tensor_tensor(n["at"], n["lp"], n["lq"], ALU.subtract))
                    c(v.tensor_scalar(n["at"], n["at"], 0.5, None, ALU.mult))
                    c(v.tensor_tensor(n["ser"], n["ser"], n["at"], ALU.subtract))
                    c(v.tensor_tensor(n["ser"], n["ser"], n["msk"], ALU.mult))
                    c(v.tensor_tensor(n["at"], n["at"], n["ser"], ALU.add))

                c(v.scalar_tensor_tensor(out=n["n0"], in0=n["n0"], scalar=float(D) ** 0.5, in1=n["rstd"], op0=ALU.mult, op1=ALU.mult))
                c(v.tensor_scalar(n["n0"], n["n0"], MIN_NORM, None, ALU.max))
                c(v.tensor_scalar(n["nc"], n["n0"], ATANH_MAX, None, ALU.min))
                atanh(n["nc"], 4)
                c(v.reciprocal(n["t0"], n["n0"]))
                c(v.tensor_tensor(n["s1"], n["at"], n["t0"], ALU.mult))

                v.wait_ge(e_in, 16)
                v.wait_ge(const_ready, 2)
                v.tensor_copy(firstf[:], firsts[:]).then_inc(cf_used, 1)
                v.wait_ge(cf_psum, 1)
                v.tensor_scalar(ge[:], bank[2][0:T - 1, 0:CH - 1], thr[:], None, ALU.is_ge).then_inc(cf_used, 1)
                v.wait_ge(cf_psum, 2)
                c(v.tensor_tensor(AC[:], bank[3][:, 0:CH - 1], iotc[:], ALU.add))
                for b in range(SB):
                    c(v.tensor_scalar(ejunk[:], AC[:], stepid[:, b:b + 1], 0.0, ALU.is_le, ALU.add, accum_out=cif[:, b:b + 1]))
                c(v.tensor_tensor(tf[:], stepid[:], cif[:], ALU.subtract))
                c(v.tensor_scalar(t125[:], tf[:], float(R), None, ALU.mult))
                v.tensor_copy(cii[:], cif[:]).then_inc(ci_ready, 1)
                c(v.tensor_scalar(tf[:], tf[:], 0.0, float(T - 1), ALU.max, ALU.min))
                v.sem_inc(cf_used, 1)
                v.wait_ge(cf_psum, 3)
                c(v.tensor_copy(tI[:], bank[2][0:1, 0:STEPS]))

                def norm_tile(t, par):
                    v.wait_ge(xt_full, done(t - 2))
                    v.wait_ge(xns_kept, done(t - 2))
                    v.tensor_scalar(xns[:, par, 0:D], row(X, t), col("mean", t), col("rstd", t), ALU.subtract, ALU.mult).then_inc(xns_full, 1)

                v.sem_inc(u_kept, 2)
                v.sem_inc(xns_full, 2)
                v.sem_inc(xts_kept, 2)
                norm_tile(0, 0)

                def node_tile(t, par):
                    if not isinstance(t, int):
                        norm_tile(t + 1, 1 - par)
                    v.wait_ge(xts_full, done(t))
                    v.tensor_copy(XNT[:, :, bass.ds(t * R, R)], xts[:, par]).then_inc(xts_kept, 1)
                    v.wait_ge(u_full, done(t))
                    v.tensor_copy(row(ACC, t), bank[5][0:R, 0:D])
                    v.tensor_copy(col("uh", t), bank[5][0:R, D:D + 1]).then_inc(u_kept, 1)
                over_tiles(v, node_tile)
                v.wait_ge(cs_full, 1)
                c(v.tensor_scalar(CSE[:], bank[7][:, 0:D + 1], EPS_ATT, None, ALU.mult))

                v.wait_ge(u_kept, done(T - 1))
                v.wait_ge(sq_done, done(T - 1))
                v.tensor_scalar(n["t0"], n["usq"], 0.0, None, ALU.max).then_inc(sc_v, 1)
                v.wait_ge(sc_a, 5)
                c(v.tensor_tensor(n["nu"], n["nu"], n["s1"], ALU.mult))
                v.tensor_scalar(n["t1"], n["nu"], MIN_NORM, None, ALU.max).then_inc(sc_v, 1)
                v.wait_ge(sc_v, 6)
                c(v.reciprocal(n["f1"], n["t1"]))
                c(v.tensor_tensor(n["f1"], n["f1"], n["s1"], ALU.mult))
                v.wait_ge(sc_a, 6)
                c(v.tensor_scalar(n["th"], n["th"], MAXN, None, ALU.min))
                c(v.tensor_tensor(n["f1"], n["f1"], n["th"], ALU.mult))
                c(v.tensor_tensor(n["x2"], n["th"], n["th"], ALU.mult))
                c(v.tensor_tensor(n["xy"], n["uh"], n["f1"], ALU.mult))
                y2 = hs[0:R, 5:6]
                c(v.tensor_scalar(n["A"], n["xy"], 2.0, 1.0, ALU.mult, ALU.add))
                c(v.scalar_tensor_tensor(out=n["den"], in0=n["x2"], scalar=y2, in1=n["A"], op0=ALU.mult, op1=ALU.add))
                c(v.tensor_scalar(n["A"], n["A"], y2, None, ALU.add))
                c(v.tensor_scalar(n["B"], n["x2"], -1.0, 1.0, ALU.mult, ALU.add))
                c(v.tensor_scalar(n["den"], n["den"], MIN_NORM, None, ALU.max))
                c(v.reciprocal(n["den"], n["den"]))
                c(v.tensor_tensor(n["P"], n["A"], n["f1"], ALU.mult))
                c(v.tensor_tensor(n["P"], n["P"], n["den"], ALU.mult))
                c(v.tensor_tensor(n["Q"], n["B"], n["den"], ALU.mult))
                c(v.tensor_tensor(n["t0"], n["P"], n["usq"], ALU.mult))
                c(v.scalar_tensor_tensor(out=n["t1"], in0=n["Q"], scalar=2.0, in1=n["uh"], op0=ALU.mult, op1=ALU.mult))
                c(v.tensor_tensor(n["t0"], n["t0"], n["t1"], ALU.add))
                c(v.tensor_tensor(n["t0"], n["t0"], n["P"], ALU.mult))
                c(v.tensor_tensor(n["t1"], n["Q"], n["Q"], ALU.mult))
                c(v.scalar_tensor_tensor(out=n["t0"], in0=n["t1"], scalar=y2, in1=n["t0"], op0=ALU.mult, op1=ALU.add))
                v.tensor_scalar(n["nv2"], n["t0"], 0.0, None, ALU.max).then_inc(sc_v, 1)
                v.wait_ge(sc_a, 7)
                c(v.tensor_scalar(n["nv"], n["nv"], MIN_NORM, None, ALU.max))
                c(v.tensor_scalar(n["nc"], n["nv"], MAXN, ATANH_MAX, ALU.min, ALU.min))
                atanh(n["nc"], 8)
                c(v.reciprocal(n["t0"], n["nv"]))
                c(v.tensor_tensor(n["g"], n["at"], n["t0"], ALU.mult))
                c(v.tensor_tensor(n["a1"], n["g"], n["P"], ALU.mult))
                v.tensor_tensor(n["a2"], n["g"], n["Q"], ALU.mult).then_inc(sc_v, 1)
                v.sem_inc(lx_done, 2)

                def lx_tile(t, par):
                    v.wait_ge(hbs_full, done(t))
                    v.scalar_tensor_tensor(out=row(ACC, t), in0=row(ACC, t), scalar=col("a1", t), in1=hbs[:, par, :],
                                           op0=ALU.mult, op1=ALU.add).then_inc(lx_done, 1)
                over_tiles(v, lx_tile)

                v.wait_ge(er_rows, 16 * SB)
                c(v.tensor_copy(erf[:], er[:]))
                de = erf[:, :, 1:1 + P]
                for b in range(SB):
                    c(v.tensor_scalar(rel[:, b, :], de[:, b, :], t125[:, b:b + 1], -1.0, ALU.subtract, ALU.max))
                c(v.tensor_scalar(rel[:], rel[:], float(R), None, ALU.min))
                c(v.tensor_copy(relb[:], rel[:]))
                c(v.tensor_tensor(m1[:], de, erf[:, :, 0:P], ALU.not_equal))
                c(v.tensor_scalar(PEN[:], rel[:], 0.0, None, ALU.is_ge))
                c(v.scalar_tensor_tensor(out=PEN[:], in0=rel[:], scalar=float(R) - 0.5, in1=PEN[:], op0=ALU.is_lt, op1=ALU.mult))
                c(v.scalar_tensor_tensor(out=D0[:], in0=m1[:], scalar=-BIG, in1=PEN[:], op0=ALU.mult, op1=ALU.mult))
                c(v.tensor_scalar(PEN[:], PEN[:], -1.0, BIG, ALU.add, ALU.mult))
                v.sem_inc(rel_ready, 2)
                v.wait_ge(eT_psum, 1)
                c(v.tensor_copy(relT[:], bank[0][:, 0:STEPS]))
                c(v.tensor_copy(idxT[:], bank[1][:, 0:STEPS]))

                v.wait_ge(nt_in, 16 * GH)

                def score_tile(t, par):
                    nt = row(NTs, t).rearrange("r (h d) -> r h d", h=GH)
                    for s_ in range(2):
                        last = v.tensor_tensor(prod[:, par, s_], nt, attr[:, s_], ALU.mult)
                    c(last)
                    v.tensor_reduce(row(SIJ, t), prod[:, par].rearrange("r s h d -> r (s h) d"), AX.X, ALU.add).then_inc(sij_ready, 1)
                with v.Fori(0, T // 2) as i:
                    c.enter(i, 2)
                    score_tile(2 * i, 0)
                    score_tile(2 * i + 1, 1)
                c.leave(T // 2)
                score_tile(T - 1, 0)


        wp_in = sem("wp_in"); set_pe = sem("set_pe"); set_v = sem("set_v"); set_a = sem("set_a")
        fin_v = sem("fin_v"); fin_pe = sem("fin_pe"); v2 = sem("v2")
        xtm_full = sem("xtm_full"); pj_full = sem("pj_full"); pj_used = sem("pj_used"); nsq_full = sem("nsq_full")
        u2_full = sem("u2_full"); e_full = sem("e_full"); e_used = sem("e_used")
        phi_full = sem("phi_full"); att_full = sem("att_full"); rz_full = sem("rz_full"); acc_half = sem("acc_half")
        att_used = sem("att_used")
        oht_done = sem("oht_done"); sd_full = sem("sd_full"); sd_kept = sem("sd_kept"); r_full = sem("r_full")
        c_in = sem("c_in"); p_ready = sem("p_ready"); rb_in = sem("rb_in"); stg = sem("stg"); sj_in = [sem("sj_in0"), sem("sj_in1")]
        sj_kept = sem("sj_kept"); p2 = sem("p2"); stg_seen = sem("stg_seen"); g_in = [sem("g_in0"), sem("g_in1")]; o_full = sem("o_full"); o_used = sem("o_used")
        v3 = sem("v3")
        HB = T + 1
        HALVES = STEPS // 4
        flat = GACC[:, :, :].rearrange("p t c -> p (t c)")
        SJ = flat[:, 0:SB * P * GH].rearrange("p (s h) -> p s h", h=GH)
        SD = flat[:, SB * P * GH:3 * SB * P * GH].rearrange("p (s h) -> p s h", h=2 * GH)
        projT = sb("projT", [P, DT, D])
        zr = sb("zr", [1, P]); zw = sb("zw", [1, D + 1])

        def row(buf, t):
            return buf[:, bass.ds(t, 1), :].rearrange("r a c -> r (a c)")

        def steps_tiles(eng_type, u):
            _, regs = nc.values_load_multi_w_load_instructions(tI[0:1, bass.ds(4 * u, 4)], engines=[eng_type],
                                                               min_val=0, max_val=T - 1)
            return regs

        def mixer_block(first):
            ctx = ExitStack()
            with ctx:
                n_ = "A" if first else "B"
                mk = lambda name, shape, dt=F32: sb(name + n_, shape, dt, ctx=ctx)
                WS = {k: mk(f"W{k}S", [P, DT, PW]) for k in "kqv"}
                WoS = mk("WoS", [P, 4, D])
                WTs = {k: mk(f"W{k}T", [P, 4, D]) for k in "kqv"}
                MS = {k: mk(f"M{k}S", [P, DT, PW]) for k in "kq"}
                WVO = mk("WVO", [P, 4, D])
                BVWO = mk("BVWO", [P, PW])
                KVX = mk("KVX", [P, 4, D + 1])
                KVXT = WTs["k"]
                KVO = mk("KVO", [P, 4, D + 1])
                bc = mk("bc", [P, 3, 16])
                bcp = mk("bcp", [P, 3, 4])
                brow = KVX[0:1, :, :].rearrange("p b c -> p (b c)")[:, 0:2 * PW].rearrange("p (i k) -> p i k", i=2)
                kvo_flat = KVO[:].rearrange("p b c -> p (b c)")
                BVB = kvo_flat[:, 0:PW].rearrange("p (c k) -> p c k", c=4)
                rr = kvo_flat[0:1, PW:2 * PW]
                mid = mk("mid", [1, PW], BF16)
                b3 = {k: mk(f"b3{k}", [65, PW], BF16) for k in ("k", "q", "ck", "cq")}
                ones3 = mk("ones3", [65, R], BF16)
                spare = WTs["v"][:].rearrange("p c d -> p (c d)")
                xtm = spare[:, 0:2 * DT * R].rearrange("p (a k r) -> p a k r", a=2, k=DT)
                PT = spare[:, 2 * D:2 * D + 4 * R].rearrange("p (b r) -> p b r", b=4)
                EB = WTs["q"][0:R].rearrange("p c d -> p (c d)").rearrange("p (a k) -> p a k", a=2)
                sq = mk("sq", [R, 2, 2])
                nsq = mk("nsq", [R, 2, 2])
                rz = mk("rz", [R, 2])
                sidx = mk("sidx", [P, 2, 4], I32)
                if first:
                    pn = mk("pn", [P, DT, D])
                    RB = mk("RB", [R, 4 * P], BF16)
                    OHT = mk("OHT", [R, 4 * P])
                    sjst = mk("sjst", [P, 2, 4, GH])
                else:
                    G = [mk(f"G{i}", [P, 4, D]) for i in range(2)]
                    RS = mk("RS", [P, 2, 4, 265])
                    OH = mk("OH", [P, 2, 4, R])
                g0 = 0 if first else 2
                block = ctx.enter_context(nc.Block())

                def loops(g, ph, tile):
                    B0, Q0, u0 = (2 * g + ph) * T, g * T, (2 * (g - g0) + ph) * HB
                    tile(0, 0, B0, Q0, u0)
                    with_loop = lambda i, k: tile(2 * i + k, k % 2, B0 + 2 * i + k, Q0 + 2 * i + k, u0 + 2 * i + k)
                    return B0, with_loop, (T, 1, B0 + T, Q0 + T, u0 + T)

                def run(eng, g, ph, tile, peeled=0):
                    _, inner, last = loops(g, ph, tile)
                    with eng.Fori(0, T // 2 - peeled) as i:
                        inner(i, 1)
                        inner(i, 2)
                    for i in range(T // 2 - peeled, T // 2):
                        inner(i, 1)
                        inner(i, 2)
                    tile(*last)

                zero = lambda t: isinstance(t, int) and t == 0
                last_ = lambda t: isinstance(t, int) and t == T
                SV, SA, SPE = 6, 2, 7

                @block.sync
                def _(sp):
                    if first:
                        sp.dma_start(pn[:], proj.rearrange("(o p) k -> p o k", p=P)).then_inc(c_in, 16)
                    with nc.allow_non_contiguous_dma("bias columns"):
                        for i_, b_ in enumerate((bk, bq, bv)):
                            sp.dma_start(bc[:, i_, :], b_.rearrange("h k -> (h k)").rearrange("(c p) -> p c", p=P)).then_inc(c_in, 16)
                    for g in (g0, g0 + 1):
                        if g > g0:
                            sp.wait_ge(u2_full, done(2 * g * T - 1))
                        for k, w_ in (("k", Wk), ("q", Wq), ("v", Wv)):
                            sp.dma_start(WS[k][:], w_.rearrange("(o p) h k -> p o (h k)", p=P)[:, :, PW * g:PW * (g + 1)]).then_inc(wp_in, 16)
                        sp.dma_start(WoS[:], Wo.rearrange("h k d -> (h k) d").rearrange("(c p) d -> p c d", p=P)[:, 4 * g:4 * g + 4, :]).then_inc(wp_in, 16)
                        for i_, b_ in enumerate((bk, bq)):
                            sp.dma_start(brow[:, i_, :], b_.rearrange("h k -> (h k)")[PW * g:PW * (g + 1)].rearrange("(a k) -> a k", a=1)).then_inc(wp_in, 16)
                        if first:
                            with sp.Fori(0, 2 * HB) as i:
                                u = 2 * HB * (g - g0) + i
                                sp.wait_ge(oht_done, done(u - 1))
                                sp.dma_start(RB[:], bass.AP(rel_dram.tensor, u * 4 * P, [[0, R], [1, 4 * P]])).then_inc(rb_in, 16)

                @block.gpsimd
                def _(pool):
                    if first:
                        pool.memset(zr[:], 0.0)
                        pool.memset(zw[:], 0.0)
                        pool.sem_inc(sj_kept, 2)
                        pool.memset(ACC[:], 0.0).then_inc(p_ready, 1)
                    else:
                        pool.memset(GACC[:], 0.0).then_inc(p_ready, 1)
                    if first:
                        pool.memset(SJ[:, STEPS:, :], 0.0)
                        pool.memset(SD[:, STEPS:, :], 0.0)

                        def fetch(u, par):
                            pool.tensor_copy(sidx[:, par, :], idxT[:, bass.ds(4 * u, 4)]).then_inc(stg, 1)
                            pool.wait_ge(stg, u + 1)
                            if not (isinstance(u, int) and u < 2):
                                pool.wait_ge(sj_kept, done(u - 2))
                            pool.sem_inc(stg_seen, 1)
                            for k in range(4):
                                pool.indirect_dma_start(out=sjst[:, par, k, :], out_offset=None, in_=sj_dram,
                                                        in_offset=bass.IndirectOffsetOnAxis(ap=sidx[:, par, k:k + 1], axis=0)).then_inc(sj_in[par], 16)

                        def keep(u, par, n):
                            pool.wait_ge(sj_in[par], 64 * n)
                            pool.tensor_copy(SJ[:, bass.ds(4 * u, 4), :], sjst[:, par]).then_inc(sj_kept, 1)

                        fetch(0, 0)
                        with pool.Fori(0, HALVES // 2 - 1) as j:
                            fetch(2 * j + 1, 1)
                            keep(2 * j, 0, j + 1)
                            fetch(2 * j + 2, 0)
                            keep(2 * j + 1, 1, j + 1)
                        fetch(HALVES - 1, 1)
                        keep(HALVES - 2, 0, HALVES // 2)
                        keep(HALVES - 1, 1, HALVES // 2)
                    else:
                        def fetch(u, par):
                            pool.wait_ge(r_full, done(u - 2))
                            pool.tensor_copy(sidx[:, par, :], idxT[:, bass.ds(4 * u, 4)]).then_inc(stg, 1)
                            pool.wait_ge(stg, HALVES + u + 1)
                            pool.sem_inc(stg_seen, 1)
                            for k in range(4):
                                pool.indirect_dma_start(out=G[par][:, k, :], out_offset=None, in_=ft_dram,
                                                        in_offset=bass.IndirectOffsetOnAxis(ap=sidx[:, par, k:k + 1], axis=0)).then_inc(g_in[par], 16)

                        with pool.Fori(0, HALVES // 2) as j:
                            fetch(2 * j, 0)
                            fetch(2 * j + 1, 1)

                @block.tensor
                def _(pe):
                    pe.wait_ge(p_ready, 1 if first else 2)
                    if first:
                        pe.sem_inc(pj_full, 2); pe.sem_inc(u2_full, 2); pe.sem_inc(e_used, 2)
                        pe.sem_inc(att_full, 2); pe.sem_inc(sd_full, 2)
                        pe.wait_ge(c_in, 64)
                        for o in range(DT):
                            for k in range(DT):
                                last = pe.transpose(bank[5][:, k * D + o * P:k * D + (o + 1) * P], pn[:, o, k * P:(k + 1) * P], ident[:])
                        last.then_inc(fin_pe, 1)
                        pe.wait_ge(fin_v, 1)

                    def setup(g):
                        pe.wait_ge(wp_in, 96 * (g + 1))
                        pe.wait_ge(pj_used, done(2 * g * T - 1))
                        pe.wait_ge(e_full, done(2 * g * T - 1))
                        pe.wait_ge(att_used, done(g * T - 1))
                        for i_, k in enumerate("kqv"):
                            for h in range(2):
                                for c_ in range(2):
                                    for o in range(DT):
                                        last = pe.transpose(bank[2 * i_ + h][:, c_ * D + o * P:c_ * D + (o + 1) * P],
                                                            WS[k][:, o, h * D + c_ * P:h * D + (c_ + 1) * P], ident[:])
                            last.then_inc(set_pe, 1)
                        for i_, (k, s_, n) in enumerate((("k", set_v, SV * g + 2), ("q", set_a, SA * g + 1))):
                            pe.wait_ge(s_, n)
                            for o in range(DT):
                                for h in range(2):
                                    for c_ in range(2):
                                        last = pe.matmul(bank[2 * i_ + o][:, h * D:(h + 1) * D], WTs[k][:, 2 * h + c_, o * P:(o + 1) * P],
                                                         projT[:, c_, :], start=(c_ == 0), stop=(c_ == 1))
                            last.then_inc(set_pe, 1)
                        pe.wait_ge(set_v, SV * g + 3)
                        for h in range(2):
                            for o in range(DT):
                                for c_ in range(2):
                                    last = pe.matmul(bank[4 + h][:, o * D:(o + 1) * D], WTs["v"][:, 2 * h + c_, o * P:(o + 1) * P],
                                                     WoS[:, 2 * h + c_, :], start=(c_ == 0), stop=(c_ == 1))
                        last.then_inc(set_pe, 1)
                        pe.wait_ge(set_v, SV * g + 5)
                        pe.wait_ge(set_a, SA * g + 2)
                        for h in range(2):
                            for c_ in range(2):
                                kw = dict(start=(c_ == 0), stop=(c_ == 1))
                                for i_ in range(2):
                                    pe.matmul(bank[2 * i_][0:1, h * D:(h + 1) * D], bcp[:, i_, 2 * h + c_:2 * h + c_ + 1], projT[:, c_, :], **kw)
                                last = pe.matmul(bank[4][:, h * D:(h + 1) * D], BVB[:, 2 * h + c_, :], WoS[:, 2 * h + c_, :], **kw)
                        last.then_inc(set_pe, 1)
                        pe.wait_ge(set_v, SV * g + 6)

                    def finish_keys(g):
                        pe.wait_ge(fin_v, 1 + 3 * g + 1)
                        for h in range(2):
                            for mb in range(2):
                                for o in range(DT):
                                    last = pe.transpose(bank[h][:, o * D + mb * P:o * D + (mb + 1) * P], KVX[:, 2 * h + mb, o * P:(o + 1) * P], ident[:])
                        last.then_inc(fin_pe, 1)
                        pe.wait_ge(fin_v, 1 + 3 * g + 2)
                        for h in range(2):
                            for mb in range(2):
                                for o in range(DT):
                                    last = pe.matmul(bank[2 + 2 * h + mb][:, 0:D], KVXT[:, 2 * h + o, mb * P:(mb + 1) * P], WVO[:, 2 * h + o, :],
                                                     start=(o == 0), stop=(o == DT - 1))
                        last.then_inc(fin_pe, 1)
                        pe.wait_ge(fin_v, 1 + 3 * g + 3)

                    def edges(u, k0, k1, regs):
                        for k in range(k0, k1):
                            if first:
                                last = pe.matmul(bank[6][:, 8 * k:8 * k + 8], OHT[:, k * P:(k + 1) * P],
                                                 SIJ[:, bass.ds(regs[k], 1), :].rearrange("r a c -> r (a c)"), start=True, stop=True)
                                if k == 3:
                                    last.then_inc(sd_full, 1)
                            else:
                                par, n = edges.par, 4 * u + k
                                pe.wait_ge(o_used, done(n - 2))
                                pe.matmul(bank[6 + k % 2][0:R, 0:265], OH[:, par, k, :], RS[:, par, k, :], start=True, stop=True).then_inc(o_full, 1)

                    def make(ph):
                        kq = "kq"[ph]

                        def tile(t, par, B, Q, u):
                            regs = steps_tiles(mybir.EngineType.PE, u) if first else None
                            if ph == 0 and zero(t):
                                for b in range(4):
                                    pe.matmul(bank[2 + b][:, 0:D + 1], zr[:], zw[:], start=True, stop=False, skip_group_check=True)
                            if ph == 1 and not zero(t):
                                pe.wait_ge(e_full, done(B - 1))
                                pe.wait_ge(phi_full, done(Q - 2))
                                for b in range(4):
                                    last = pe.transpose(bank[2][:, b * R:(b + 1) * R], EB[:, 1 - par, b * P:(b + 1) * P], ident[0:R, 0:R])
                                last.then_inc(e_used, 1)
                            work = first or not (isinstance(u, int) and u == 0)
                            ue = u if first else u - 1
                            edges.par = 1 - par
                            if not last_(t):
                                pe.wait_ge(xtm_full, done(B))
                                pe.wait_ge(pj_used, done(B - 1))
                                for k in range(DT):
                                    pe.matmul(bank[0][0:R, :], xtm[:, par, k, :], WS[kq][:, k, :], start=(k == 0), stop=False)
                                pe.matmul(bank[0][0:R, :], ones3[:], b3[kq][:], start=False, stop=True).then_inc(pj_full, 1)
                            if first:
                                pe.wait_ge(oht_done, done(u))
                                pe.wait_ge(sd_kept, done(u - 1))
                            elif work:
                                pe.wait_ge(r_full, done(u - 1))
                            if work:
                                edges(ue, 0, 2, regs)
                            if not last_(t):
                                pe.wait_ge(e_full, done(B - 1))
                                for k in range(DT):
                                    pe.matmul(bank[1][0:R, :], xtm[:, par, k, :], MS[kq][:, k, :], start=(k == 0), stop=False)
                                pe.matmul(bank[1][0:R, :], ones3[:], b3["c" + kq][:], start=False, stop=True).then_inc(u2_full, 1)
                            if work:
                                edges(ue, 2, 4, regs)
                            if ph == 0 and not zero(t):
                                pe.wait_ge(e_full, done(B - 1))
                                for b in range(4):
                                    last = pe.matmul(bank[2 + b][:, 0:D + 1], EB[:, 1 - par, b * P:(b + 1) * P], row(XN, t - 1),
                                                     start=False, stop=last_(t), skip_group_check=True)
                                last.then_inc(e_used, 1)
                            if ph == 1 and not zero(t):
                                pe.wait_ge(phi_full, done(Q - 1))
                                pe.wait_ge(att_used, done(Q - 2))
                                for h in range(2):
                                    for mb in range(2):
                                        last = pe.matmul(bank[3 + h][0:R, 0:D + 1], PT[:, 2 * h + mb, :], KVO[:, 2 * h + mb, :],
                                                         start=(mb == 0), stop=(mb == 1))
                                last.then_inc(att_full, 1)
                        return tile

                    for g in (g0, g0 + 1):
                        setup(g)
                        run(pe, g, 0, make(0))
                        finish_keys(g)
                        run(pe, g, 1, make(1))
                    if not first:
                        pe.wait_ge(r_full, done(HALVES - 1))
                        edges.par = 1
                        edges(HALVES - 1, 0, 4, None)

                @block.scalar
                def _(act):
                    if first:
                        for s_ in (xtm_full, pj_used, nsq_full, e_full, phi_full):
                            act.sem_inc(s_, 2)

                    def setup(g):
                        act.wait_ge(set_pe, SPE * g + 2)
                        for h in range(2):
                            last = act.activation(WTs["q"][:, 2 * h:2 * h + 2, :], bank[2 + h][:].rearrange("p (c d) -> p c d", c=2), ACT.Copy)
                        last.then_inc(set_a, 1)
                        act.wait_ge(set_pe, SPE * g + 5)
                        for o in range(DT):
                            last = act.activation(MS["q"][:, o, :], bank[2 + o][:], ACT.Copy, scale=SCALE)
                        last.then_inc(set_a, 1)
                        act.wait_ge(set_pe, SPE * g + 7)

                    def stage(t, par, B):
                        act.wait_ge(u2_full, done(B - (1 if zero(t) else 2)))
                        act.activation(xtm[:, par], XNT[:, :, bass.ds(t * R, R)], ACT.Copy).then_inc(xtm_full, 1)

                    def make(ph):
                        def tile(t, par, B, Q, u):
                            if zero(t):
                                stage(t, par, B)
                            if ph == 1 and not zero(t):
                                act.wait_ge(e_used, done(B - 1))
                                act.wait_ge(att_full, done(Q - 2))
                                act.activation(PT[:], bank[2][:, 0:4 * R].rearrange("p (b r) -> p b r", b=4), ACT.Copy,
                                               scale=1.0 / 16, bias=EPS_ATT).then_inc(phi_full, 1)
                            if not last_(t):
                                act.wait_ge(pj_full, done(B))
                                act.wait_ge(e_used, done(B - (1 if zero(t) else 2)))
                                for h in range(2):
                                    last = act.activation(EB[:, par, h * D:(h + 1) * D], bank[0][0:R, h * D:(h + 1) * D], ACT.Square, scale=SCALE * 0.5 ** 0.5,
                                                          accum_out=sq[:, par, h:h + 1])
                                last.then_inc(pj_used, 1)
                                act.wait_ge(pj_used, done(B))
                                act.mul(nsq[:, par, :], sq[:, par, :], -1.0).then_inc(nsq_full, 1)
                                if not (isinstance(t, int) and t == T - 1):
                                    stage(t + 1, 1 - par, B + 1)
                                act.wait_ge(nsq_full, done(B))
                                act.wait_ge(u2_full, done(B))
                                for h in range(2):
                                    last = act.activation(EB[:, par, h * D:(h + 1) * D], bank[1][0:R, h * D:(h + 1) * D], ACT.Exp,
                                                          bias=nsq[:, par, h:h + 1])
                                last.then_inc(e_full, 1)
                        return tile

                    for g in (g0, g0 + 1):
                        setup(g)
                        run(act, g, 0, make(0), 1)
                        run(act, g, 1, make(1), 1)

                @block.vector
                def _(v):
                    c = Chain(v, v2 if first else v3)
                    if first:
                        for s_ in (oht_done, sd_kept, r_full, att_used, rz_full, acc_half, o_used):
                            v.sem_inc(s_, 2)
                        v.wait_ge(fin_pe, 1)
                        v.tensor_copy(projT[:], bank[5][:].rearrange("p (k m) -> p k m", k=DT)).then_inc(fin_v, 1)
                    for k in b3:
                        v.memset(b3[k][:], 0.0)
                    c(v.memset(ones3[:], 0.0))
                    for p_ in (0, 32, 64):
                        v.memset(ones3[p_:p_ + 1, :], 1.0)
                    v.wait_ge(p_ready, 1 if first else 2)
                    v.wait_ge(c_in, 64 if first else 112)

                    def three(name, src_):
                        c(v.tensor_copy(b3[name][0:1, :], src_))
                        c(v.tensor_tensor(rr, src_, b3[name][0:1, :], ALU.subtract))
                        c(v.tensor_copy(mid[:], rr))
                        c(v.tensor_copy(b3[name][32:33, :], mid[:]))
                        c(v.tensor_tensor(rr, rr, mid[:], ALU.subtract))
                        c(v.tensor_copy(b3[name][64:65, :], rr))

                    def setup(g):
                        c(v.tensor_copy(bcp[:], bc[:, :, 4 * g:4 * g + 4]))
                        v.tensor_copy(BVB, bcp[:, 2, :].unsqueeze(2).to_broadcast([P, 4, P])).then_inc(set_v, 1)
                        for k, n, s_ in (("k", 1, 0), ("v", 3, 4)):
                            v.wait_ge(set_pe, SPE * g + n)
                            for h in range(2):
                                last = v.tensor_copy(WTs[k][:, 2 * h:2 * h + 2, :], bank[s_ + h][:].rearrange("p (c d) -> p c d", c=2))
                            last.then_inc(set_v, 1)
                        v.wait_ge(set_pe, SPE * g + 4)
                        for o in range(DT):
                            last = v.tensor_scalar(MS["k"][:, o, :], bank[o][:], SCALE, None, ALU.mult)
                        last.then_inc(set_v, 1)
                        v.wait_ge(set_pe, SPE * g + 6)
                        for h in range(2):
                            last = v.tensor_copy(WVO[:, 2 * h:2 * h + 2, :], bank[4 + h][:].rearrange("p (o d) -> p o d", o=2))
                        last.then_inc(set_v, 1)
                        v.wait_ge(set_pe, SPE * g + 7)
                        v.wait_ge(wp_in, 96 * (g + 1))
                        c(v.tensor_copy(BVWO[:], bank[4][:]))
                        for i_, k in enumerate("kq"):
                            three(k, brow[:, i_, :])
                            c(v.tensor_scalar(brow[:, i_, :], bank[2 * i_][0:1, :], SCALE, None, ALU.mult))
                            three("c" + k, brow[:, i_, :])
                        v.sem_inc(set_v, 1)

                    def finish_keys(g):
                        v.wait_ge(e_used, done((2 * g + 1) * T - 1))
                        v.wait_ge(pj_used, done((2 * g + 1) * T - 1))
                        v.wait_ge(e_full, done((2 * g + 1) * T - 1))
                        for b in range(4):
                            last = v.scalar_tensor_tensor(out=KVX[:, b, :], in0=bank[2 + b][:, 0:D + 1], scalar=1.0 / 16, in1=CSE[:],
                                                          op0=ALU.mult, op1=ALU.add)
                        last.then_inc(fin_v, 1)
                        v.wait_ge(fin_pe, 1 + 2 * g + 1)
                        for h in range(2):
                            last = v.tensor_copy(KVXT[:, 2 * h:2 * h + 2, :], bank[h][:].rearrange("p (o m) -> p o m", o=2))
                        last.then_inc(fin_v, 1)
                        v.wait_ge(fin_pe, 1 + 2 * g + 2)
                        for b in range(4):
                            v.scalar_tensor_tensor(out=KVO[:, b, 0:D], in0=BVWO[:, (b // 2) * D:(b // 2 + 1) * D], scalar=KVX[:, b, D:D + 1],
                                                   in1=bank[2 + b][:, 0:D], op0=ALU.mult, op1=ALU.add)
                        v.tensor_copy(KVO[:, :, D:D + 1], KVX[:, :, D:D + 1]).then_inc(fin_v, 1)

                    def targets(u):
                        v.wait_ge(rb_in, 16 * (u + 1))
                        v.tensor_scalar(OHT[:], RB[:], iota_p[0:R, :], None, ALU.is_equal).then_inc(oht_done, 1)

                    def sums(u, regs, k0, k1):
                        for k in range(k0, k1):
                            v.wait_ge(o_full, 4 * u + k + 1)
                            v.wait_ge(o_used, done(4 * u + k - 1))
                            acc = GACC[0:R, bass.ds(regs[k], 1), :].rearrange("r a c -> r (a c)")
                            v.tensor_tensor(acc, bank[6 + k % 2][0:R, 0:265], acc, ALU.add).then_inc(o_used, 1)

                    def make(ph):
                        def tile(t, par, B, Q, u):
                            sums_due = not first and not (isinstance(u, int) and u == 0)
                            if first:
                                v.wait_ge(sd_full, done(u))
                                v.tensor_copy(SD[:, bass.ds(4 * u, 4), :], bank[6][:, 0:32].rearrange("p (s c) -> p s c", c=8)).then_inc(sd_kept, 1)
                                if not (isinstance(u, int) and u == HALVES - 1):
                                    targets(u + 1)
                            else:
                                if sums_due:
                                    regs = steps_tiles(mybir.EngineType.DVE, u - 1)
                                    sums(u - 1, regs, 0, 2)
                                if not (isinstance(u, int) and u < 2):
                                    v.wait_ge(o_full, 4 * (u - 1))
                                v.wait_ge(g_in[par], (64 * (u - par) // 2 if isinstance(u, int) else 32 * (u - par)) + 64)
                                rel4 = relT[:, bass.ds(4 * u, 4)].unsqueeze(2).to_broadcast([P, 4, R])
                                v.tensor_tensor(OH[:, par], iota_f[:, 0:R].unsqueeze(1).to_broadcast([P, 4, R]), rel4, ALU.is_equal)
                                at4 = AT[:, bass.ds(4 * u, 4), :]
                                v.tensor_copy(RS[:, par, :, D:], at4)
                                for k in range(4):
                                    last = v.tensor_tensor(RS[:, par, k, 0:D].rearrange("p (h d) -> p h d", h=GH),
                                                           G[par][:, k, :].rearrange("p (h d) -> p h d", h=GH),
                                                           AT[:, bass.ds(4 * u + k, 1), 0:GH].rearrange("p a h -> p (a h)").unsqueeze(2).to_broadcast([P, GH, DH]), ALU.mult)
                                last.then_inc(r_full, 1)
                                if sums_due:
                                    sums(u - 1, regs, 2, 4)
                            if ph == 1 and not zero(t):
                                v.wait_ge(att_full, done(Q - 1))
                                v.reciprocal(rz[:, 0:1], bank[3][0:R, D:D + 1])
                                v.reciprocal(rz[:, 1:2], bank[4][0:R, D:D + 1]).then_inc(rz_full, 1)
                                v.wait_ge(rz_full, done(Q - 1))
                                acc = row(ACC, t - 1)
                                v.scalar_tensor_tensor(out=acc, in0=bank[3][0:R, 0:D], scalar=rz[:, 0:1], in1=acc,
                                                       op0=ALU.mult, op1=ALU.add).then_inc(acc_half, 1)
                                v.wait_ge(acc_half, done(Q - 1))
                                v.scalar_tensor_tensor(out=acc, in0=bank[4][0:R, 0:D], scalar=rz[:, 1:2], in1=acc,
                                                       op0=ALU.mult, op1=ALU.add).then_inc(att_used, 1)
                        return tile

                    if first:
                        targets(0)
                    for g in (g0, g0 + 1):
                        setup(g)
                        run(v, g, 0, make(0))
                        finish_keys(g)
                        run(v, g, 1, make(1))
                    if not first:
                        sums(HALVES - 1, steps_tiles(mybir.EngineType.DVE, HALVES - 1), 0, 4)

        mixer_block(True)
        AT = sb("AT", [P, STEPS, 9])

        tr = sem("tr"); ev_v = sem("ev_v"); ev_a = sem("ev_a"); v4 = sem("v4"); ex_in = sem("ex_in"); ex_done = sem("ex_done")
        with ExitStack() as ctx:
            big = lambda name: sb(name, [P, GH, SB * P], ctx=ctx)
            XS, SI, SS, M, M2 = big("XS"), big("SI"), big("SS"), big("M"), big("M2")
            D0L = sb("D0L", [P, SB * P + 1], ctx=ctx)
            X0 = sb("X0", [P, GH, SB], ctx=ctx)
            CI = sb("CI", [P, SB, GH], ctx=ctx)
            TL = sb("TL", [P, SB, GH], ctx=ctx)
            AL = sb("AL", [P, SB], ctx=ctx)
            ALB = sb("ALB", [P, SB, GH], ctx=ctx)
            TR = sb("TR", [GH, SB * P], ctx=ctx)
            AR = sb("AR", [GH, SB * P], ctx=ctx)
            CR = sb("CR", [GH, SB * P + 1], ctx=ctx)
            FI = sb("FI", [P, SB * P], ctx=ctx)
            pen = PEN[:].rearrange("p b e -> p (b e)")
            d0 = D0[:].rearrange("p b e -> p (b e)")
            D00 = D0[:, :, 0:1].rearrange("p b e -> p (b e)")
            block = ctx.enter_context(nc.Block())

            @block.tensor
            def _(pe):
                def turn(banks, source):
                    for h in range(GH):
                        for b in range(SB):
                            last = pe.transpose(bank[banks + h][:, b * P:(b + 1) * P], source(b, h), ident[:])
                    last.then_inc(tr, 1)
                turn(0, lambda b, h: SJ[:, b * P:(b + 1) * P, h])
                turn(4, lambda b, h: SD[:, b * P:(b + 1) * P, h])
                pe.wait_ge(ev_v, 1)
                turn(0, lambda b, h: SD[:, b * P:(b + 1) * P, GH + h])
                n = 2
                for k in range(2):
                    pe.wait_ge(ev_v, n + 1)
                    if k == 0:
                        pe.wait_ge(ev_a, 1)
                    for b in range(SB):
                        pe.transpose(bank[4][0:GH, b * P:(b + 1) * P], TL[:, b, :], ident[:])
                        last = pe.transpose(bank[5][0:GH, b * P:(b + 1) * P], ALB[:, b, :], ident[:])
                    last.then_inc(tr, 1)
                    pe.wait_ge(ev_v, n + 2)
                    for b in range(SB):
                        last = pe.transpose(bank[6][:, b * GH:(b + 1) * GH], CR[:, k + b * P:k + (b + 1) * P], ident[0:GH, 0:GH])
                    last.then_inc(tr, 1)
                    n += 2

                def back(bank_, source):
                    for b in range(SB):
                        w = min(P, STEPS - b * P)
                        last = pe.transpose(bank[bank_][:, b * P:b * P + w], source(b)[0:w], ident[0:w, 0:w])
                    return last
                pe.wait_ge(ex_done, 1)
                for h in range(GH):
                    back(h, lambda b: XS[:, h, b * P:(b + 1) * P]).then_inc(tr, 1)
                pe.wait_ge(ev_v, n + 1)
                for h in range(GH):
                    back(4 + h, lambda b: SS[:, h, b * P:(b + 1) * P]).then_inc(tr, 1)
                pe.wait_ge(ev_v, n + 2)
                back(0, lambda b: FI[:, b * P:(b + 1) * P]).then_inc(tr, 1)

            @block.scalar
            def _(act):
                act.wait_ge(tr, 2)
                for h in range(GH):
                    last = act.activation(SI[:, h, :], bank[4 + h][:], ACT.Copy)
                last.then_inc(ev_a, 1)
                act.wait_ge(ex_in, 1)
                act.activation(XS[:], XS[:], ACT.Exp).then_inc(ex_done, 1)
                act.activation(SS[:], SS[:], ACT.Exp).then_inc(ex_done, 1)

            @block.vector
            def _(v):
                c = Chain(v, v4)
                c(v.tensor_copy(D0L[:, 0:SB * P], d0))
                c(v.memset(D0L[:, 0:SB * P].rearrange("p (b e) -> p b e", b=SB)[:, :, 0:1], -BIG))
                v.memset(D0L[:, SB * P:], -BIG)
                v.tensor_reduce(AL[:], D0[:], AX.X, ALU.min)
                c(v.tensor_scalar(FI[:], d0, -1.0, None, ALU.is_lt))
                c(v.tensor_copy(ALB[:], AL[:].unsqueeze(2).to_broadcast([P, SB, GH])))
                v.wait_ge(tr, 1)
                for h in range(GH):
                    last = v.tensor_tensor(XS[:, h, :], bank[h][:], pen, ALU.add)
                last.then_inc(ev_v, 1)
                v.wait_ge(tr, 3)
                for h in range(GH):
                    last = v.tensor_copy(SS[:, h, :], bank[h][:])
                last.then_inc(ev_v, 1)
                v.wait_ge(ev_v, 2)
                c(v.tensor_copy(X0[:], XS[:].rearrange("p h (b e) -> p h b e", b=SB)[:, :, :, 0]))

                def ends(buf, e):
                    return buf[:].rearrange("p h (b e) -> p h b e", b=SB)[:, :, :, e]

                def scan(out_, data, way):
                    for h in range(GH):
                        if way > 0:
                            last = v.tensor_tensor_scan(out_[:, h, :], D0L[:, 0:SB * P], data[:, h, :], -BIG, ALU.add, ALU.max)
                        else:
                            last = v.tensor_tensor_scan(out_[:, h, :][:, ::-1], D0L[:, 1:][:, ::-1], data[:, h, :][:, ::-1], -BIG, ALU.add, ALU.max)
                    c(last)

                bh = lambda ap: ap.rearrange("p h b -> p b h")
                d00 = D00.unsqueeze(2).to_broadcast([P, SB, GH])
                scan(M, XS, 1)
                v.tensor_copy(TL[:], bh(ends(M, P - 1))).then_inc(ev_v, 1)
                v.wait_ge(tr, 4)
                v.tensor_copy(TR[:], bank[4][0:GH, :])
                c(v.tensor_copy(AR[:], bank[5][0:GH, :]))
                c(v.memset(CR[:, 0:1], -BIG))
                v.tensor_tensor_scan(CR[:, 1:], AR[:], TR[:], -BIG, ALU.add, ALU.max).then_inc(ev_v, 1)
                v.wait_ge(tr, 5)
                c(v.tensor_tensor(CI[:], bank[6][:, 0:SB * GH].rearrange("p (b h) -> p b h", b=SB), d00, ALU.add))
                c(v.tensor_tensor(ends(XS, 0), ends(XS, 0), CI[:].rearrange("p b h -> p h b"), ALU.max))
                scan(M, XS, 1)
                c(v.tensor_copy(ends(XS, 0), X0[:]))
                scan(M2, M, -1)
                v.tensor_tensor(TL[:], bh(ends(M2, 0)), d00, ALU.add).then_inc(ev_v, 1)
                v.wait_ge(tr, 6)
                c(v.tensor_copy(TR[:], bank[4][0:GH, :]))
                c(v.memset(CR[:, SB * P:], -BIG))
                v.tensor_tensor_scan(CR[:, 0:SB * P][:, ::-1], AR[:, ::-1], TR[:, ::-1], -BIG, ALU.add, ALU.max).then_inc(ev_v, 1)
                v.wait_ge(tr, 7)
                c(v.tensor_tensor(ends(M, P - 1), ends(M, P - 1), bank[6][:, 0:SB * GH].rearrange("p (b h) -> p h b", b=SB), ALU.max))
                scan(M2, M, -1)
                c(v.tensor_tensor(M2[:], M2[:], SS[:], ALU.max))
                v.wait_ge(ev_a, 1)
                for buf in (XS, M2, SS):
                    last = v.tensor_tensor(buf[:], buf[:], SI[:], ALU.add)
                c(last)
                for buf in (XS, M2, SS):
                    last = v.scalar_tensor_tensor(out=buf[:], in0=buf[:], scalar=0.2, in1=buf[:], op0=ALU.mult, op1=ALU.max)
                c(last)
                for buf in (XS, SS):
                    last = v.tensor_tensor(buf[:], buf[:], M2[:], ALU.subtract)
                last.then_inc(ex_in, 1)
                v.wait_ge(ex_done, 2)
                v.tensor_tensor(SS[:], SS[:], FI[:].unsqueeze(1).to_broadcast([P, GH, SB * P]), ALU.mult).then_inc(ev_v, 1)
                for h in range(GH):
                    v.wait_ge(tr, 8 + h)
                    last = v.tensor_copy(AT[:, :, h], bank[h][:, 0:STEPS])
                last.then_inc(ev_v, 1)
                for h in range(GH):
                    v.wait_ge(tr, 8 + GH + h)
                    v.tensor_copy(AT[:, :, GH + h], bank[4 + h][:, 0:STEPS])
                v.wait_ge(tr, 8 + 2 * GH)
                v.tensor_copy(AT[:, :, 2 * GH], bank[0][:, 0:STEPS])

        mixer_block(False)

        buf_dram = nc.dram_tensor("buf_dram", (XE * SLOT, D), F32).ap()
        y_dram = nc.dram_tensor("y_dram", (XE * SLOT, D), F32).ap()
        g_dram = nc.dram_tensor("g_dram", (N, D), F32).ap()
        sums_ready = sem("sums_ready"); g_out = sem("g_out"); g_in = sem("g_in"); gn_sq = sem("gn_sq")
        slot = sb("slot", [R, T], I32)
        wgt = sb("wgt", [R, T])
        f_in = sem("f_in"); x2_in = sem("x2_in"); z_out = sem("z_out"); xn_used = sem("xn_used"); asr_ready = sem("asr_ready")
        nt_done = sem("nt_done"); v5 = sem("v5"); p5 = sem("p5"); st_n = sem("st_n"); sq_v = sem("sq_v"); sq_a = sem("sq_a"); gn_v = sem("gn_v"); gn_a = sem("gn_a")
        zset = sem("zset"); tri_ready = sem("tri_ready"); lg_done = sem("lg_done"); oh_ready = sem("oh_ready")
        cnt_done = sem("cnt_done"); sc_ready = sem("sc_ready"); sc_out = sem("sc_out")
        s_full = sem("s_full"); t_full = sem("t_full"); tt_full = sem("tt_full"); h_full = sem("h_full"); hr_full = sem("hr_full")
        m_full = sem("m_full"); m_used = sem("m_used"); n1_done = sem("n1_done"); n3_done = sem("n3_done"); loops5 = sem("loops5")

        def over_tiles(eng, body):
            body(0, 0)
            with eng.Fori(0, T // 2 - 1) as i:
                body(2 * i + 1, 1)
                body(2 * i + 2, 0)
            body(T - 2, 1)
            body(T - 1, 0)

        before = lambda t, n_: not isinstance(t, int) or t < n_
        zero = lambda t: isinstance(t, int) and t == 0

        with ExitStack() as ctx:
            mk = lambda name, shape, dt=F32: sb(name, shape, dt, ctx=ctx)
            NTB = mk("NTB", [R, T, D])
            RW = mk("RW", [R, 7, D])
            b1c = mk("b1c", [P, DT])
            W1s = mk("W1s", [P, DT, D]); W2s = mk("W2s", [P, DT, D])
            gw = mk("gw", [P, DT, XE]); gbr = mk("gbr", [R, XE])
            Z = mk("Z", [P, 8 * D])
            TRI = mk("TRI", [R, R])
            stg_ = mk("stg_", [R, 2, D])
            stT = mk("stT", [P, 2, DT, R])
            hT = mk("hT5", [P, 2, DT, R])
            s6 = mk("s6", [R, T, 6])
            sc = {k: mk("f_" + k, [R, T]) for k in ("mean", "dm", "var", "t1", "std", "rstd", "gn", "gr", "th", "gs", "mx", "sm", "prb", "idx", "pos", "kept", "sf", "drop")}
            q4 = {k: mk("q_" + k, [R, T, GH]) for k in ("as", "den", "r", "asr")}
            hm = mk("hm", [R, T])
            e8 = {k: mk("e_" + k, [R, T, XE]) for k in ("lg", "ex", "eq", "oh", "tot", "inc", "po")}
            one_t = mk("one_t", [R, T])
            sidx = mk("scidx", [R, T], I32)
            n = {k: b[:] for k, b in sc.items()}
            GN = GACC[0:R, :, 0:D]
            GN_ = GACC[0:R]
            GN4 = GN.rearrange("r t (h d) -> r t h d", h=GH)
            XX = XN[:, :, 0:D]
            wide = lambda k: RW[:, k, :].unsqueeze(1).to_broadcast([R, T, D])
            over = lambda ap: ap.unsqueeze(2).to_broadcast([R, T, D])
            block = ctx.enter_context(nc.Block())

            @block.sync
            def _(sp):
                sp.dma_start(NTB[:], ft_dram.rearrange("(t r) d -> r t d", r=R)).then_inc(f_in, 16)
                for k, a_ in enumerate((bo, g1, beta1, bias2, g2, beta2, gbc)):
                    sp.dma_start(RW[:, k, :], bcast(a_, R, D)).then_inc(f_in, 16)
                with nc.allow_non_contiguous_dma("bias column"):
                    sp.dma_start(b1c[:], bias1.rearrange("(o p) -> p o", p=P)).then_inc(f_in, 16)
                sp.dma_start(W1s[:], W1.rearrange("(k p) f -> p k f", p=P)).then_inc(f_in, 16)
                sp.dma_start(W2s[:], W2.rearrange("(k p) f -> p k f", p=P)).then_inc(f_in, 16)
                sp.dma_start(gw[:], gate_w.rearrange("(k p) e -> p k e", p=P)).then_inc(f_in, 16)
                sp.dma_start(gbr[:], bcast(gate_b, R, XE)).then_inc(f_in, 16)
                sp.wait_ge(zset, 1)
                for k in range(4):
                    sp.dma_start(buf_dram[k * 1024:(k + 1) * 1024, :].rearrange("(p j) d -> p (j d)", p=P), Z[:]).then_inc(z_out, 16)
                sp.wait_ge(xn_used, 1)
                sp.dma_start(XX, x.rearrange("(t r) d -> r t d", r=R)).then_inc(x2_in, 16)
                sp.wait_ge(sums_ready, 1)
                for h in range(GH):
                    sp.dma_start(bass.AP(g_dram.tensor, h * N * DH, [[DH, R], [R * DH, T], [1, DH]]), GN4[:, :, h, :]).then_inc(g_out, 16)
                sp.wait_ge(g_out, 16 * GH)
                sp.dma_start(GN, g_dram.rearrange("(t r) d -> r t d", r=R)).then_inc(g_in, 16)

            @block.gpsimd
            def _(pool):
                c = Chain(pool, p5)
                pool.memset(Z[:], 0.0).then_inc(zset, 1)
                c(pool.memset(TRI[:], 1.0))
                pool.affine_select(out=TRI[:], in_=TRI[:], compare_op=ALU.is_ge, fill=0.0, base=0, pattern=[[1, R]],
                                   channel_multiplier=-1).then_inc(tri_ready, 1)
                pool.wait_ge(asr_ready, 1)
                pool.wait_ge(f_in, 16 * 13)
                nt4 = NTB[:].rearrange("r t (h d) -> r t h d", h=GH)
                pool.tensor_tensor(nt4, nt4, q4["asr"][:].unsqueeze(3).to_broadcast([R, T, GH, DH]), ALU.mult).then_inc(nt_done, 1)
                c(pool.tensor_tensor(GN4, GN4, q4["r"][:].unsqueeze(3).to_broadcast([R, T, GH, DH]), ALU.mult))
                pool.wait_ge(nt_done, 1)
                pool.tensor_tensor(GN, GN, NTB[:], ALU.add).then_inc(sums_ready, 1)
                pool.wait_ge(sc_ready, 1)
                pool.wait_ge(z_out, 64)
                for t in range(T):
                    pool.indirect_dma_start(out=buf_dram, out_offset=bass.IndirectOffsetOnAxis(ap=sidx[:, t:t + 1], axis=0),
                                            in_=ACC[:, t, :], in_offset=None, bounds_check=XE * SLOT - 1, oob_is_err=False).then_inc(sc_out, 16)
                pool.wait_ge(sc_out, 16 * T)

            @block.tensor
            def _(pe):
                pe.sem_inc(t_full, 2); pe.sem_inc(h_full, 2); pe.sem_inc(m_full, 2)
                pe.wait_ge(f_in, 16 * 13)
                pe.wait_ge(tri_ready, 1)

                def turn(t, par, pass_=0):
                    n_ = pass_ * T + t
                    pe.wait_ge(s_full, done(n_))
                    pe.wait_ge(tt_full, done(n_ - (1 if zero(t) else 2)))
                    for k in range(DT):
                        last = pe.transpose(bank[6 * par][:, k * P:k * P + R], stg_[:, par, k * P:(k + 1) * P], ident[0:R, 0:R])
                    last.then_inc(t_full, 1)

                def second(t, par):
                    pe.wait_ge(hr_full, done(t))
                    pe.wait_ge(m_used, done(t - 2))
                    for f in range(DT):
                        last = pe.matmul(bank[2 + 3 * par][0:R, 0:D], hT[:, par, f, :], W2s[:, f, :], start=(f == 0), stop=(f == 1))
                    last.then_inc(m_full, 1)

                def mlp(t, par):
                    if before(t, T - 1):
                        turn(t + 1, 1 - par)
                    pe.wait_ge(tt_full, done(t))
                    pe.wait_ge(hr_full, done(t - 2))
                    for f in range(DT):
                        for k in range(DT):
                            last = pe.matmul(bank[1 + 6 * par][:, f * P:f * P + R], W1s[:, k, f * P:(f + 1) * P], stT[:, par, k, :], start=(k == 0), stop=(k == 1))
                    last.then_inc(h_full, 1)
                    if not zero(t):
                        second(t - 1, 1 - par)
                turn(0, 0)
                over_tiles(pe, mlp)
                second(T - 1, 0)

                def gates(t, par):
                    if before(t, T - 1):
                        turn(t + 1, 1 - par, 1)
                    pe.wait_ge(tt_full, done(T + t))
                    for k in range(DT):
                        last = pe.matmul(bank[3][0:R, bass.ds(t * XE, XE)], stT[:, par, k, :], gw[:, k, :], start=(k == 0), stop=(k == 1))
                    last.then_inc(lg_done, 1)
                pe.sem_inc(lg_done, 2)
                turn(0, 0, 1)
                over_tiles(pe, gates)
                pe.wait_ge(oh_ready, 1)
                oh = e8["oh"][:].rearrange("r t e -> r (t e)")
                pe.matmul(bank[4][0:R, 0:T * XE], TRI[:], oh, start=True, stop=True)
                pe.matmul(bank[5][0:R, 0:T * XE], ones[0:R, 0:R], oh, start=True, stop=True).then_inc(cnt_done, 1)

            @block.scalar
            def _(act):
                act.sem_inc(s_full, 2); act.sem_inc(tt_full, 2); act.sem_inc(hr_full, 2)
                act.wait_ge(f_in, 16 * 13)
                act.wait_ge(sq_v, 1)
                act.activation(n["std"], n["t1"], ACT.Sqrt).then_inc(sq_a, 1)

                def stage(t, par, pass_=0):
                    n_ = pass_ * T + t
                    act.wait_ge((n1_done, n3_done)[pass_], done(t))
                    act.wait_ge(t_full, done(n_ - (1 if zero(t) else 2)))
                    act.activation(stg_[:, par, :], row(ACC, t), ACT.Copy).then_inc(s_full, 1)

                def turned(t, par, pass_=0):
                    n_ = pass_ * T + t
                    act.wait_ge(t_full, done(n_))
                    act.wait_ge((h_full, lg_done)[pass_], done(t - 2))
                    act.activation(stT[:, par], bank[6 * par][:, 0:D].rearrange("p (k r) -> p k r", k=DT)[:, :, 0:R], ACT.Copy).then_inc(tt_full, 1)

                def mlp(t, par):
                    if before(t, T - 2):
                        stage(t + 2, par)
                    if before(t, T - 1):
                        turned(t + 1, 1 - par)
                    act.wait_ge(h_full, done(t))
                    act.wait_ge(m_full, done(t - 2))
                    for f in range(DT):
                        last = act.activation(hT[:, par, f, :], bank[1 + 6 * par][:, f * P:f * P + R], ACT.Relu, bias=b1c[:, f:f + 1])
                    last.then_inc(hr_full, 1)
                stage(0, 0)
                stage(1, 1)
                turned(0, 0)
                over_tiles(act, mlp)
                act.wait_ge(sq_v, 2)
                act.activation(n["std"], n["t1"], ACT.Sqrt).then_inc(sq_a, 1)
                act.wait_ge(gn_v, 1)
                act.activation(GN, GN, ACT.Relu).then_inc(gn_a, 1)
                act.wait_ge(gn_a, 1)

                def square(t, par):
                    act.activation(row(NTB, t), row(GN_, t)[:, 0:D], ACT.Square, accum_out=sc["gn"][:, bass.ds(t, 1)]).then_inc(gn_sq, 1)
                over_tiles(act, square)
                act.wait_ge(gn_sq, T)
                act.activation(n["gr"], n["gn"], ACT.Sqrt).then_inc(gn_a, 1)
                act.wait_ge(gn_v, 2)
                act.activation(n["th"], n["gr"], ACT.Tanh).then_inc(gn_a, 1)
                act.wait_ge(sq_v, 3)
                act.activation(n["std"], n["t1"], ACT.Sqrt).then_inc(sq_a, 1)

                def gates(t, par):
                    if before(t, T - 2):
                        stage(t + 2, par, 1)
                    if before(t, T - 1):
                        turned(t + 1, 1 - par, 1)
                stage(0, 0, 1)
                stage(1, 1, 1)
                turned(0, 0, 1)
                over_tiles(act, gates)
                act.wait_ge(gn_v, 3)
                act.activation(e8["ex"][:], e8["lg"][:], ACT.Exp).then_inc(gn_a, 1)

            @block.vector
            def _(v):
                c = Chain(v, v5)
                v.sem_inc(m_used, 2)
                v.memset(one_t[:], 1.0)
                c(v.tensor_scalar(hm[:], GACC[0:R, :, 264], -1.0, 1.0, ALU.mult, ALU.add))
                c(v.tensor_tensor(q4["as"][:], GACC[0:R, :, 260:264], hm[:].unsqueeze(2).to_broadcast([R, T, GH]), ALU.add))
                c(v.tensor_tensor(q4["den"][:], GACC[0:R, :, 256:260], q4["as"][:], ALU.add))
                c(v.tensor_scalar(q4["den"][:], q4["den"][:], MIN_NORM, None, ALU.max))
                c(v.reciprocal(q4["r"][:], q4["den"][:]))
                v.tensor_tensor(q4["asr"][:], q4["as"][:], q4["r"][:], ALU.mult).then_inc(asr_ready, 1)
                c(v.tensor_tensor(ACC[:], ACC[:], XX, ALU.add))
                v.sem_inc(xn_used, 1)
                v.wait_ge(f_in, 16 * 13)
                c(v.tensor_tensor(ACC[:], ACC[:], wide(0), ALU.add))

                def each(k, body):
                    with v.Fori(0, T // 2) as i:
                        c.enter(i, k)
                        body([2 * i, 2 * i + 1])
                    c.leave(T // 2)
                    body([T - 1])

                def stats(t, buf):
                    v.bn_stats(row(s6, t), row(buf, t)[:, 0:D]).then_inc(st_n, 1)

                def moments(eps, k):
                    v.wait_ge(st_n, k * T)
                    s = [s6[:, :, j] for j in range(6)]
                    c(v.tensor_tensor(n["mean"], s[1], s[4], ALU.add))
                    c(v.tensor_scalar(n["mean"], n["mean"], 0.5, None, ALU.mult))
                    c(v.tensor_tensor(n["dm"], s[1], s[4], ALU.subtract))
                    c(v.tensor_tensor(n["dm"], n["dm"], n["dm"], ALU.mult))
                    c(v.tensor_tensor(n["var"], s[2], s[5], ALU.add))
                    c(v.tensor_scalar(n["var"], n["var"], 1.0 / D, eps, ALU.mult, ALU.add))
                    v.scalar_tensor_tensor(out=n["t1"], in0=n["dm"], scalar=0.25, in1=n["var"], op0=ALU.mult, op1=ALU.add).then_inc(sq_v, 1)
                    v.wait_ge(sq_a, k)
                    c(v.reciprocal(n["rstd"], n["std"]))

                scalar = lambda name, t: sc[name][:, bass.ds(t, 1)]

                def centre(t, gain):
                    return v.scalar_tensor_tensor(out=row(ACC, t), in0=row(ACC, t), scalar=scalar("mean", t), in1=RW[:, gain, :],
                                                  op0=ALU.subtract, op1=ALU.mult)

                each(0, lambda ts: [stats(t, ACC) for t in ts])
                moments(1e-6, 1)
                v.sem_inc(n1_done, 2)

                def norm1(ts):
                    for t in ts:
                        last = centre(t, 1)
                    c(last)
                    for t in ts:
                        v.scalar_tensor_tensor(out=row(ACC, t), in0=row(ACC, t), scalar=scalar("rstd", t), in1=RW[:, 2, :],
                                               op0=ALU.mult, op1=ALU.add).then_inc(n1_done, 1)
                each(1, norm1)
                v.wait_ge(n1_done, done(T - 1))

                def add_mlp(t, par):
                    v.wait_ge(m_full, done(t))
                    v.tensor_tensor(row(ACC, t), bank[2 + 3 * par][0:R, 0:D], row(ACC, t), ALU.add).then_inc(m_used, 1)
                    v.tensor_tensor(row(XN, t)[:, 0:D], row(XN, t)[:, 0:D], RW[:, 5, :], ALU.add)
                    v.wait_ge(m_used, done(t))
                    v.tensor_tensor(row(ACC, t), row(ACC, t), RW[:, 3, :], ALU.add).then_inc(loops5, 1)
                    v.wait_ge(loops5, t + 1)
                    stats(t, ACC)
                v.wait_ge(x2_in, 16)
                over_tiles(v, add_mlp)
                v.wait_ge(g_in, 16)
                v.tensor_tensor(GN, GN, wide(6), ALU.add).then_inc(gn_v, 1)
                moments(1e-6, 2)

                def norm2(ts):
                    for t in ts:
                        last = centre(t, 4)
                    c(last)
                    for t in ts:
                        last = v.scalar_tensor_tensor(out=row(XN, t)[:, 0:D], in0=row(ACC, t), scalar=scalar("rstd", t), in1=row(XN, t)[:, 0:D],
                                                      op0=ALU.mult, op1=ALU.add)
                    c(last)
                each(2, norm2)
                v.wait_ge(gn_a, 2)
                v.tensor_scalar(n["gr"], n["gr"], MIN_NORM, None, ALU.max).then_inc(gn_v, 1)
                v.wait_ge(gn_v, 2)
                c(v.reciprocal(n["gs"], n["gr"]))
                v.wait_ge(gn_a, 3)
                c(v.tensor_scalar(n["th"], n["th"], MAXN, None, ALU.min))
                c(v.tensor_tensor(n["gs"], n["gs"], n["th"], ALU.mult))

                def add_graph(ts):
                    for t in ts:
                        last = v.scalar_tensor_tensor(out=row(XN, t)[:, 0:D], in0=row(GN_, t)[:, 0:D], scalar=scalar("gs", t), in1=row(XN, t)[:, 0:D],
                                                      op0=ALU.mult, op1=ALU.add)
                    c(last)
                    for t in ts:
                        stats(t, XN)
                each(1, add_graph)
                moments(1e-5, 3)
                v.sem_inc(n3_done, 2)

                def norm3(ts):
                    for t in ts:
                        v.tensor_scalar(row(ACC, t), row(XN, t)[:, 0:D], scalar("mean", t), scalar("rstd", t), ALU.subtract, ALU.mult).then_inc(n3_done, 1)
                each(0, norm3)

                v.wait_ge(lg_done, done(T - 1))
                lg, oh = e8["lg"][:], e8["oh"][:]
                c(v.tensor_tensor(lg, bank[3][0:R, 0:T * XE].rearrange("r (t e) -> r t e", e=XE), gbr[:].unsqueeze(1).to_broadcast([R, T, XE]), ALU.add))
                c(v.tensor_reduce(n["mx"], lg, AX.X, ALU.max))
                over8 = lambda ap: ap.unsqueeze(2).to_broadcast([R, T, XE])
                v.tensor_tensor(lg, lg, over8(n["mx"]), ALU.subtract).then_inc(gn_v, 1)
                v.wait_ge(gn_v, 3)
                c(v.tensor_scalar(e8["eq"][:], lg, 0.0, None, ALU.is_equal))
                c(v.scalar_tensor_tensor(out=e8["eq"][:], in0=e8["eq"][:], scalar=-float(XE), in1=iota_f[0:R, XE:2 * XE].unsqueeze(1).to_broadcast([R, T, XE]),
                                         op0=ALU.mult, op1=ALU.add))
                c(v.tensor_reduce(n["idx"], e8["eq"][:], AX.X, ALU.min))
                v.tensor_tensor(oh, iota_f[0:R, 0:XE].unsqueeze(1).to_broadcast([R, T, XE]), over8(n["idx"]), ALU.is_equal).then_inc(oh_ready, 1)
                v.wait_ge(gn_a, 4)
                c(v.tensor_reduce(n["sm"], e8["ex"][:], AX.X, ALU.add))
                c(v.reciprocal(n["prb"], n["sm"]))
                v.wait_ge(cnt_done, 1)
                v.wait_ge(oh_ready, 1)
                c(v.tensor_copy(e8["tot"][:], bank[5][0:R, 0:T * XE].rearrange("r (t e) -> r t e", e=XE)))
                for e in range(XE):
                    last = v.tensor_tensor_scan(e8["inc"][:, :, e], one_t[:], e8["tot"][:, :, e], 0.0, ALU.mult, ALU.add)
                c(last)
                c(v.tensor_tensor(e8["inc"][:], e8["inc"][:], e8["tot"][:], ALU.subtract))
                c(v.tensor_tensor(e8["po"][:], bank[4][0:R, 0:T * XE].rearrange("r (t e) -> r t e", e=XE), e8["inc"][:], ALU.add))
                c(v.tensor_tensor(e8["po"][:], e8["po"][:], oh, ALU.mult))
                c(v.tensor_reduce(n["pos"], e8["po"][:], AX.X, ALU.add))
                c(v.tensor_scalar(n["kept"], n["pos"], CAP + 0.5, None, ALU.is_lt))
                c(v.tensor_scalar(n["pos"], n["pos"], float(CAP), -1.0, ALU.min, ALU.add))
                c(v.scalar_tensor_tensor(out=n["sf"], in0=n["idx"], scalar=float(SLOT), in1=n["pos"], op0=ALU.mult, op1=ALU.add))
                c(v.tensor_scalar(n["drop"], n["kept"], -float(XE * SLOT), float(XE * SLOT), ALU.mult, ALU.add))
                c(v.tensor_tensor(n["drop"], n["drop"], n["sf"], ALU.add))
                c(v.tensor_copy(slot[:], n["sf"]))
                c(v.tensor_copy(sidx[:], n["drop"]))
                v.tensor_tensor(wgt[:], n["prb"], n["kept"], ALU.mult).then_inc(sc_ready, 1)

        w_full = [sem("w_full0"), sem("w_full1")]
        bt_full = sem("bt_full"); bT_full = sem("bT_full"); y_full = sem("y_full"); y_out = [sem("y_out0"), sem("y_out1")]; y_free = sem("y_free")
        hp_full = sem("hp_full"); hh_full = sem("hh_full"); yp_full = sem("yp_full"); yy_full = sem("yy_full")
        with ExitStack() as ctx:
            mk = lambda name, shape, dt=F32: sb(name, shape, dt, ctx=ctx)
            W1e = mk("W1e", [P, 2, DT, FF]); W2e = mk("W2e", [P, 2, FF // P, D])
            b1e = mk("b1e", [P, 2, FF // P]); b2e = mk("b2e", [P, 2, D])
            BE = mk("BE", [P, 2, 4, D]); BT = XNT[:, :, 0:SLOT]
            H = mk("H", [P, FF // P, CAP])
            Y = mk("Y", [P, 2, 4, D])
            NF, NQ, LASTQ = FF // P, 4, CAP - 3 * P
            block = ctx.enter_context(nc.Block())

            def experts(eng, body):
                with eng.Fori(0, XE // 2) as i:
                    body(2 * i, 0, i)
                    body(2 * i + 1, 1, i)

            @block.sync
            def _(sp):
                def load(e, par, i):
                    sp.wait_ge(y_full, done(e - 2))
                    one = bass.ds(e, 1)
                    sp.dma_start(BE[:, par], buf_dram.rearrange("(e j p) d -> e p j d", e=XE, p=P)[one].rearrange("e p j d -> (e p) j d")).then_inc(w_full[par], 16)
                    sp.dma_start(W1e[:, par], w1.rearrange("e (k p) f -> e p k f", p=P)[one].rearrange("e p k f -> (e p) k f")).then_inc(w_full[par], 16)
                    sp.dma_start(W2e[:, par], w2.rearrange("e (c p) d -> e p c d", p=P)[one].rearrange("e p c d -> (e p) c d")).then_inc(w_full[par], 16)
                    with nc.allow_non_contiguous_dma("bias column"):
                        sp.dma_start(b1e[:, par], b1.rearrange("e (c p) -> e p c", p=P)[one].rearrange("e p c -> (e p) c")).then_inc(w_full[par], 16)
                    sp.dma_start(b2e[:, par], bass.AP(b2.tensor, e * D, [[0, P], [1, D]])).then_inc(w_full[par], 16)
                experts(sp, load)
                sp.wait_ge(y_out[0], 16 * (XE // 2))
                sp.wait_ge(y_out[1], 16 * (XE // 2))

            @block.gpsimd
            def _(pool):
                def store(e, par, i):
                    pool.wait_ge(y_full, done(e))
                    rows = y_dram.rearrange("(e j p) d -> e p j d", e=XE, p=P)[bass.ds(e, 1)].rearrange("e p j d -> (e p) j d")
                    pool.dma_start(rows, Y[:, par]).then_inc(y_out[par], 16)
                    pool.wait_ge(y_out[par], 16 * (i + 1))
                    pool.sem_inc(y_free, 1)
                pool.memset(Y[:, :, 3, :], 0.0).then_inc(y_free, 2)
                experts(pool, store)

            @block.tensor
            def _(pe):
                pe.sem_inc(bt_full, 2); pe.sem_inc(hp_full, 8); pe.sem_inc(yp_full, 4)

                def expert(e, par, i):
                    pe.wait_ge(w_full[par], 80 * (i + 1))
                    pe.wait_ge(bT_full, done(e - 1))
                    for k in range(DT):
                        for j in range(4):
                            last = pe.transpose(bank[k][:, j * P:(j + 1) * P], BE[:, par, j, k * P:(k + 1) * P], ident[:])
                    last.then_inc(bt_full, 1)
                    pe.wait_ge(bT_full, done(e))
                    for f in range(NF):
                        pe.wait_ge(hh_full, NF * e + f + 8 - 3)
                        for k in range(DT):
                            last = pe.matmul(bank[2 + f % 4][:, 0:CAP], W1e[:, par, k, f * P:(f + 1) * P], BT[:, k, 0:CAP], start=(k == 0), stop=(k == 1))
                        last.then_inc(hp_full, 1)
                    pe.wait_ge(hh_full, NF * e + NF + 8)
                    for j in range(NQ):
                        m = P if j < 3 else LASTQ
                        pe.wait_ge(yy_full, NQ * e + j + 4 - 1)
                        for f in range(NF):
                            last = pe.matmul(bank[6 + j % 2][0:m, 0:D], H[:, f, j * P:j * P + m], W2e[:, par, f, :], start=(f == 0), stop=(f == NF - 1))
                        last.then_inc(yp_full, 1)
                experts(pe, expert)

            @block.scalar
            def _(act):
                act.sem_inc(bT_full, 2); act.sem_inc(hh_full, 8)

                def expert(e, par, i):
                    act.wait_ge(bt_full, done(e))
                    act.wait_ge(yp_full, NQ * e + 4)
                    for k in range(DT):
                        last = act.activation(BT[:, k, :], bank[k][:], ACT.Copy)
                    last.then_inc(bT_full, 1)
                    for f in range(NF):
                        act.wait_ge(hp_full, NF * e + f + 9)
                        act.activation(H[:, f, :], bank[2 + f % 4][:, 0:CAP], ACT.Relu, bias=b1e[:, par, f:f + 1]).then_inc(hh_full, 1)
                experts(act, expert)

            @block.vector
            def _(v):
                v.sem_inc(y_full, 2); v.sem_inc(yy_full, 4)

                def expert(e, par, i):
                    v.wait_ge(y_free, done(e - 2))
                    for j in range(NQ):
                        m = P if j < 3 else LASTQ
                        v.wait_ge(yp_full, NQ * e + j + 5)
                        ins = v.tensor_tensor(Y[0:m, par, j, :], bank[6 + j % 2][0:m, 0:D], b2e[0:m, par, :], ALU.add)
                        ins.then_inc(yy_full, 1)
                    v.wait_ge(yy_full, NQ * e + NQ + 4)
                    v.sem_inc(y_full, 1)
                experts(v, expert)

        GT = 5
        yg_in = [sem(f"yg_in{k}") for k in range(T // GT)]; yw_full = sem("yw_full"); ot_done = sem("ot_done"); ot_out = sem("ot_out")
        alt_seen = sem("alt_seen"); v7 = sem("v7")
        with ExitStack() as ctx:
            mk = lambda name, shape, dt=F32: sb(name, shape, dt, ctx=ctx)
            YG = GACC[0:R, :, 0:D]
            yw = mk("yw", [R, T, D]); alt = mk("alt", [R, 2, GT, D]); neg_ = mk("neg_", [R, 2, GT, D])
            fin = mk("fin", [R, 2, GT, D], I32)
            block = ctx.enter_context(nc.Block())

            @block.gpsimd
            def _(pool):
                for t in range(T):
                    pool.indirect_dma_start(out=YG[:, t, :], out_offset=None, in_=y_dram,
                                            in_offset=bass.IndirectOffsetOnAxis(ap=slot[:, t:t + 1], axis=0)).then_inc(yg_in[t // GT], 16)

            @block.scalar
            def _(act):
                for k in range(T // GT):
                    act.wait_ge(yg_in[k], 16 * GT)
                    for t in range(GT * k, GT * (k + 1)):
                        last = act.activation(yw[:, t, :], YG[:, t, :], ACT.Copy, scale=wgt[:, t:t + 1])
                    last.then_inc(yw_full, 1)

            @block.vector
            def _(v):
                c = Chain(v, v7)
                for k in range(T // GT):
                    v.wait_ge(yw_full, k + 1)
                    ts, par = slice(GT * k, GT * (k + 1)), k % 2
                    y = yw[:, ts, :]
                    v.tensor_scalar(fin[:, par], y, 0.0, 0.0, ALU.mult, ALU.is_equal)
                    v.tensor_scalar(alt[:, par], y, 0.0, 1.0e4, ALU.max, ALU.min)
                    c(v.tensor_scalar(neg_[:, par], y, 0.0, -1.0e4, ALU.min, ALU.max))
                    c(v.tensor_tensor(alt[:, par], alt[:, par], neg_[:, par], ALU.add))
                    v.sem_inc(alt_seen, 1)
                    c(v.copy_predicated(alt[:, par], fin[:, par], y))
                    v.tensor_tensor(XN[:, ts, 0:D], XN[:, ts, 0:D], alt[:, par], ALU.add).then_inc(ot_done, 1)

            @block.sync
            def _(sp):
                for k in range(T // GT):
                    sp.wait_ge(ot_done, k + 1)
                    sp.dma_start(out[GT * k * R:GT * (k + 1) * R, :].rearrange("(t r) d -> r t d", r=R), XN[:, GT * k:GT * (k + 1), 0:D]).then_inc(ot_out, 16)
                sp.wait_ge(ot_out, 16 * (T // GT))


_INS = ['x', 'src', 'dst', 'L0_gnn_W', 'L0_gnn_b_lin', 'L0_gnn_att', 'L0_gnn_b_conv', 'L0_mix_Wq', 'L0_mix_bq',
        'L0_mix_Wk', 'L0_mix_bk', 'L0_mix_Wv', 'L0_mix_bv', 'L0_mix_Wo', 'L0_mix_bo', 'L0_mix_proj', 'L0_mix_W1',
        'L0_mix_bias1', 'L0_mix_W2', 'L0_mix_bias2', 'L0_mix_g1', 'L0_mix_beta1', 'L0_mix_g2', 'L0_mix_beta2',
        'L0_ffn_gate_w', 'L0_ffn_gate_b', 'L0_ffn_w1', 'L0_ffn_b1', 'L0_ffn_w2', 'L0_ffn_b2']
_OUTS = [((3125, 256), 'float32')]


def kernel(**inputs):
    import numpy as _np
    import concourse.bacc as _bacc
    from concourse import mybir as _mybir
    from concourse.bass_utils import run_bass_kernel_spmd as _run

    nc = _bacc.Bacc("TRN2", target_bir_lowering=False, num_devices=1)
    arrays, args = {}, []
    for name in _INS:
        a = _np.ascontiguousarray(inputs[name])
        arrays[f"in_{name}_dram"] = a
        args.append(nc.dram_tensor(f"in_{name}_dram", a.shape, _mybir.dt.from_np(a.dtype), kind="ExternalInput").ap())
    for i, (shape, dtype) in enumerate(_OUTS):
        dt = _mybir.dt.from_np(_np.dtype(dtype))
        args.append(nc.dram_tensor(f"out_{i}_dram", shape, dt, kind="ExternalOutput").ap())
    build(nc, *args)
    r = _run(nc, [arrays], core_ids=[0])
    got = tuple(r.results[0][f"out_{i}_dram"] for i in range(len(_OUTS)))
    return got[0]
```

```python
from contextlib import ExitStack

import numpy as np
import concourse.bass as bass
from concourse import mybir

ALU = mybir.AluOpType
ACT = mybir.ActivationFunctionType
F32 = mybir.dt.float32
BF16 = mybir.dt.bfloat16
F32R = mybir.dt.float32r
I32 = mybir.dt.int32
AX = mybir.AxisListType

P = 128
N, D, E = 3125, 256, 50000
T, R = 25, 125
DT = D // P
CH = -(-E // P)
STEPS = 416
GS = 8
NG = STEPS // GS
SB = 4
GH = 4
DH = D // GH
MH = 8
PAIRS = MH // 2
PW = 2 * D
BIG = 1.0e30
MIN_NORM = 1e-15
MAXN = 1.0 - 0.004
EPS_ATT = 1e-6
SCALE = float(D) ** -0.25
ATANH_MAX = float(np.float32(1.0 - 1e-7))
XE, FF = 8, 1024
CAP = 489
SLOT = 512


class Chain:

    def __init__(self, sem):
        self.sem, self.base, self.n = sem, 0, 0

    def on(self, eng):
        self.eng = eng
        return self

    def __call__(self, ins):
        ins.then_inc(self.sem, 1)
        self.n += 1
        self.eng.wait_ge(self.sem, self.base + self.n)

    def enter(self, i, k):
        self.outer = (self.base, self.n)
        self.base = i * k + (self.base + self.n)
        self.n, self.k = 0, k

    def leave(self, count):
        assert self.n == self.k, (self.n, self.k)
        base, n = self.outer
        self.base, self.n = base, n + count * self.k


def done(t):
    return t + 3


def one_pass(ap):
    return ap.bitcast(F32R)


def bcast(ap, rows, cols, offset=0):
    return bass.AP(ap.tensor, offset, [[0, rows], [1, cols]])


def build(nc, x, src, dst, gW, gb, gatt, gbc, Wq, bq, Wk, bk, Wv, bv, Wo, bo, proj, W1, bias1, W2, bias2,
          g1, beta1, g2, beta2, gate_w, gate_b, w1, b1, w2, b2, out):
    top = ExitStack()
    with top:
        def keep(name, shape, dt=F32):
            return top.enter_context(nc.sbuf_tensor(name, shape, dt))

        def pb(name, shape, dt=F32, ctx=top):
            return ctx.enter_context(nc.psum_tensor(name, shape, dt))

        def sem(name):
            return top.enter_context(nc.semaphore(name))

        dve_steps, pool_steps = Chain(sem("dve_steps")), Chain(sem("pool_steps"))

        lx_dram = nc.dram_tensor("lx_dram", (N, D), F32).ap()
        ft_dram = nc.dram_tensor("ft_dram", (N, D), F32).ap()
        sj_dram = nc.dram_tensor("sj_dram", (N, GH), F32).ap()
        er_dram = nc.dram_tensor("er_dram", (CH, 1 + 2 * P), I32).ap()
        rel_dram = nc.dram_tensor("rel_dram", (SB * P, P), BF16).ap()

        XN = keep("XN", [R, T, D + 1])
        slot = keep("slot", [R, T], I32)
        wgt = keep("wgt", [R, T])
        ident = keep("ident", [P, P])
        layers = top.enter_context(ExitStack())

        def sb(name, shape, dt=F32, ctx=layers):
            return ctx.enter_context(nc.sbuf_tensor(name, shape, dt))

        XNT = sb("XNT", [P, DT, N])
        ACC = sb("ACC", [R, T, D])
        GACC = sb("GACC", [P, T, 265])
        SIJ = sb("SIJ", [R, T, 2 * GH])
        ones = sb("ones", [P, P])
        iota_p = sb("iota_p", [P, 1])
        iota_f = sb("iota_f", [P, P])
        CSE = sb("CSE", [P, D + 1])
        idxT = sb("idxT", [P, STEPS], I32)
        relT = sb("relT", [P, STEPS])
        PD = sb("PD", [P, 2, SB, P])
        PEN = PD[:, 0]
        D0 = PD[:, 1]
        tI = sb("tI", [1, STEPS], I32)

        bank = [pb(f"bank{i}", [P, 512]) for i in range(8)]

        x_in = sem("x_in"); w_in = sem("w_in"); e_in = sem("e_in"); er_ready = sem("er_ready")
        const_ready = sem("const_ready")
        xns_full = sem("xns_full"); xns_kept = sem("xns_kept"); xt_full = sem("xt_full"); xts_full = sem("xts_full")
        xts_kept = sem("xts_kept"); u_full = sem("u_full"); u_kept = sem("u_kept"); sq_done = sem("sq_done")
        hbs_full = sem("hbs_full"); lx_done = sem("lx_done")
        stat_n = sem("stat_n"); cs_full = sem("cs_full")
        pre_psum = sem("pre_psum"); pre_used = sem("pre_used"); sc_v = sem("sc_v"); sc_a = sem("sc_a")
        hb2 = sem("hb2"); lx_out = [sem(f"lx_out{k}") for k in range(5)]; nt_in = [sem(f"nt_in{h}") for h in range(GH)]
        sij_ready = sem("sij_ready"); tab_out = sem("tab_out"); cf_psum = sem("cf_psum"); cf_used = sem("cf_used")
        ci_ready = sem("ci_ready"); er_rows = sem("er_rows"); rel_ready = sem("rel_ready"); rel_out = sem("rel_out")
        eT_psum = sem("eT_psum")

        with ExitStack() as ctx:
            Wn = sb("Wn", [P, DT, D], ctx=ctx)
            WT = sb("WT", [P, DT, D + 1], ctx=ctx)
            bcol = sb("bcol", [P, DT], ctx=ctx)
            hbcol = sb("hbcol", [P, DT], ctx=ctx)
            hbrow = sb("hbrow", [R, D], ctx=ctx)
            attr = sb("attr", [R, 2, GH, DH], ctx=ctx)
            st6 = sb("st6", [R, T, 6], ctx=ctx)
            xns = sb("xns", [R, 2, D + 1], ctx=ctx)
            xts = sb("xts", [P, 2, DT, R], ctx=ctx)
            hbs = sb("hbs", [R, 2, D], ctx=ctx)
            junk = sb("junk", [R, 2, D], ctx=ctx)
            prod = ACC[:].rearrange("r t d -> r (t d)").rearrange("r (a s t d) -> r a s t d", a=2, s=2, t=T)
            bsq = sb("bsq", [P, DT], ctx=ctx)
            zrow = sb("zrow", [1, P], ctx=ctx)
            zwide = sb("zwide", [1, D + 1], ctx=ctx)
            hs = sb("hs", [P, 8], ctx=ctx)
            ns = {k: sb("ns_" + k, [R, T], ctx=ctx) for k in (
                "mean", "var", "dm", "std", "rstd", "n0", "nc", "p", "q", "lp", "lq", "at", "ser", "msk", "s1",
                "usq", "uh", "nu", "th", "f1", "x2", "xy", "A", "B", "den", "P", "Q", "nv2", "nv", "g",
                "a1", "a2", "t0", "t1")}
            er = sb("er", [P, SB, 1 + 2 * P], I32, ctx=ctx)
            erf = sb("erf", [P, SB, 1 + 2 * P], ctx=ctx)
            firsts = sb("firsts", [1, CH - 1], I32, ctx=ctx)
            firstf = sb("firstf", [1, CH - 1], ctx=ctx)
            thr = sb("thr", [T - 1, 1], ctx=ctx)
            ge = sb("ge", [T - 1, CH - 1], ctx=ctx)
            iotc = sb("iotc", [P, CH - 1], ctx=ctx)
            stepid = sb("stepid", [P, SB], ctx=ctx)
            cif = sb("cif", [P, SB], ctx=ctx)
            cii = sb("cii", [P, SB], I32, ctx=ctx)
            tf = sb("tf", [P, SB], ctx=ctx)
            t125 = sb("t125", [P, SB], ctx=ctx)
            AC = sb("AC", [P, CH - 1], ctx=ctx)
            ejunk = sb("ejunk", [P, CH - 1], ctx=ctx)
            rel = sb("rel", [P, SB, P], ctx=ctx)
            relb = sb("relb", [P, SB, P], BF16, ctx=ctx)
            m1 = sb("m1", [P, SB, P], ctx=ctx)
            padd = sb("padd", [1, 48], I32, ctx=ctx)
            pads = sb("pads", [1, 48], I32, ctx=ctx)
            X = GACC[0:R, :, 0:D]
            NTs = GACC[0:R, :, 0:D]
            NT = GACC[0:R, :, 0:D].rearrange("r t (h d) -> r t h d", h=GH)
            TAIL = E - (CH - 1) * P
            col = lambda name, t: ns[name][:, bass.ds(t, 1)]

            def row(buf, t):
                return buf[:, bass.ds(t, 1), :].rearrange("r a c -> r (a c)")

            def over_tiles(eng, body):
                with eng.Fori(0, T // 2 - 1) as i:
                    body(2 * i, 0)
                    body(2 * i + 1, 1)
                for t in range(T - 3, T):
                    body(t, t % 2)

            before = lambda t, n_: not isinstance(t, int) or t < n_

            block = ctx.enter_context(nc.Block())

            @block.sync
            def _(sp):
                for k in range(5):
                    sp.dma_start(X[:, 5 * k:5 * k + 5, :],
                                 x[5 * k * R:5 * (k + 1) * R, :].rearrange("(t r) d -> r t d", r=R)).then_inc(x_in, 16)
                sp.dma_start(Wn[:], gW.rearrange("(o p) d -> p o d", p=P)).then_inc(w_in, 16)
                with nc.allow_non_contiguous_dma("bias column"):
                    sp.dma_start(bcol[:], gb.rearrange("(o p) -> p o", p=P)).then_inc(w_in, 16)
                sp.dma_start(hbrow[:], bcast(gb, R, D)).then_inc(w_in, 16)
                for s in range(2):
                    sp.dma_start(attr[:, s], bass.AP(gatt.tensor, s * DH, [[0, R], [2 * DH, GH], [1, DH]])).then_inc(w_in, 16)
                full = (CH - 1) * P
                with nc.allow_non_contiguous_dma("chunk edges"):
                    sp.dma_start(er_dram[0:CH - 1, 1:1 + P], dst[0:full].rearrange("(c e) -> c e", e=P)).then_inc(er_ready, 16)
                    sp.dma_start(er_dram[0:CH - 1, 1 + P:], src[0:full].rearrange("(c e) -> c e", e=P)).then_inc(er_ready, 16)
                    sp.dma_start(er_dram[CH - 1:CH, 1:1 + TAIL], dst[full:E].rearrange("(c e) -> c e", c=1)).then_inc(er_ready, 16)
                    sp.dma_start(er_dram[CH - 1:CH, 1 + P:1 + P + TAIL], src[full:E].rearrange("(c e) -> c e", c=1)).then_inc(er_ready, 16)
                    sp.dma_start(er_dram[1:CH, 0:1], bass.AP(dst.tensor, P - 1, [[P, CH - 1], [1, 1]])).then_inc(er_ready, 16)
                    sp.dma_start(firsts[:], bass.AP(dst.tensor, P, [[0, 1], [P, CH - 1]])).then_inc(e_in, 16)
                    sp.wait_ge(const_ready, 1)
                    sp.dma_start(er_dram[CH - 1:CH, 1 + TAIL:1 + P], padd[:, 0:P - TAIL]).then_inc(er_ready, 16)
                    sp.dma_start(er_dram[CH - 1:CH, 1 + P + TAIL:], pads[:, 0:P - TAIL]).then_inc(er_ready, 16)
                    sp.dma_start(er_dram[0:1, 0:1], padd[:, 0:1]).then_inc(er_ready, 16)
                for k in range(5):
                    sp.wait_ge(lx_done, done(5 * k + 4))
                    sp.dma_start(lx_dram[5 * k * R:5 * (k + 1) * R, :].rearrange("(t r) d -> r t d", r=R), ACC[:, 5 * k:5 * k + 5, :]).then_inc(lx_out[k], 16)
                for h in range(GH):
                    for k in range(5):
                        if 5 * k * R < (h + 1) * N // GH + 1:
                            sp.wait_ge(lx_out[k], 16)
                    sp.dma_start(NT[:, :, h, :], bass.AP(lx_dram.tensor, h * N * DH, [[DH, R], [R * DH, T], [1, DH]])).then_inc(nt_in[h], 16)
                sp.wait_ge(rel_ready, 1)
                for b in range(SB):
                    sp.dma_start(rel_dram[b * P:(b + 1) * P, :], relb[:, b, :]).then_inc(rel_out, 16)
                for h in range(GH):
                    sp.wait_ge(nt_in[h], 16)
                sp.dma_start(ft_dram.rearrange("(t r) d -> r t d", r=R), X).then_inc(tab_out, 16)
                sp.wait_ge(sij_ready, GH)
                with nc.allow_non_contiguous_dma("source scores"):
                    sp.dma_start(sj_dram.rearrange("(t r) h -> r t h", r=R), SIJ[:, :, GH:]).then_inc(tab_out, 16)
                sp.wait_ge(tab_out, 32)
                sp.wait_ge(rel_out, 16 * SB)

            @block.gpsimd
            def _(pool):
                c = pool_steps.on(pool)
                pool.memset(padd[:], 4095)
                pool.memset(pads[:], 0).then_inc(const_ready, 1)
                pool.memset(XN[:, :, D:D + 1], 1.0)
                pool.memset(xns[:, :, D:D + 1], 1.0)
                pool.memset(ones[:], 1.0)
                pool.memset(zrow[:], 0.0)
                pool.memset(zwide[:], 0.0)
                c(pool.memset(ident[:], 0.0))
                c(pool.affine_select(out=ident[:], in_=ident[:], compare_op=ALU.not_equal, fill=1.0, base=0,
                                     pattern=[[-1, P]], channel_multiplier=1))
                kw = dict(allow_small_or_imprecise_dtypes=True)
                pool.iota(iota_p[:], pattern=[[0, 1]], base=0, channel_multiplier=1, **kw)
                pool.iota(iota_f[:], pattern=[[1, P]], base=0, channel_multiplier=0, **kw)
                pool.iota(thr[:], pattern=[[0, 1]], base=R, channel_multiplier=R, **kw)
                pool.iota(iotc[:], pattern=[[1, CH - 1]], base=1, channel_multiplier=0, **kw)
                c(pool.iota(stepid[:], pattern=[[P, SB]], base=0, channel_multiplier=1, **kw))
                pool.engine_nop().then_inc(const_ready, 1)
                def keep_tile(t, par):
                    pool.wait_ge(xns_full, done(t))
                    pool.tensor_copy(row(XN, t)[:, 0:D], xns[:, par, 0:D]).then_inc(xns_kept, 1)

                pool.sem_inc(xns_kept, 2)
                over_tiles(pool, keep_tile)
                pool.wait_ge(ci_ready, 1)
                pool.wait_ge(er_ready, 16 * 8)
                for b in range(SB):
                    pool.indirect_dma_start(out=er[:, b, :], out_offset=None, in_=er_dram,
                                            in_offset=bass.IndirectOffsetOnAxis(ap=cii[:, b:b + 1], axis=0)).then_inc(er_rows, 16)
                pool.wait_ge(er_rows, 16 * SB)

            @block.tensor
            def _(pe):
                pe.sem_inc(xt_full, 2)
                pe.sem_inc(u_full, 2)
                pe.wait_ge(const_ready, 2)
                pe.wait_ge(w_in, 80)
                for o in range(DT):
                    for k in range(DT):
                        last = pe.transpose(bank[0][:, (o * DT + k) * P:(o * DT + k + 1) * P], Wn[:, o, k * P:(k + 1) * P], ident[:])
                last.then_inc(pre_psum, 1)
                pe.wait_ge(hb2, 1)
                for o in range(DT):
                    last = pe.matmul(bank[1][:, 0:1], ones[:], bsq[:, o:o + 1], start=(o == 0), stop=(o == DT - 1))
                last.then_inc(pre_psum, 1)
                pe.wait_ge(hb2, 2)
                for k in range(DT):
                    for o in range(DT):
                        last = pe.matmul(bank[1][:, 8 + k:9 + k], Wn[:, o, k * P:(k + 1) * P], hbcol[:, o:o + 1], start=(o == 0), stop=(o == DT - 1))
                last.then_inc(pre_psum, 1)
                pe.wait_ge(cf_used, 1)
                pe.matmul(bank[2][0:T - 1, 0:CH - 1], ones[0:1, 0:T - 1], firstf[:], start=True, stop=True).then_inc(cf_psum, 1)
                pe.wait_ge(cf_used, 2)
                pe.matmul(bank[3][:, 0:CH - 1], ones[0:T - 1, :], ge[:], start=True, stop=True).then_inc(cf_psum, 1)
                pe.wait_ge(cf_used, 3)
                for b in range(SB):
                    last = pe.transpose(bank[2][0:1, b * P:(b + 1) * P], tf[:, b:b + 1], ident[:])
                last.then_inc(cf_psum, 1)
                pe.wait_ge(pre_used, 3)

                def turn(t, par):
                    pe.wait_ge(xns_full, done(t))
                    pe.matmul(bank[7][:, 0:D + 1], ones[0:R, :], xns[:, par, :], start=False, stop=False,
                              skip_group_check=True)
                    pe.wait_ge(xts_full, done(t - 2))
                    for k in range(DT):
                        last = pe.transpose(bank[4 + 2 * par][:, k * P:k * P + R], xns[:, par, k * P:(k + 1) * P], ident[0:R, 0:R])
                    last.then_inc(xt_full, 1)

                def node_tile(t, par):
                    if before(t, T - 1):
                        turn(t + 1, 1 - par)
                    pe.wait_ge(xts_full, done(t))
                    pe.wait_ge(u_kept, done(t - 2))
                    for k in range(DT):
                        last = pe.matmul(bank[5 - 2 * par][0:R, 0:D + 1], xts[:, par, k, :], WT[:, k, :], start=(k == 0), stop=(k == DT - 1))
                    last.then_inc(u_full, 1)

                pe.matmul(bank[7][:, 0:D + 1], zrow[:], zwide[:], start=True, stop=False, skip_group_check=True)
                turn(0, 0)
                over_tiles(pe, node_tile)
                pe.matmul(bank[7][:, 0:D + 1], zrow[:], zwide[:], start=False, stop=True, skip_group_check=True).then_inc(cs_full, 1)

                pe.wait_ge(rel_ready, 2)
                for b in range(SB):
                    w = min(P, STEPS - b * P)
                    pe.transpose(bank[0][:, b * P:b * P + w], rel[0:w, b, :], ident[0:w, 0:w])
                    last = pe.transpose(bank[1][:, b * P:b * P + w], erf[0:w, b, 1 + P:], ident[0:w, 0:w])
                last.then_inc(eT_psum, 1)

            @block.scalar
            def _(act):
                act.sem_inc(xts_full, 2)
                act.sem_inc(sq_done, 2)
                act.sem_inc(hbs_full, 2)
                act.wait_ge(w_in, 80)
                act.activation(bsq[:], bcol[:], ACT.Square).then_inc(hb2, 1)
                act.wait_ge(sc_v, 1)
                act.activation(ns["std"][:], ns["t1"][:], ACT.Sqrt)
                act.activation(ns["n0"][:], ns["var"][:], ACT.Sqrt).then_inc(sc_a, 1)
                act.wait_ge(sc_v, 2)
                act.activation(hs[:, 1:2], hs[:, 0:1], ACT.Sqrt).then_inc(sc_a, 1)
                act.wait_ge(sc_v, 3)
                act.activation(hs[:, 3:4], hs[:, 2:3], ACT.Tanh).then_inc(sc_a, 1)
                act.wait_ge(sc_v, 4)
                act.activation(ns["lp"][:], ns["p"][:], ACT.Ln)
                act.activation(ns["lq"][:], ns["q"][:], ACT.Ln).then_inc(sc_a, 1)

                def turned(t, par):
                    act.wait_ge(xt_full, done(t))
                    act.wait_ge(u_full, done(t - 2))
                    act.wait_ge(xts_kept, done(t - 2))
                    act.activation(xts[:, par, :, :], bank[4 + 2 * par][:, 0:D].rearrange("p (k r) -> p k r", k=DT)[:, :, 0:R], ACT.Copy).then_inc(xts_full, 1)

                def node_tile(t, par):
                    if before(t, T - 1):
                        turned(t + 1, 1 - par)
                    act.wait_ge(u_kept, done(t))
                    act.activation(junk[:, par, :], row(ACC, t), ACT.Square, accum_out=col("usq", t)).then_inc(sq_done, 1)
                turned(0, 0)
                over_tiles(act, node_tile)
                act.wait_ge(sc_v, 5)
                act.activation(ns["nu"][:], ns["t0"][:], ACT.Sqrt).then_inc(sc_a, 1)
                act.wait_ge(sc_v, 6)
                act.activation(ns["th"][:], ns["t1"][:], ACT.Tanh).then_inc(sc_a, 1)
                act.wait_ge(sc_v, 7)
                act.activation(ns["nv"][:], ns["nv2"][:], ACT.Sqrt).then_inc(sc_a, 1)
                act.wait_ge(sc_v, 8)
                act.activation(ns["lp"][:], ns["p"][:], ACT.Ln)
                act.activation(ns["lq"][:], ns["q"][:], ACT.Ln).then_inc(sc_a, 1)
                act.wait_ge(sc_v, 9)

                def hb_tile(t, par):
                    act.wait_ge(lx_done, done(t - 2))
                    act.activation(hbs[:, par, :], hbrow[:], ACT.Copy, scale=col("a2", t)).then_inc(hbs_full, 1)
                over_tiles(act, hb_tile)

            @block.vector
            def _(v):
                c = dve_steps.on(v)

                def stats(t, par):
                    v.bn_stats(row(st6, t), row(X, t)).then_inc(stat_n, 1)
                v.wait_ge(x_in, 80)
                over_tiles(v, stats)
                v.wait_ge(stat_n, T)
                s = [st6[:, :, k] for k in range(6)]
                n = {k: b[:] for k, b in ns.items()}
                c(v.tensor_tensor(n["mean"], s[1], s[4], ALU.add))
                c(v.tensor_scalar(n["mean"], n["mean"], 0.5, None, ALU.mult))
                c(v.tensor_tensor(n["dm"], s[1], s[4], ALU.subtract))
                c(v.tensor_tensor(n["dm"], n["dm"], n["dm"], ALU.mult))
                c(v.tensor_tensor(n["var"], s[2], s[5], ALU.add))
                c(v.tensor_scalar(n["var"], n["var"], 1.0 / D, None, ALU.mult))
                c(v.scalar_tensor_tensor(out=n["var"], in0=n["dm"], scalar=0.25, in1=n["var"], op0=ALU.mult, op1=ALU.add))
                v.tensor_scalar(n["t1"], n["var"], 1e-5, None, ALU.add).then_inc(sc_v, 1)
                v.wait_ge(sc_a, 1)
                c(v.reciprocal(n["rstd"], n["std"]))

                v.wait_ge(pre_psum, 2)
                v.tensor_copy(hs[:, 0:1], bank[1][:, 0:1]).then_inc(sc_v, 1)
                v.wait_ge(sc_a, 2)
                v.tensor_scalar(hs[:, 2:3], hs[:, 1:2], MIN_NORM, None, ALU.max).then_inc(sc_v, 1)
                v.wait_ge(sc_a, 3)
                c(v.tensor_scalar(hs[:, 3:4], hs[:, 3:4], MAXN, None, ALU.min))
                c(v.tensor_tensor(hs[:, 5:6], hs[:, 3:4], hs[:, 3:4], ALU.mult))
                c(v.reciprocal(hs[:, 4:5], hs[:, 2:3]))
                c(v.tensor_tensor(hs[:, 6:7], hs[:, 3:4], hs[:, 4:5], ALU.mult))
                c(v.tensor_scalar(hbrow[:], hbrow[:], hs[0:R, 6:7], None, ALU.mult))
                v.tensor_scalar(hbcol[:], bcol[:], hs[:, 6:7], None, ALU.mult).then_inc(hb2, 1)
                v.wait_ge(pre_psum, 3)
                for o in range(DT):
                    for k in range(DT):
                        v.tensor_copy(WT[:, k, o * P:(o + 1) * P], bank[0][:, (o * DT + k) * P:(o * DT + k + 1) * P]).then_inc(pre_used, 1)
                v.tensor_copy(WT[:, :, D:D + 1], bank[1][:, 8:8 + DT]).then_inc(pre_used, 1)

                def atanh(norm, extra):
                    c(v.tensor_scalar(n["p"], norm, 1.0, None, ALU.add))
                    v.tensor_scalar(n["q"], norm, -1.0, 1.0, ALU.mult, ALU.add).then_inc(sc_v, 1)
                    c(v.tensor_tensor(n["t0"], norm, norm, ALU.mult))
                    c(v.tensor_scalar(n["ser"], n["t0"], 1.0 / 7, 1.0 / 5, ALU.mult, ALU.add))
                    c(v.tensor_tensor(n["ser"], n["ser"], n["t0"], ALU.mult))
                    c(v.tensor_scalar(n["ser"], n["ser"], 1.0 / 3, None, ALU.add))
                    c(v.tensor_tensor(n["ser"], n["ser"], n["t0"], ALU.mult))
                    c(v.scalar_tensor_tensor(out=n["ser"], in0=n["ser"], scalar=1.0, in1=norm, op0=ALU.add, op1=ALU.mult))
                    c(v.tensor_scalar(n["msk"], norm, 0.1, None, ALU.is_lt))
                    v.wait_ge(sc_a, extra)
                    c(v.tensor_tensor(n["at"], n["lp"], n["lq"], ALU.subtract))
                    c(v.tensor_scalar(n["at"], n["at"], 0.5, None, ALU.mult))
                    c(v.tensor_tensor(n["ser"], n["ser"], n["at"], ALU.subtract))
                    c(v.tensor_tensor(n["ser"], n["ser"], n["msk"], ALU.mult))
                    c(v.tensor_tensor(n["at"], n["at"], n["ser"], ALU.add))

                c(v.scalar_tensor_tensor(out=n["n0"], in0=n["n0"], scalar=float(D) ** 0.5, in1=n["rstd"], op0=ALU.mult, op1=ALU.mult))
                c(v.tensor_scalar(n["n0"], n["n0"], MIN_NORM, None, ALU.max))
                c(v.tensor_scalar(n["nc"], n["n0"], ATANH_MAX, None, ALU.min))
                atanh(n["nc"], 4)
                c(v.reciprocal(n["t0"], n["n0"]))
                c(v.tensor_tensor(n["s1"], n["at"], n["t0"], ALU.mult))

                v.wait_ge(e_in, 16)
                v.wait_ge(const_ready, 2)
                v.tensor_copy(firstf[:], firsts[:]).then_inc(cf_used, 1)
                v.wait_ge(cf_psum, 1)
                v.tensor_scalar(ge[:], bank[2][0:T - 1, 0:CH - 1], thr[:], None, ALU.is_ge).then_inc(cf_used, 1)
                v.wait_ge(cf_psum, 2)
                c(v.tensor_tensor(AC[:], bank[3][:, 0:CH - 1], iotc[:], ALU.add))
                for b in range(SB):
                    c(v.tensor_scalar(ejunk[:], AC[:], stepid[:, b:b + 1], 0.0, ALU.is_le, ALU.add, accum_out=cif[:, b:b + 1]))
                c(v.tensor_tensor(tf[:], stepid[:], cif[:], ALU.subtract))
                c(v.tensor_scalar(t125[:], tf[:], float(R), None, ALU.mult))
                v.tensor_copy(cii[:], cif[:]).then_inc(ci_ready, 1)
                c(v.tensor_scalar(tf[:], tf[:], 0.0, float(T - 1), ALU.max, ALU.min))
                v.sem_inc(cf_used, 1)
                v.wait_ge(cf_psum, 3)
                c(v.tensor_copy(tI[:], bank[2][0:1, 0:STEPS]))

                def norm_tile(t, par):
                    v.wait_ge(xt_full, done(t - 2))
                    v.wait_ge(xns_kept, done(t - 2))
                    v.tensor_scalar(xns[:, par, 0:D], row(X, t), col("mean", t), col("rstd", t), ALU.subtract, ALU.mult).then_inc(xns_full, 1)

                v.sem_inc(u_kept, 2)
                v.sem_inc(xns_full, 2)
                v.sem_inc(xts_kept, 2)
                norm_tile(0, 0)
                norm_tile(1, 1)

                def node_tile(t, par):
                    if before(t, T - 2):
                        norm_tile(t + 2, par)
                    v.wait_ge(xts_full, done(t))
                    v.tensor_copy(XNT[:, :, bass.ds(t * R, R)], xts[:, par]).then_inc(xts_kept, 1)
                    v.wait_ge(u_full, done(t))
                    v.tensor_copy(row(ACC, t), bank[5 - 2 * par][0:R, 0:D])
                    v.tensor_copy(col("uh", t), bank[5 - 2 * par][0:R, D:D + 1]).then_inc(u_kept, 1)
                over_tiles(v, node_tile)
                v.wait_ge(cs_full, 1)
                c(v.tensor_scalar(CSE[:], bank[7][:, 0:D + 1], EPS_ATT, None, ALU.mult))

                v.wait_ge(u_kept, done(T - 1))
                v.wait_ge(sq_done, done(T - 1))
                v.tensor_scalar(n["t0"], n["usq"], 0.0, None, ALU.max).then_inc(sc_v, 1)
                v.wait_ge(sc_a, 5)
                c(v.tensor_tensor(n["nu"], n["nu"], n["s1"], ALU.mult))
                v.tensor_scalar(n["t1"], n["nu"], MIN_NORM, None, ALU.max).then_inc(sc_v, 1)
                v.wait_ge(sc_v, 6)
                c(v.reciprocal(n["f1"], n["t1"]))
                c(v.tensor_tensor(n["f1"], n["f1"], n["s1"], ALU.mult))
                v.wait_ge(sc_a, 6)
                c(v.tensor_scalar(n["th"], n["th"], MAXN, None, ALU.min))
                c(v.tensor_tensor(n["f1"], n["f1"], n["th"], ALU.mult))
                c(v.tensor_tensor(n["x2"], n["th"], n["th"], ALU.mult))
                c(v.tensor_tensor(n["xy"], n["uh"], n["f1"], ALU.mult))
                y2 = hs[0:R, 5:6]
                c(v.tensor_scalar(n["A"], n["xy"], 2.0, 1.0, ALU.mult, ALU.add))
                c(v.scalar_tensor_tensor(out=n["den"], in0=n["x2"], scalar=y2, in1=n["A"], op0=ALU.mult, op1=ALU.add))
                c(v.tensor_scalar(n["A"], n["A"], y2, None, ALU.add))
                c(v.tensor_scalar(n["B"], n["x2"], -1.0, 1.0, ALU.mult, ALU.add))
                c(v.tensor_scalar(n["den"], n["den"], MIN_NORM, None, ALU.max))
                c(v.reciprocal(n["den"], n["den"]))
                c(v.tensor_tensor(n["P"], n["A"], n["f1"], ALU.mult))
                c(v.tensor_tensor(n["P"], n["P"], n["den"], ALU.mult))
                c(v.tensor_tensor(n["Q"], n["B"], n["den"], ALU.mult))
                c(v.tensor_tensor(n["t0"], n["P"], n["usq"], ALU.mult))
                c(v.scalar_tensor_tensor(out=n["t1"], in0=n["Q"], scalar=2.0, in1=n["uh"], op0=ALU.mult, op1=ALU.mult))
                c(v.tensor_tensor(n["t0"], n["t0"], n["t1"], ALU.add))
                c(v.tensor_tensor(n["t0"], n["t0"], n["P"], ALU.mult))
                c(v.tensor_tensor(n["t1"], n["Q"], n["Q"], ALU.mult))
                c(v.scalar_tensor_tensor(out=n["t0"], in0=n["t1"], scalar=y2, in1=n["t0"], op0=ALU.mult, op1=ALU.add))
                v.tensor_scalar(n["nv2"], n["t0"], 0.0, None, ALU.max).then_inc(sc_v, 1)
                v.wait_ge(sc_a, 7)
                c(v.tensor_scalar(n["nv"], n["nv"], MIN_NORM, None, ALU.max))
                c(v.tensor_scalar(n["nc"], n["nv"], MAXN, ATANH_MAX, ALU.min, ALU.min))
                atanh(n["nc"], 8)
                c(v.reciprocal(n["t0"], n["nv"]))
                c(v.tensor_tensor(n["g"], n["at"], n["t0"], ALU.mult))
                c(v.tensor_tensor(n["a1"], n["g"], n["P"], ALU.mult))
                v.tensor_tensor(n["a2"], n["g"], n["Q"], ALU.mult).then_inc(sc_v, 1)
                v.sem_inc(lx_done, 2)

                def lx_tile(t, par):
                    v.wait_ge(hbs_full, done(t))
                    v.scalar_tensor_tensor(out=row(ACC, t), in0=row(ACC, t), scalar=col("a1", t), in1=hbs[:, par, :],
                                           op0=ALU.mult, op1=ALU.add).then_inc(lx_done, 1)
                over_tiles(v, lx_tile)

                v.wait_ge(er_rows, 16 * SB)
                c(v.tensor_copy(erf[:], er[:]))
                de = erf[:, :, 1:1 + P]
                for b in range(SB):
                    c(v.tensor_scalar(rel[:, b, :], de[:, b, :], t125[:, b:b + 1], -1.0, ALU.subtract, ALU.max))
                c(v.tensor_scalar(rel[:], rel[:], float(R), None, ALU.min))
                c(v.tensor_copy(relb[:], rel[:]))
                c(v.tensor_tensor(m1[:], de, erf[:, :, 0:P], ALU.not_equal))
                c(v.tensor_scalar(PEN, rel[:], 0.0, None, ALU.is_ge))
                c(v.scalar_tensor_tensor(out=PEN, in0=rel[:], scalar=float(R) - 0.5, in1=PEN, op0=ALU.is_lt, op1=ALU.mult))
                c(v.scalar_tensor_tensor(out=D0, in0=m1[:], scalar=-BIG, in1=PEN, op0=ALU.mult, op1=ALU.mult))
                c(v.tensor_scalar(PEN, PEN, -1.0, BIG, ALU.add, ALU.mult))
                v.sem_inc(rel_ready, 2)
                v.wait_ge(eT_psum, 1)
                c(v.tensor_copy(relT[:], bank[0][:, 0:STEPS]))
                c(v.tensor_copy(idxT[:], bank[1][:, 0:STEPS]))

                for k in range(5):
                    v.wait_ge(lx_out[k], 16)
                for h in range(GH):
                    v.wait_ge(nt_in[h], 16)
                    if h > 1:
                        v.wait_ge(sij_ready, h - 1)
                    for s_ in range(2):
                        last = v.tensor_tensor(prod[:, h % 2, s_], NT[:, :, h, :], attr[:, s_, h, :].unsqueeze(1).to_broadcast([R, T, DH]), ALU.mult)
                    c(last)
                    v.tensor_reduce(SIJ[:].rearrange("r t (s h) -> r h s t", s=2)[:, h], prod[:, h % 2], AX.X, ALU.add).then_inc(sij_ready, 1)

        wk_in = sem("wk_in"); wq_in = sem("wq_in"); wv_in = sem("wv_in"); wp_in = sem("wp_in"); set_pe = sem("set_pe"); set_v = sem("set_v"); set_a = sem("set_a")
        fin_v = sem("fin_v"); fin_pe = sem("fin_pe")
        xtm_full = sem("xtm_full"); pj_full = sem("pj_full"); pj_used = sem("pj_used"); nsq_full = sem("nsq_full")
        u2_full = sem("u2_full"); e_full = sem("e_full"); e_used = sem("e_used")
        xh_full = sem("xh_full"); eh_full = sem("eh_full"); el_full = sem("el_full"); ph_full = sem("ph_full"); pl_full = sem("pl_full")
        phi_full = sem("phi_full"); att_full = sem("att_full"); rz_full = sem("rz_full"); acc_half = sem("acc_half")
        att_used = sem("att_used")
        oht_done = sem("oht_done"); sd_full = sem("sd_full"); sd_kept = sem("sd_kept"); r_full = sem("r_full")
        c_in = sem("c_in"); p_ready = sem("p_ready"); rb_in = sem("rb_in"); stg = sem("stg"); sj_in = [sem("sj_in0"), sem("sj_in1")]
        sj_kept = sem("sj_kept"); stg_seen = sem("stg_seen"); g_in = [sem("g_in0"), sem("g_in1")]; o_full = sem("o_full"); o_used = sem("o_used")
       
        w_hi = sem("w_hi"); k_split = sem("k_split"); w_split = sem("w_split"); xtl_full = sem("xtl_full")
        HB = T + 1
        HALVES = STEPS // 4
        flat = GACC[:, :, :].rearrange("p t c -> p (t c)")
        SJ = flat[:, 0:SB * P * GH].rearrange("p (s h) -> p s h", h=GH)
        SD = flat[:, SB * P * GH:3 * SB * P * GH].rearrange("p (s h) -> p s h", h=2 * GH)
        projT = sb("projT", [P, DT, D])
        zr = sb("zr", [1, P]); zw = sb("zw", [1, D + 2])

        def row(buf, t):
            return buf[:, bass.ds(t, 1), :].rearrange("r a c -> r (a c)")

        def steps_tiles(eng_type, u):
            _, regs = nc.values_load_multi_w_load_instructions(tI[0:1, bass.ds(4 * u, 4)], engines=[eng_type],
                                                               min_val=0, max_val=T - 1)
            return regs

        def mixer_block(first):
            ctx = ExitStack()
            with ctx:
                n_ = "A" if first else "B"
                mk = lambda name, shape, dt=F32: sb(name + n_, shape, dt, ctx=ctx)
                S0, S1 = mk("S0", [P, DT, PW]), mk("S1", [P, DT, PW])
                WS = {"k": S0, "q": S1, "v": S0}
                WH, WL, MH_, ML = (mk(k, [P, DT, PW]) for k in ("WH", "WL", "MH", "ML"))
                WoS = mk("WoS", [P, 4, D])
                WTs = {k: mk(f"W{k}T", [P, 4, D]) for k in "kqv"}
                WVO = WoS
                KVX = mk("KVX", [P, 4, D + 1])
                KVXT = WTs["k"]
                KVO = mk("KVO", [P, 4, D + 1])
                bc = mk("bc", [P, 3, 16])
                bcp = mk("bcp", [P, 3, 4])
                brow = KVX[0:1, :, :].rearrange("p b c -> p (b c)")[:, 0:2 * PW].rearrange("p (i k) -> p i k", i=2)
                kvo_flat = KVO[:].rearrange("p b c -> p (b c)")
                BVB = kvo_flat[:, 0:PW].rearrange("p (c k) -> p c k", c=4)
                rr = kvo_flat[0:1, PW:2 * PW]
                mid = mk("mid", [1, PW], BF16)
                b3 = {k: mk(f"b3{k}", [65, PW], BF16) for k in ("k", "q", "ck", "cq")}
                ones3 = mk("ones3", [65, R], BF16)
                spare = WTs["v"][:].rearrange("p c d -> p (c d)")
                BVWO = spare[:, 0:PW]
                xtm, xtl = mk("xtm", [P, 2, DT, R]), mk("xtl", [P, 2, DT, R])
                PT = spare[:, 2 * D:2 * D + 4 * R].rearrange("p (b r) -> p b r", b=4)
                EB = WTs["q"][0:R].rearrange("p c d -> p (c d)").rearrange("p (a k) -> p a k", a=2)
                sq = mk("sq", [R, 2, 2])
                nsq = mk("nsq", [R, 2, 2])
                rz = mk("rz", [R, 2])
                sidx = mk("sidx", [P, 2, 4], I32)
                if first:
                    pn = spare[:, PW:2 * PW].rearrange("p (o k) -> p o k", o=DT)
                    RB = mk("RB", [R, 4 * P], BF16)
                    OHT = mk("OHT", [R, 4 * P], BF16)
                    EBH, EBL = mk("EBH", [R, 2, PW]), mk("EBL", [R, 2, PW])
                    XH, XL = mk("XH", [R, 2, D + 2]), mk("XL", [R, 2, D + 2])
                    PTH, PTL = mk("PTH", [P, 4, R]), mk("PTL", [P, 4, R])
                    KVH, KVL = mk("KVH", [P, 4, D + 2]), mk("KVL", [P, 4, D + 2])
                    SIJ3 = mk("SIJ3", [R, T, 3, 2 * GH], BF16)
                    rest = kvo_flat[0:R, 0:T * 2 * GH].rearrange("r (t c) -> r t c", t=T)
                    sjst = mk("sjst", [P, 2, 4, GH])
                else:
                    G = [mk(f"G{i}", [P, 4, D]) for i in range(2)]
                    RS = mk("RS", [P, 2, 4, 265])
                    OH = PD[:].rearrange("p a b e -> p (a b e)")[:, 0:8 * R].rearrange("p (a k r) -> p a k r", a=2, k=4)
                g0 = 0 if first else 2
                block = ctx.enter_context(nc.Block())

                def loops(g, ph, tile):
                    B0, Q0, u0 = (2 * g + ph) * T, g * T, (2 * (g - g0) + ph) * HB
                    tile(0, 0, B0, Q0, u0)
                    with_loop = lambda i, k: tile(2 * i + k, k % 2, B0 + 2 * i + k, Q0 + 2 * i + k, u0 + 2 * i + k)
                    return B0, with_loop, (T, 1, B0 + T, Q0 + T, u0 + T)

                def run(eng, g, ph, tile, peeled=0):
                    _, inner, last = loops(g, ph, tile)
                    with eng.Fori(0, T // 2 - peeled) as i:
                        inner(i, 1)
                        inner(i, 2)
                    for i in range(T // 2 - peeled, T // 2):
                        inner(i, 1)
                        inner(i, 2)
                    tile(*last)

                zero = lambda t: isinstance(t, int) and t == 0
                last_ = lambda t: isinstance(t, int) and t == T
                SV, SA, SPE = 6, 2, 8

                @block.sync
                def _(sp):
                    if first:
                        sp.dma_start(pn, proj.rearrange("(o p) k -> p o k", p=P)).then_inc(c_in, 16)
                    with nc.allow_non_contiguous_dma("bias columns"):
                        for i_, b_ in enumerate((bk, bq, bv)):
                            sp.dma_start(bc[:, i_, :], b_.rearrange("h k -> (h k)").rearrange("(c p) -> p c", p=P)).then_inc(c_in, 16)
                    head_cols = lambda w_, g: w_.rearrange("(o p) h k -> p o (h k)", p=P)[:, :, PW * g:PW * (g + 1)]

                    def targets(u0, count):
                        with sp.Fori(0, count) as i:
                            u = u0 + i
                            sp.wait_ge(oht_done, done(u - 1))
                            sp.dma_start(RB[:], bass.AP(rel_dram.tensor, u * 4 * P, [[0, R], [1, 4 * P]])).then_inc(rb_in, 16)

                    def weights(g):
                        sp.dma_start(WS["k"][:], head_cols(Wk, g)).then_inc(wk_in, 16)
                        sp.dma_start(WS["q"][:], head_cols(Wq, g)).then_inc(wq_in, 16)
                        for i_, b_ in enumerate((bk, bq)):
                            sp.dma_start(brow[:, i_, :], b_.rearrange("h k -> (h k)")[PW * g:PW * (g + 1)].rearrange("(a k) -> a k", a=1)).then_inc(wp_in, 16)
                        sp.dma_start(WoS[:], Wo.rearrange("h k d -> (h k) d").rearrange("(c p) d -> p c d", p=P)[:, 4 * g:4 * g + 4, :]).then_inc(wp_in, 16)

                    weights(g0)
                    if first:
                        targets(0, 1)
                    for g in (g0, g0 + 1):
                        sp.wait_ge(set_pe, SPE * g + 1)
                        sp.wait_ge(k_split, g + 1)
                        sp.dma_start(WS["v"][:], head_cols(Wv, g)).then_inc(wv_in, 16)
                        if first:
                            targets(2 * HB * (g - g0) + 1, HB)
                        if g == g0:
                            sp.wait_ge(w_split, g + 1)
                            sp.wait_ge(fin_v, 1 + 3 * (g + 1))
                            weights(g + 1)
                        if first:
                            targets(2 * HB * (g - g0) + HB + 1, HB if g == g0 else HB - 1)

                @block.gpsimd
                def _(pool):
                    if first:
                        pool.memset(zr[:], 0.0)
                        pool.memset(zw[:], 0.0).then_inc(p_ready, 1)
                        pool.sem_inc(sj_kept, 2)
                        pool.memset(ACC[:], 0.0).then_inc(p_ready, 1)
                    else:
                        pool.memset(GACC[:], 0.0).then_inc(p_ready, 1)
                    if first:
                        pool.memset(SJ[:, STEPS:, :], 0.0)
                        pool.memset(SD[:, STEPS:, :], 0.0)

                        def fetch(u, par):
                            pool.tensor_copy(sidx[:, par, :], idxT[:, bass.ds(4 * u, 4)]).then_inc(stg, 1)
                            pool.wait_ge(stg, u + 1)
                            if not (isinstance(u, int) and u < 2):
                                pool.wait_ge(sj_kept, done(u - 2))
                            pool.sem_inc(stg_seen, 1)
                            for k in range(4):
                                pool.indirect_dma_start(out=sjst[:, par, k, :], out_offset=None, in_=sj_dram,
                                                        in_offset=bass.IndirectOffsetOnAxis(ap=sidx[:, par, k:k + 1], axis=0)).then_inc(sj_in[par], 16)

                        def keep(u, par, n):
                            pool.wait_ge(sj_in[par], 64 * n)
                            pool.tensor_copy(SJ[:, bass.ds(4 * u, 4), :], sjst[:, par]).then_inc(sj_kept, 1)

                        fetch(0, 0)
                        with pool.Fori(0, HALVES // 2 - 1) as j:
                            fetch(2 * j + 1, 1)
                            keep(2 * j, 0, j + 1)
                            fetch(2 * j + 2, 0)
                            keep(2 * j + 1, 1, j + 1)
                        fetch(HALVES - 1, 1)
                        keep(HALVES - 2, 0, HALVES // 2)
                        keep(HALVES - 1, 1, HALVES // 2)
                    else:
                        def fetch(u, par):
                            pool.wait_ge(r_full, done(u - 2))
                            pool.tensor_copy(sidx[:, par, :], idxT[:, bass.ds(4 * u, 4)]).then_inc(stg, 1)
                            pool.wait_ge(stg, HALVES + u + 1)
                            pool.sem_inc(stg_seen, 1)
                            for k in range(4):
                                pool.indirect_dma_start(out=G[par][:, k, :], out_offset=None, in_=ft_dram,
                                                        in_offset=bass.IndirectOffsetOnAxis(ap=sidx[:, par, k:k + 1], axis=0)).then_inc(g_in[par], 16)

                        with pool.Fori(0, HALVES // 2) as j:
                            fetch(2 * j, 0)
                            fetch(2 * j + 1, 1)

                @block.tensor
                def _(pe):
                    if first:
                        pe.wait_ge(p_ready, 1)
                        pe.sem_inc(pj_full, 2); pe.sem_inc(u2_full, 2); pe.sem_inc(e_used, 2)
                        pe.sem_inc(att_full, 2); pe.sem_inc(sd_full, 2)
                        pe.wait_ge(c_in, 64)
                        for o in range(DT):
                            for k in range(DT):
                                last = pe.transpose(bank[5][:, k * D + o * P:k * D + (o + 1) * P], pn[:, o, k * P:(k + 1) * P], ident[:])
                        last.then_inc(fin_pe, 1)
                        pe.wait_ge(fin_v, 1)

                    def setup(g):
                        pe.wait_ge(pj_used, done(2 * g * T - 1))
                        pe.wait_ge(e_full, done(2 * g * T - 1))
                        pe.wait_ge(att_used, done(g * T - 1))

                        def turn(k, to, loaded):
                            pe.wait_ge(loaded, 16 * (g + 1))
                            for h in range(2):
                                for c_ in range(2):
                                    for o in range(DT):
                                        last = pe.transpose(bank[to + h][:, c_ * D + o * P:c_ * D + (o + 1) * P],
                                                            WS[k][:, o, h * D + c_ * P:h * D + (c_ + 1) * P], ident[:])
                            last.then_inc(set_pe, 1)
                        turn("k", 0, wk_in)
                        turn("q", 2, wq_in)
                        pe.wait_ge(set_v, SV * g + 1)
                        for i_ in range(2):
                            for h in range(2):
                                for c_ in range(2):
                                    last = pe.matmul(bank[4 + i_][0:1, h * D:(h + 1) * D], bcp[:, i_, 2 * h + c_:2 * h + c_ + 1], projT[:, c_, :],
                                                     start=(c_ == 0), stop=(c_ == 1))
                        last.then_inc(set_pe, 1)
                        for i_, (k, s_, n) in enumerate((("k", set_v, SV * g + 2), ("q", set_a, SA * g + 1))):
                            pe.wait_ge(s_, n)
                            for o in range(DT):
                                for h in range(2):
                                    for c_ in range(2):
                                        last = pe.matmul(bank[2 * i_ + o][:, h * D:(h + 1) * D], WTs[k][:, 2 * h + c_, o * P:(o + 1) * P],
                                                         projT[:, c_, :], start=(c_ == 0), stop=(c_ == 1))
                            last.then_inc(set_pe, 1)
                        pe.wait_ge(set_v, SV * g + 3)
                        turn("v", 4, wv_in)
                        pe.wait_ge(wp_in, 48 * (g + 1))
                        pe.wait_ge(set_v, SV * g + 4)
                        for h in range(2):
                            for c_ in range(2):
                                last = pe.matmul(bank[0][:, h * D:(h + 1) * D], BVB[:, 2 * h + c_, :], WoS[:, 2 * h + c_, :], start=(c_ == 0), stop=(c_ == 1))
                        last.then_inc(set_pe, 1)
                        pe.wait_ge(set_v, SV * g + 5)
                        pe.wait_ge(set_a, SA * g + 2)
                        for h in range(2):
                            for o in range(DT):
                                for c_ in range(2):
                                    last = pe.matmul(bank[2 + h][:, o * D:(o + 1) * D], WTs["v"][:, 2 * h + c_, o * P:(o + 1) * P],
                                                     WoS[:, 2 * h + c_, :], start=(c_ == 0), stop=(c_ == 1))
                        last.then_inc(set_pe, 1)
                        pe.wait_ge(set_v, SV * g + 6)

                    def finish_keys(g):
                        pe.wait_ge(fin_v, 1 + 3 * g + 1)
                        for h in range(2):
                            for mb in range(2):
                                for o in range(DT):
                                    last = pe.transpose(bank[h][:, o * D + mb * P:o * D + (mb + 1) * P], KVX[:, 2 * h + mb, o * P:(o + 1) * P], ident[:])
                        last.then_inc(fin_pe, 1)
                        pe.wait_ge(fin_v, 1 + 3 * g + 2)
                        for h in range(2):
                            for mb in range(2):
                                for o in range(DT):
                                    last = pe.matmul(bank[2 + 2 * h + mb][:, 0:D], KVXT[:, 2 * h + o, mb * P:(mb + 1) * P], WVO[:, 2 * h + o, :],
                                                     start=(o == 0), stop=(o == DT - 1))
                        last.then_inc(fin_pe, 1)
                        pe.wait_ge(fin_v, 1 + 3 * g + 3)

                    def edges(u, k0, k1, regs):
                        for k in range(k0, k1):
                            if first:
                                last = pe.matmul(bank[6][:, 24 * k:24 * (k + 1)], OHT[:, k * P:(k + 1) * P],
                                                 SIJ3[:, bass.ds(regs[k], 1)].rearrange("r a s c -> r (a s c)"), start=True, stop=True)
                                if k == 3:
                                    last.then_inc(sd_full, 1)
                            else:
                                par, n = edges.par, 4 * u + k
                                pe.wait_ge(o_used, done(n - 2))
                                pe.matmul(bank[6 + k % 2][0:R, 0:265], OH[:, par, k, :], RS[:, par, k, :], start=True, stop=True).then_inc(o_full, 1)

                    def products(to, par, B, high, low):
                        for n, (x_, w_) in enumerate(((xtm, high), (xtm, low), (xtl, high))):
                            if n == 2:
                                pe.wait_ge(xtl_full, done(B))
                            for k in range(DT):
                                pe.matmul(to[0:R, :], one_pass(x_[:, par, k, :]), one_pass(w_[:, k, :]), start=(n + k == 0), stop=False)

                    def make(ph, g):
                        kq = "kq"[ph]

                        def tile(t, par, B, Q, u):
                            regs = steps_tiles(mybir.EngineType.PE, u) if first else None
                            if ph == 0 and zero(t):
                                for b in range(4):
                                    pe.matmul(bank[2 + b][:, 0:D + 2], zr[:], zw[:], start=True, stop=False, skip_group_check=True)
                            if ph == 1 and not zero(t):
                                pe.wait_ge(e_full, done(B - 1))
                                pe.wait_ge(phi_full, done(Q - 2))
                                for b in range(4):
                                    last = pe.transpose(bank[2][:, b * R:(b + 1) * R], EB[:, 1 - par, b * P:(b + 1) * P], ident[0:R, 0:R])
                                last.then_inc(e_used, 1)
                            work = first or not (isinstance(u, int) and u == 0)
                            ue = u if first else u - 1
                            edges.par = 1 - par
                            if not last_(t):
                                pe.wait_ge(xtm_full, done(B))
                                pe.wait_ge(pj_used, done(B - 1))
                                products(bank[0], par, B, WH, WL)
                                pe.matmul(bank[0][0:R, :], ones3[:], b3[kq][:], start=False, stop=True).then_inc(pj_full, 1)
                            if first:
                                pe.wait_ge(oht_done, done(u))
                                pe.wait_ge(sd_kept, done(u - 1))
                            elif work:
                                pe.wait_ge(r_full, done(u - 1))
                            if work:
                                edges(ue, 0, 2, regs)
                            if not last_(t):
                                pe.wait_ge(e_full, done(B - 1))
                                products(bank[1], par, B, MH_, ML)
                                pe.matmul(bank[1][0:R, :], ones3[:], b3["c" + kq][:], start=False, stop=True).then_inc(u2_full, 1)
                            if work:
                                edges(ue, 2, 4, regs)
                            if ph == 0 and not zero(t):
                                pe.wait_ge(e_full, done(B - 1))
                                if first:
                                    pe.wait_ge(el_full, done(B - 1 - g * T))
                                for b in range(4):
                                    to, cols = bank[2 + b][:, 0:D + 2 if first else D + 1], slice(b * P, (b + 1) * P)
                                    kw = dict(start=False, skip_group_check=True)
                                    if first:
                                        pe.matmul(to, one_pass(EBH[:, 1 - par, cols]), one_pass(XH[:, 1 - par, :]), stop=False, **kw)
                                        pe.matmul(to, one_pass(EBH[:, 1 - par, cols]), one_pass(XL[:, 1 - par, :]), stop=False, **kw)
                                        last = pe.matmul(to, one_pass(EBL[:, 1 - par, cols]), one_pass(XH[:, 1 - par, :]), stop=last_(t), **kw)
                                    else:
                                        last = pe.matmul(to, EB[:, 1 - par, cols], row(XN, t - 1), stop=last_(t), **kw)
                                last.then_inc(e_used, 1)
                            if ph == 1 and not zero(t):
                                pe.wait_ge(phi_full, done(Q - 1))
                                pe.wait_ge(att_used, done(Q - 2))
                                if first:
                                    pe.wait_ge(pl_full, done(Q - 1))
                                parts = [(one_pass(p_[:]), one_pass(k_[:])) for p_, k_ in ((PTH, KVH), (PTH, KVL), (PTL, KVH))] if first else [(PT, KVO)]
                                for h in range(2):
                                    for n, (mb, (p_, k_)) in enumerate((mb, part) for mb in range(2) for part in parts):
                                        last = pe.matmul(bank[3 + h][0:R, 0:D + 2 if first else D + 1], p_[:, 2 * h + mb, :], k_[:, 2 * h + mb, :],
                                                         start=(n == 0), stop=(n == 2 * len(parts) - 1))
                                last.then_inc(att_full, 1)
                        return tile

                    for g in (g0, g0 + 1):
                        setup(g)
                        run(pe, g, 0, make(0, g))
                        finish_keys(g)
                        pe.wait_ge(w_split, g + 1)
                        run(pe, g, 1, make(1, g))
                    if not first:
                        pe.wait_ge(r_full, done(HALVES - 1))
                        edges.par = 1
                        edges(HALVES - 1, 0, 4, None)

                @block.scalar
                def _(act):
                    if first:
                        for s_ in (eh_full, ph_full, xtm_full, pj_used, nsq_full, e_full, phi_full):
                            act.sem_inc(s_, 2)

                    def setup(g):
                        act.wait_ge(u2_full, done(2 * g * T - 1))
                        act.wait_ge(wk_in, 16 * (g + 1))
                        act.activation(one_pass(WH[:]), WS["k"][:], ACT.Copy).then_inc(w_hi, 1)
                        act.wait_ge(set_pe, SPE * g + 2)
                        for h in range(2):
                            last = act.activation(WTs["q"][:, 2 * h:2 * h + 2, :], bank[2 + h][:].rearrange("p (c d) -> p c d", c=2), ACT.Copy)
                        last.then_inc(set_a, 1)
                        act.wait_ge(set_pe, SPE * g + 4)
                        for o in range(DT):
                            last = act.activation(one_pass(MH_[:, o, :]), bank[o][:], ACT.Copy, scale=SCALE)
                        last.then_inc(w_hi, 1)
                        act.wait_ge(set_pe, SPE * g + 6)
                        for o in range(DT):
                            last = act.activation(S0[:, o, :], bank[2 + o][:], ACT.Copy, scale=SCALE)
                        last.then_inc(set_a, 1)
                        act.wait_ge(set_pe, SPE * g + 8)

                    def queries(g):
                        act.wait_ge(u2_full, done((2 * g + 1) * T - 1))
                        act.wait_ge(set_a, SA * g + 2)
                        act.activation(one_pass(WH[:]), S1[:], ACT.Copy).then_inc(w_hi, 1)
                        act.activation(one_pass(MH_[:]), S0[:], ACT.Copy).then_inc(w_hi, 1)

                    def stage(t, par, B):
                        act.wait_ge(u2_full, done(B - (1 if zero(t) else 2)))
                        act.activation(one_pass(xtm[:, par]), XNT[:, :, bass.ds(t * R, R)], ACT.Copy).then_inc(xtm_full, 1)

                    def make(ph, g):
                        def tile(t, par, B, Q, u):
                            if zero(t):
                                stage(t, par, B)
                            if ph == 1 and not zero(t):
                                act.wait_ge(e_used, done(B - 1))
                                act.wait_ge(att_full, done(Q - 2))
                                act.activation(PT[:], bank[2][:, 0:4 * R].rearrange("p (b r) -> p b r", b=4), ACT.Copy,
                                               scale=1.0 / 16, bias=EPS_ATT).then_inc(phi_full, 1)
                                if first:
                                    act.wait_ge(phi_full, done(Q - 1))
                                    act.activation(one_pass(PTH[:]), PT[:], ACT.Copy).then_inc(ph_full, 1)
                            if not last_(t):
                                act.wait_ge(pj_full, done(B))
                                act.wait_ge(e_used, done(B - (1 if zero(t) else 2)))
                                for h in range(2):
                                    last = act.activation(EB[:, par, h * D:(h + 1) * D], bank[0][0:R, h * D:(h + 1) * D], ACT.Square, scale=SCALE * 0.5 ** 0.5,
                                                          accum_out=sq[:, par, h:h + 1])
                                last.then_inc(pj_used, 1)
                                act.wait_ge(pj_used, done(B))
                                act.mul(nsq[:, par, :], sq[:, par, :], -1.0).then_inc(nsq_full, 1)
                                if not (isinstance(t, int) and t == T - 1):
                                    stage(t + 1, 1 - par, B + 1)
                                act.wait_ge(nsq_full, done(B))
                                act.wait_ge(u2_full, done(B))
                                for h in range(2):
                                    last = act.activation(EB[:, par, h * D:(h + 1) * D], bank[1][0:R, h * D:(h + 1) * D], ACT.Exp,
                                                          bias=nsq[:, par, h:h + 1])
                                last.then_inc(e_full, 1)
                                if first and ph == 0:
                                    act.wait_ge(e_full, done(B))
                                    act.activation(one_pass(EBH[:, par, :]), EB[:, par, :], ACT.Copy).then_inc(eh_full, 1)
                        return tile

                    for g in (g0, g0 + 1):
                        setup(g)
                        run(act, g, 0, make(0, g), 1)
                        queries(g)
                        run(act, g, 1, make(1, g), 1)

                @block.vector
                def _(v):
                    c = dve_steps.on(v)
                    if first:
                        for s_ in (el_full, pl_full, xtl_full, oht_done, sd_kept, r_full, att_used, rz_full, acc_half, o_used):
                            v.sem_inc(s_, 2)
                        for buf in (XH, XL, KVH, KVL):
                            v.memset(buf[:, :, D + 1:], 0.0)
                        c(v.tensor_copy(SIJ3[:, :, 0, :], SIJ[:]))
                        c(v.tensor_tensor(rest, SIJ[:], SIJ3[:, :, 0, :], ALU.subtract))
                        c(v.tensor_copy(SIJ3[:, :, 1, :], rest))
                        c(v.tensor_tensor(rest, rest, SIJ3[:, :, 1, :], ALU.subtract))
                        c(v.tensor_copy(SIJ3[:, :, 2, :], rest))
                        v.wait_ge(fin_pe, 1)
                        v.tensor_copy(projT[:], bank[5][:].rearrange("p (k m) -> p k m", k=DT)).then_inc(fin_v, 1)
                    for k in b3:
                        v.memset(b3[k][:], 0.0)
                    c(v.memset(ones3[:], 0.0))
                    for p_ in (0, 32, 64):
                        v.memset(ones3[p_:p_ + 1, :], 1.0)
                    v.wait_ge(c_in, 64 if first else 112)

                    def three(name, src_):
                        c(v.tensor_copy(b3[name][0:1, :], src_))
                        c(v.tensor_tensor(rr, src_, b3[name][0:1, :], ALU.subtract))
                        c(v.tensor_copy(mid[:], rr))
                        c(v.tensor_copy(b3[name][32:33, :], mid[:]))
                        c(v.tensor_tensor(rr, rr, mid[:], ALU.subtract))
                        c(v.tensor_copy(b3[name][64:65, :], rr))

                    def setup(g):
                        c(v.tensor_copy(bcp[:], bc[:, :, 4 * g:4 * g + 4]))
                        v.tensor_copy(BVB, bcp[:, 2, :].unsqueeze(2).to_broadcast([P, 4, P])).then_inc(set_v, 1)
                        v.wait_ge(wp_in, 48 * (g + 1))
                        three("k", brow[:, 0, :])
                        v.wait_ge(set_pe, SPE * g + 1)
                        for h in range(2):
                            last = v.tensor_copy(WTs["k"][:, 2 * h:2 * h + 2, :], bank[h][:].rearrange("p (c d) -> p c d", c=2))
                        last.then_inc(set_v, 1)
                        v.wait_ge(w_hi, 4 * g + 1)
                        v.tensor_tensor(one_pass(WL[:]), WS["k"][:], WH[:], ALU.subtract).then_inc(k_split, 1)
                        three("q", brow[:, 1, :])
                        v.wait_ge(set_pe, SPE * g + 3)
                        for i_ in range(2):
                            last = v.tensor_scalar(brow[:, i_, :], bank[4 + i_][0:1, :], SCALE, None, ALU.mult)
                        c(last)
                        v.sem_inc(set_v, 1)
                        v.wait_ge(w_hi, 4 * g + 2)
                        for o in range(DT):
                            last = v.scalar_tensor_tensor(out=one_pass(ML[:, o, :]), in0=bank[o][:], scalar=SCALE, in1=MH_[:, o, :], op0=ALU.mult, op1=ALU.subtract)
                        last.then_inc(set_v, 1)
                        three("ck", brow[:, 0, :])
                        v.wait_ge(set_pe, SPE * g + 6)
                        for h in range(2):
                            last = v.tensor_copy(WTs["v"][:, 2 * h:2 * h + 2, :], bank[4 + h][:].rearrange("p (c d) -> p c d", c=2))
                        last.then_inc(set_v, 1)
                        three("cq", brow[:, 1, :])
                        v.wait_ge(set_pe, SPE * g + 8)
                        v.tensor_copy(BVWO, bank[0][:])
                        for h in range(2):
                            last = v.tensor_copy(WVO[:, 2 * h:2 * h + 2, :], bank[2 + h][:].rearrange("p (o d) -> p o d", o=2))
                        last.then_inc(set_v, 1)

                    def lows(g):
                        v.wait_ge(w_hi, 4 * (g + 1))
                        v.tensor_tensor(one_pass(WL[:]), S1[:], WH[:], ALU.subtract)
                        v.tensor_tensor(one_pass(ML[:]), S0[:], MH_[:], ALU.subtract).then_inc(w_split, 1)

                    def tile_low(t, par, B):
                        v.wait_ge(xtm_full, done(B))
                        v.tensor_tensor(one_pass(xtl[:, par]), XNT[:, :, bass.ds(t * R, R)], xtm[:, par], ALU.subtract).then_inc(xtl_full, 1)

                    def finish_keys(g):
                        v.wait_ge(e_used, done((2 * g + 1) * T - 1))
                        v.wait_ge(pj_used, done((2 * g + 1) * T - 1))
                        v.wait_ge(e_full, done((2 * g + 1) * T - 1))
                        for b in range(4):
                            last = v.scalar_tensor_tensor(out=KVX[:, b, :], in0=bank[2 + b][:, 0:D + 1], scalar=1.0 / 16, in1=CSE[:],
                                                          op0=ALU.mult, op1=ALU.add)
                        last.then_inc(fin_v, 1)
                        v.wait_ge(fin_pe, 1 + 2 * g + 1)
                        for h in range(2):
                            last = v.tensor_copy(KVXT[:, 2 * h:2 * h + 2, :], bank[h][:].rearrange("p (o m) -> p o m", o=2))
                        last.then_inc(fin_v, 1)
                        lows(g)
                        v.wait_ge(fin_pe, 1 + 2 * g + 2)
                        for b in range(4):
                            v.scalar_tensor_tensor(out=KVO[:, b, 0:D], in0=BVWO[:, (b // 2) * D:(b // 2 + 1) * D], scalar=KVX[:, b, D:D + 1],
                                                   in1=bank[2 + b][:, 0:D], op0=ALU.mult, op1=ALU.add)
                        last = v.tensor_copy(KVO[:, :, D:D + 1], KVX[:, :, D:D + 1])
                        if first:
                            c(last)
                            c(v.tensor_copy(one_pass(KVH[:, :, 0:D + 1]), KVO[:]))
                            last = v.tensor_tensor(one_pass(KVL[:, :, 0:D + 1]), KVO[:], KVH[:, :, 0:D + 1], ALU.subtract)
                        last.then_inc(fin_v, 1)

                    def targets(u):
                        v.wait_ge(rb_in, 16 * (u + 1))
                        v.tensor_scalar(OHT[:], RB[:], iota_p[0:R, :], None, ALU.is_equal).then_inc(oht_done, 1)

                    def sums(u, regs, k0, k1):
                        for k in range(k0, k1):
                            v.wait_ge(o_full, 4 * u + k + 1)
                            v.wait_ge(o_used, done(4 * u + k - 1))
                            acc = GACC[0:R, bass.ds(regs[k], 1), :].rearrange("r a c -> r (a c)")
                            v.tensor_tensor(acc, bank[6 + k % 2][0:R, 0:265], acc, ALU.add).then_inc(o_used, 1)

                    def make(ph, g):
                        def tile(t, par, B, Q, u):
                            if zero(t):
                                tile_low(t, par, B)
                            if first and ph == 1 and not zero(t):
                                v.wait_ge(ph_full, done(Q - 1))
                                v.tensor_tensor(one_pass(PTL[:]), PT[:], PTH[:], ALU.subtract).then_inc(pl_full, 1)
                            sums_due = not first and not (isinstance(u, int) and u == 0)
                            if first:
                                v.wait_ge(sd_full, done(u))
                                v.tensor_reduce(SD[:, bass.ds(4 * u, 4), :], bank[6][:, 0:96].rearrange("p (k s c) -> p k c s", s=3, c=2 * GH),
                                                AX.X, ALU.add).then_inc(sd_kept, 1)
                                if not (isinstance(u, int) and u == HALVES - 1):
                                    targets(u + 1)
                            else:
                                if sums_due:
                                    regs = steps_tiles(mybir.EngineType.DVE, u - 1)
                                    sums(u - 1, regs, 0, 2)
                                if not (isinstance(u, int) and u < 2):
                                    v.wait_ge(o_full, 4 * (u - 1))
                                v.wait_ge(g_in[par], (64 * (u - par) // 2 if isinstance(u, int) else 32 * (u - par)) + 64)
                                rel4 = relT[:, bass.ds(4 * u, 4)].unsqueeze(2).to_broadcast([P, 4, R])
                                v.tensor_tensor(OH[:, par], iota_f[:, 0:R].unsqueeze(1).to_broadcast([P, 4, R]), rel4, ALU.is_equal)
                                at4 = AT[:, bass.ds(4 * u, 4), :]
                                v.tensor_copy(RS[:, par, :, D:], at4)
                                for k in range(4):
                                    last = v.tensor_tensor(RS[:, par, k, 0:D].rearrange("p (h d) -> p h d", h=GH),
                                                           G[par][:, k, :].rearrange("p (h d) -> p h d", h=GH),
                                                           AT[:, bass.ds(4 * u + k, 1), 0:GH].rearrange("p a h -> p (a h)").unsqueeze(2).to_broadcast([P, GH, DH]), ALU.mult)
                                last.then_inc(r_full, 1)
                                if sums_due:
                                    sums(u - 1, regs, 2, 4)
                            if not (isinstance(t, int) and t >= T - 1):
                                tile_low(t + 1, 1 - par, B + 1)
                            if first and ph == 0 and not last_(t):
                                v.wait_ge(eh_full, done(B - g * T))
                                v.tensor_copy(one_pass(XH[:, par, 0:D + 1]), row(XN, t)).then_inc(xh_full, 1)
                                v.wait_ge(xh_full, B - g * T + 1)
                                v.tensor_tensor(one_pass(XL[:, par, 0:D + 1]), row(XN, t), XH[:, par, 0:D + 1], ALU.subtract)
                                v.tensor_tensor(one_pass(EBL[:, par, :]), EB[:, par, :], EBH[:, par, :], ALU.subtract).then_inc(el_full, 1)
                            if ph == 1 and not zero(t):
                                v.wait_ge(att_full, done(Q - 1))
                                v.reciprocal(rz[:, 0:1], bank[3][0:R, D:D + 1])
                                v.reciprocal(rz[:, 1:2], bank[4][0:R, D:D + 1]).then_inc(rz_full, 1)
                                v.wait_ge(rz_full, done(Q - 1))
                                acc = row(ACC, t - 1)
                                v.scalar_tensor_tensor(out=acc, in0=bank[3][0:R, 0:D], scalar=rz[:, 0:1], in1=acc,
                                                       op0=ALU.mult, op1=ALU.add).then_inc(acc_half, 1)
                                v.wait_ge(acc_half, done(Q - 1))
                                v.scalar_tensor_tensor(out=acc, in0=bank[4][0:R, 0:D], scalar=rz[:, 1:2], in1=acc,
                                                       op0=ALU.mult, op1=ALU.add).then_inc(att_used, 1)
                        return tile

                    if first:
                        targets(0)
                    for g in (g0, g0 + 1):
                        setup(g)
                        if g == g0:
                            v.wait_ge(p_ready, 2 if first else 3)
                        run(v, g, 0, make(0, g), 1)
                        finish_keys(g)
                        run(v, g, 1, make(1, g), 1)
                    if not first:
                        sums(HALVES - 1, steps_tiles(mybir.EngineType.DVE, HALVES - 1), 0, 4)

        mixer_block(True)
        AT = sb("AT", [P, STEPS, 9])

        tr = sem("tr"); ev_v = sem("ev_v"); ev_a = sem("ev_a"); ex_in = sem("ex_in"); ex_done = sem("ex_done")
        with ExitStack() as ctx:
            big = lambda name: sb(name, [P, GH, SB * P], ctx=ctx)
            XS, SI, SS, M, M2 = big("XS"), big("SI"), big("SS"), big("M"), big("M2")
            D0L = sb("D0L", [P, SB * P + 1], ctx=ctx)
            X0 = sb("X0", [P, GH, SB], ctx=ctx)
            CI = sb("CI", [P, SB, GH], ctx=ctx)
            TL = sb("TL", [P, SB, GH], ctx=ctx)
            AL = sb("AL", [P, SB], ctx=ctx)
            ALB = sb("ALB", [P, SB, GH], ctx=ctx)
            TR = sb("TR", [GH, SB * P], ctx=ctx)
            AR = sb("AR", [GH, SB * P], ctx=ctx)
            CR = sb("CR", [GH, SB * P + 1], ctx=ctx)
            FI = sb("FI", [P, SB * P], ctx=ctx)
            pen = PEN.rearrange("p b e -> p (b e)")
            d0 = D0.rearrange("p b e -> p (b e)")
            D00 = D0[:, :, 0:1].rearrange("p b e -> p (b e)")
            block = ctx.enter_context(nc.Block())

            @block.tensor
            def _(pe):
                def turn(banks, source):
                    for h in range(GH):
                        for b in range(SB):
                            last = pe.transpose(bank[banks + h][:, b * P:(b + 1) * P], source(b, h), ident[:])
                    last.then_inc(tr, 1)
                turn(0, lambda b, h: SJ[:, b * P:(b + 1) * P, h])
                turn(4, lambda b, h: SD[:, b * P:(b + 1) * P, h])
                pe.wait_ge(ev_v, 1)
                turn(0, lambda b, h: SD[:, b * P:(b + 1) * P, GH + h])
                n = 2
                for k in range(2):
                    pe.wait_ge(ev_v, n + 1)
                    if k == 0:
                        pe.wait_ge(ev_a, 1)
                    for b in range(SB):
                        pe.transpose(bank[4][0:GH, b * P:(b + 1) * P], TL[:, b, :], ident[:])
                        last = pe.transpose(bank[5][0:GH, b * P:(b + 1) * P], ALB[:, b, :], ident[:])
                    last.then_inc(tr, 1)
                    pe.wait_ge(ev_v, n + 2)
                    for b in range(SB):
                        last = pe.transpose(bank[6][:, b * GH:(b + 1) * GH], CR[:, k + b * P:k + (b + 1) * P], ident[0:GH, 0:GH])
                    last.then_inc(tr, 1)
                    n += 2

                def back(bank_, source):
                    for b in range(SB):
                        w = min(P, STEPS - b * P)
                        last = pe.transpose(bank[bank_][:, b * P:b * P + w], source(b)[0:w], ident[0:w, 0:w])
                    return last
                pe.wait_ge(ex_done, 1)
                for h in range(GH):
                    back(h, lambda b: XS[:, h, b * P:(b + 1) * P]).then_inc(tr, 1)
                pe.wait_ge(ev_v, n + 1)
                for h in range(GH):
                    back(4 + h, lambda b: SS[:, h, b * P:(b + 1) * P]).then_inc(tr, 1)
                pe.wait_ge(ev_v, n + 2)
                back(0, lambda b: FI[:, b * P:(b + 1) * P]).then_inc(tr, 1)

            @block.scalar
            def _(act):
                act.wait_ge(tr, 2)
                for h in range(GH):
                    last = act.activation(SI[:, h, :], bank[4 + h][:], ACT.Copy)
                last.then_inc(ev_a, 1)
                act.wait_ge(ex_in, 1)
                act.activation(XS[:], XS[:], ACT.Exp).then_inc(ex_done, 1)
                act.activation(SS[:], SS[:], ACT.Exp).then_inc(ex_done, 1)

            @block.vector
            def _(v):
                c = dve_steps.on(v)
                c(v.tensor_copy(D0L[:, 0:SB * P], d0))
                c(v.memset(D0L[:, 0:SB * P].rearrange("p (b e) -> p b e", b=SB)[:, :, 0:1], -BIG))
                v.memset(D0L[:, SB * P:], -BIG)
                v.tensor_reduce(AL[:], D0, AX.X, ALU.min)
                c(v.tensor_scalar(FI[:], d0, -1.0, None, ALU.is_lt))
                c(v.tensor_copy(ALB[:], AL[:].unsqueeze(2).to_broadcast([P, SB, GH])))
                v.wait_ge(tr, 1)
                for h in range(GH):
                    last = v.tensor_tensor(XS[:, h, :], bank[h][:], pen, ALU.add)
                last.then_inc(ev_v, 1)
                v.wait_ge(tr, 3)
                for h in range(GH):
                    last = v.tensor_copy(SS[:, h, :], bank[h][:])
                last.then_inc(ev_v, 1)
                v.wait_ge(ev_v, 2)
                c(v.tensor_copy(X0[:], XS[:].rearrange("p h (b e) -> p h b e", b=SB)[:, :, :, 0]))

                def ends(buf, e):
                    return buf[:].rearrange("p h (b e) -> p h b e", b=SB)[:, :, :, e]

                def scan(out_, data, way):
                    for h in range(GH):
                        if way > 0:
                            last = v.tensor_tensor_scan(out_[:, h, :], D0L[:, 0:SB * P], data[:, h, :], -BIG, ALU.add, ALU.max)
                        else:
                            last = v.tensor_tensor_scan(out_[:, h, :][:, ::-1], D0L[:, 1:][:, ::-1], data[:, h, :][:, ::-1], -BIG, ALU.add, ALU.max)
                    c(last)

                bh = lambda ap: ap.rearrange("p h b -> p b h")
                d00 = D00.unsqueeze(2).to_broadcast([P, SB, GH])
                scan(M, XS, 1)
                v.tensor_copy(TL[:], bh(ends(M, P - 1))).then_inc(ev_v, 1)
                v.wait_ge(tr, 4)
                v.tensor_copy(TR[:], bank[4][0:GH, :])
                c(v.tensor_copy(AR[:], bank[5][0:GH, :]))
                c(v.memset(CR[:, 0:1], -BIG))
                v.tensor_tensor_scan(CR[:, 1:], AR[:], TR[:], -BIG, ALU.add, ALU.max).then_inc(ev_v, 1)
                v.wait_ge(tr, 5)
                c(v.tensor_tensor(CI[:], bank[6][:, 0:SB * GH].rearrange("p (b h) -> p b h", b=SB), d00, ALU.add))
                c(v.tensor_tensor(ends(XS, 0), ends(XS, 0), CI[:].rearrange("p b h -> p h b"), ALU.max))
                scan(M, XS, 1)
                c(v.tensor_copy(ends(XS, 0), X0[:]))
                scan(M2, M, -1)
                v.tensor_tensor(TL[:], bh(ends(M2, 0)), d00, ALU.add).then_inc(ev_v, 1)
                v.wait_ge(tr, 6)
                c(v.tensor_copy(TR[:], bank[4][0:GH, :]))
                c(v.memset(CR[:, SB * P:], -BIG))
                v.tensor_tensor_scan(CR[:, 0:SB * P][:, ::-1], AR[:, ::-1], TR[:, ::-1], -BIG, ALU.add, ALU.max).then_inc(ev_v, 1)
                v.wait_ge(tr, 7)
                c(v.tensor_tensor(ends(M, P - 1), ends(M, P - 1), bank[6][:, 0:SB * GH].rearrange("p (b h) -> p h b", b=SB), ALU.max))
                scan(M2, M, -1)
                c(v.tensor_tensor(M2[:], M2[:], SS[:], ALU.max))
                v.wait_ge(ev_a, 1)
                for buf in (XS, M2, SS):
                    last = v.tensor_tensor(buf[:], buf[:], SI[:], ALU.add)
                c(last)
                for buf in (XS, M2, SS):
                    last = v.scalar_tensor_tensor(out=buf[:], in0=buf[:], scalar=0.2, in1=buf[:], op0=ALU.mult, op1=ALU.max)
                c(last)
                for buf in (XS, SS):
                    last = v.tensor_tensor(buf[:], buf[:], M2[:], ALU.subtract)
                last.then_inc(ex_in, 1)
                v.wait_ge(ex_done, 2)
                v.tensor_tensor(SS[:], SS[:], FI[:].unsqueeze(1).to_broadcast([P, GH, SB * P]), ALU.mult).then_inc(ev_v, 1)
                for h in range(GH):
                    v.wait_ge(tr, 8 + h)
                    last = v.tensor_copy(AT[:, :, h], bank[h][:, 0:STEPS])
                last.then_inc(ev_v, 1)
                for h in range(GH):
                    v.wait_ge(tr, 8 + GH + h)
                    v.tensor_copy(AT[:, :, GH + h], bank[4 + h][:, 0:STEPS])
                v.wait_ge(tr, 8 + 2 * GH)
                v.tensor_copy(AT[:, :, 2 * GH], bank[0][:, 0:STEPS])

        mixer_block(False)

        buf_dram = nc.dram_tensor("buf_dram", (XE * SLOT, D), F32).ap()
        y_dram = nc.dram_tensor("y_dram", (XE * SLOT, D), F32).ap()
        g_dram = nc.dram_tensor("g_dram", (N, D), F32).ap()
        sums_ready = sem("sums_ready"); g_out = sem("g_out"); g_in = sem("g_in"); gn_sq = sem("gn_sq")
        f_in = sem("f_in"); x2_in = sem("x2_in"); z_out = sem("z_out"); xn_used = sem("xn_used"); asr_ready = sem("asr_ready")
        nt_done = sem("nt_done"); st_n = sem("st_n"); sq_v = sem("sq_v"); sq_a = sem("sq_a"); gn_v = sem("gn_v"); gn_a = sem("gn_a")
        zset = sem("zset"); tri_ready = sem("tri_ready"); lg_done = sem("lg_done"); oh_ready = sem("oh_ready")
        cnt_done = sem("cnt_done"); sc_ready = sem("sc_ready"); sc_out = sem("sc_out")
        s_full = sem("s_full"); t_full = sem("t_full"); tt_full = sem("tt_full"); h_full = sem("h_full"); hr_full = sem("hr_full")
        m_full = sem("m_full"); m_used = sem("m_used"); n1_done = sem("n1_done"); n3_done = sem("n3_done"); loops5 = sem("loops5")

        def over_tiles(eng, body):
            body(0, 0)
            with eng.Fori(0, T // 2 - 1) as i:
                body(2 * i + 1, 1)
                body(2 * i + 2, 0)
            body(T - 2, 1)
            body(T - 1, 0)

        before = lambda t, n_: not isinstance(t, int) or t < n_
        zero = lambda t: isinstance(t, int) and t == 0

        with ExitStack() as ctx:
            mk = lambda name, shape, dt=F32: sb(name, shape, dt, ctx=ctx)
            NTB = mk("NTB", [R, T, D])
            RW = mk("RW", [R, 7, D])
            b1c = mk("b1c", [P, DT])
            W1s = mk("W1s", [P, DT, D]); W2s = mk("W2s", [P, DT, D])
            gw = mk("gw", [P, DT, XE]); gbr = mk("gbr", [R, XE])
            Z = mk("Z", [P, 8 * D])
            TRI = mk("TRI", [R, R])
            stg_ = mk("stg_", [R, 2, D])
            stT = mk("stT", [P, 2, DT, R])
            hT = mk("hT5", [P, 2, DT, R])
            s6 = mk("s6", [R, T, 6])
            sc = {k: mk("f_" + k, [R, T]) for k in ("mean", "dm", "var", "t1", "std", "rstd", "gn", "gr", "th", "gs", "mx", "sm", "prb", "idx", "pos", "kept", "sf", "drop")}
            q4 = {k: mk("q_" + k, [R, T, GH]) for k in ("as", "den", "r", "asr")}
            hm = mk("hm", [R, T])
            e8 = {k: mk("e_" + k, [R, T, XE]) for k in ("lg", "ex", "eq", "oh", "tot", "inc", "po")}
            one_t = mk("one_t", [R, T])
            sidx = mk("scidx", [R, T], I32)
            n = {k: b[:] for k, b in sc.items()}
            GN = GACC[0:R, :, 0:D]
            GN_ = GACC[0:R]
            GN4 = GN.rearrange("r t (h d) -> r t h d", h=GH)
            XX = XN[:, :, 0:D]
            wide = lambda k: RW[:, k, :].unsqueeze(1).to_broadcast([R, T, D])
            over = lambda ap: ap.unsqueeze(2).to_broadcast([R, T, D])
            block = ctx.enter_context(nc.Block())

            @block.sync
            def _(sp):
                sp.dma_start(NTB[:], ft_dram.rearrange("(t r) d -> r t d", r=R)).then_inc(f_in, 16)
                for k, a_ in enumerate((bo, g1, beta1, bias2, g2, beta2, gbc)):
                    sp.dma_start(RW[:, k, :], bcast(a_, R, D)).then_inc(f_in, 16)
                with nc.allow_non_contiguous_dma("bias column"):
                    sp.dma_start(b1c[:], bias1.rearrange("(o p) -> p o", p=P)).then_inc(f_in, 16)
                sp.dma_start(W1s[:], W1.rearrange("(k p) f -> p k f", p=P)).then_inc(f_in, 16)
                sp.dma_start(W2s[:], W2.rearrange("(k p) f -> p k f", p=P)).then_inc(f_in, 16)
                sp.dma_start(gw[:], gate_w.rearrange("(k p) e -> p k e", p=P)).then_inc(f_in, 16)
                sp.dma_start(gbr[:], bcast(gate_b, R, XE)).then_inc(f_in, 16)
                sp.wait_ge(zset, 1)
                for k in range(4):
                    sp.dma_start(buf_dram[k * 1024:(k + 1) * 1024, :].rearrange("(p j) d -> p (j d)", p=P), Z[:]).then_inc(z_out, 16)
                sp.wait_ge(xn_used, 1)
                sp.dma_start(XX, x.rearrange("(t r) d -> r t d", r=R)).then_inc(x2_in, 16)
                sp.wait_ge(sums_ready, 1)
                for h in range(GH):
                    sp.dma_start(bass.AP(g_dram.tensor, h * N * DH, [[DH, R], [R * DH, T], [1, DH]]), GN4[:, :, h, :]).then_inc(g_out, 16)
                sp.wait_ge(g_out, 16 * GH)
                sp.dma_start(GN, g_dram.rearrange("(t r) d -> r t d", r=R)).then_inc(g_in, 16)

            @block.gpsimd
            def _(pool):
                c = pool_steps.on(pool)
                pool.memset(Z[:], 0.0).then_inc(zset, 1)
                c(pool.memset(TRI[:], 1.0))
                pool.affine_select(out=TRI[:], in_=TRI[:], compare_op=ALU.is_ge, fill=0.0, base=0, pattern=[[1, R]],
                                   channel_multiplier=-1).then_inc(tri_ready, 1)
                pool.wait_ge(asr_ready, 1)
                pool.wait_ge(f_in, 16 * 13)
                nt4 = NTB[:].rearrange("r t (h d) -> r t h d", h=GH)
                pool.tensor_tensor(nt4, nt4, q4["asr"][:].unsqueeze(3).to_broadcast([R, T, GH, DH]), ALU.mult).then_inc(nt_done, 1)
                c(pool.tensor_tensor(GN4, GN4, q4["r"][:].unsqueeze(3).to_broadcast([R, T, GH, DH]), ALU.mult))
                pool.wait_ge(nt_done, 1)
                pool.tensor_tensor(GN, GN, NTB[:], ALU.add).then_inc(sums_ready, 1)
                pool.wait_ge(sc_ready, 1)
                pool.wait_ge(z_out, 64)
                for t in range(T):
                    pool.indirect_dma_start(out=buf_dram, out_offset=bass.IndirectOffsetOnAxis(ap=sidx[:, t:t + 1], axis=0),
                                            in_=ACC[:, t, :], in_offset=None, bounds_check=XE * SLOT - 1, oob_is_err=False).then_inc(sc_out, 16)
                pool.wait_ge(sc_out, 16 * T)

            @block.tensor
            def _(pe):
                pe.sem_inc(t_full, 2); pe.sem_inc(h_full, 2); pe.sem_inc(m_full, 2)
                pe.wait_ge(f_in, 16 * 13)
                pe.wait_ge(tri_ready, 1)

                def turn(t, par, pass_=0):
                    n_ = pass_ * T + t
                    pe.wait_ge(s_full, done(n_))
                    pe.wait_ge(tt_full, done(n_ - (1 if zero(t) else 2)))
                    for k in range(DT):
                        last = pe.transpose(bank[6 * par][:, k * P:k * P + R], stg_[:, par, k * P:(k + 1) * P], ident[0:R, 0:R])
                    last.then_inc(t_full, 1)

                def second(t, par):
                    pe.wait_ge(hr_full, done(t))
                    pe.wait_ge(m_used, done(t - 2))
                    for f in range(DT):
                        last = pe.matmul(bank[2 + 3 * par][0:R, 0:D], hT[:, par, f, :], W2s[:, f, :], start=(f == 0), stop=(f == 1))
                    last.then_inc(m_full, 1)

                def mlp(t, par):
                    if before(t, T - 1):
                        turn(t + 1, 1 - par)
                    pe.wait_ge(tt_full, done(t))
                    pe.wait_ge(hr_full, done(t - 2))
                    for f in range(DT):
                        for k in range(DT):
                            last = pe.matmul(bank[1 + 6 * par][:, f * P:f * P + R], W1s[:, k, f * P:(f + 1) * P], stT[:, par, k, :], start=(k == 0), stop=(k == 1))
                    last.then_inc(h_full, 1)
                    if not zero(t):
                        second(t - 1, 1 - par)
                turn(0, 0)
                over_tiles(pe, mlp)
                second(T - 1, 0)

                def gates(t, par):
                    if before(t, T - 1):
                        turn(t + 1, 1 - par, 1)
                    pe.wait_ge(tt_full, done(T + t))
                    for k in range(DT):
                        last = pe.matmul(bank[3][0:R, bass.ds(t * XE, XE)], stT[:, par, k, :], gw[:, k, :], start=(k == 0), stop=(k == 1))
                    last.then_inc(lg_done, 1)
                pe.sem_inc(lg_done, 2)
                turn(0, 0, 1)
                over_tiles(pe, gates)
                pe.wait_ge(oh_ready, 1)
                oh = e8["oh"][:].rearrange("r t e -> r (t e)")
                pe.matmul(bank[4][0:R, 0:T * XE], TRI[:], oh, start=True, stop=True)
                pe.matmul(bank[5][0:R, 0:T * XE], ones[0:R, 0:R], oh, start=True, stop=True).then_inc(cnt_done, 1)

            @block.scalar
            def _(act):
                act.sem_inc(s_full, 2); act.sem_inc(tt_full, 2); act.sem_inc(hr_full, 2)
                act.wait_ge(f_in, 16 * 13)
                act.wait_ge(sq_v, 1)
                act.activation(n["std"], n["t1"], ACT.Sqrt).then_inc(sq_a, 1)

                def stage(t, par, pass_=0):
                    n_ = pass_ * T + t
                    act.wait_ge((n1_done, n3_done)[pass_], done(t))
                    act.wait_ge(t_full, done(n_ - (1 if zero(t) else 2)))
                    act.activation(stg_[:, par, :], row(ACC, t), ACT.Copy).then_inc(s_full, 1)

                def turned(t, par, pass_=0):
                    n_ = pass_ * T + t
                    act.wait_ge(t_full, done(n_))
                    act.wait_ge((h_full, lg_done)[pass_], done(t - 2))
                    act.activation(stT[:, par], bank[6 * par][:, 0:D].rearrange("p (k r) -> p k r", k=DT)[:, :, 0:R], ACT.Copy).then_inc(tt_full, 1)

                def mlp(t, par):
                    if before(t, T - 2):
                        stage(t + 2, par)
                    if before(t, T - 1):
                        turned(t + 1, 1 - par)
                    act.wait_ge(h_full, done(t))
                    act.wait_ge(m_full, done(t - 2))
                    for f in range(DT):
                        last = act.activation(hT[:, par, f, :], bank[1 + 6 * par][:, f * P:f * P + R], ACT.Relu, bias=b1c[:, f:f + 1])
                    last.then_inc(hr_full, 1)
                stage(0, 0)
                stage(1, 1)
                turned(0, 0)
                over_tiles(act, mlp)
                act.wait_ge(sq_v, 2)
                act.activation(n["std"], n["t1"], ACT.Sqrt).then_inc(sq_a, 1)
                act.wait_ge(gn_v, 1)
                act.activation(GN, GN, ACT.Relu).then_inc(gn_a, 1)
                act.wait_ge(gn_a, 1)

                def square(t, par):
                    act.activation(row(NTB, t), row(GN_, t)[:, 0:D], ACT.Square, accum_out=sc["gn"][:, bass.ds(t, 1)]).then_inc(gn_sq, 1)
                over_tiles(act, square)
                act.wait_ge(gn_sq, T)
                act.activation(n["gr"], n["gn"], ACT.Sqrt).then_inc(gn_a, 1)
                act.wait_ge(gn_v, 2)
                act.activation(n["th"], n["gr"], ACT.Tanh).then_inc(gn_a, 1)
                act.wait_ge(sq_v, 3)
                act.activation(n["std"], n["t1"], ACT.Sqrt).then_inc(sq_a, 1)

                def gates(t, par):
                    if before(t, T - 2):
                        stage(t + 2, par, 1)
                    if before(t, T - 1):
                        turned(t + 1, 1 - par, 1)
                stage(0, 0, 1)
                stage(1, 1, 1)
                turned(0, 0, 1)
                over_tiles(act, gates)
                act.wait_ge(gn_v, 3)
                act.activation(e8["ex"][:], e8["lg"][:], ACT.Exp).then_inc(gn_a, 1)

            @block.vector
            def _(v):
                c = dve_steps.on(v)
                v.sem_inc(m_used, 2)
                v.memset(one_t[:], 1.0)
                c(v.tensor_scalar(hm[:], GACC[0:R, :, 264], -1.0, 1.0, ALU.mult, ALU.add))
                c(v.tensor_tensor(q4["as"][:], GACC[0:R, :, 260:264], hm[:].unsqueeze(2).to_broadcast([R, T, GH]), ALU.add))
                c(v.tensor_tensor(q4["den"][:], GACC[0:R, :, 256:260], q4["as"][:], ALU.add))
                c(v.tensor_scalar(q4["den"][:], q4["den"][:], MIN_NORM, None, ALU.max))
                c(v.reciprocal(q4["r"][:], q4["den"][:]))
                v.tensor_tensor(q4["asr"][:], q4["as"][:], q4["r"][:], ALU.mult).then_inc(asr_ready, 1)
                c(v.tensor_tensor(ACC[:], ACC[:], XX, ALU.add))
                v.sem_inc(xn_used, 1)
                v.wait_ge(f_in, 16 * 13)
                c(v.tensor_tensor(ACC[:], ACC[:], wide(0), ALU.add))

                def each(k, body):
                    with v.Fori(0, T // 2) as i:
                        c.enter(i, k)
                        body([2 * i, 2 * i + 1])
                    c.leave(T // 2)
                    body([T - 1])

                def stats(t, buf):
                    v.bn_stats(row(s6, t), row(buf, t)[:, 0:D]).then_inc(st_n, 1)

                def moments(eps, k):
                    v.wait_ge(st_n, k * T)
                    s = [s6[:, :, j] for j in range(6)]
                    c(v.tensor_tensor(n["mean"], s[1], s[4], ALU.add))
                    c(v.tensor_scalar(n["mean"], n["mean"], 0.5, None, ALU.mult))
                    c(v.tensor_tensor(n["dm"], s[1], s[4], ALU.subtract))
                    c(v.tensor_tensor(n["dm"], n["dm"], n["dm"], ALU.mult))
                    c(v.tensor_tensor(n["var"], s[2], s[5], ALU.add))
                    c(v.tensor_scalar(n["var"], n["var"], 1.0 / D, eps, ALU.mult, ALU.add))
                    v.scalar_tensor_tensor(out=n["t1"], in0=n["dm"], scalar=0.25, in1=n["var"], op0=ALU.mult, op1=ALU.add).then_inc(sq_v, 1)
                    v.wait_ge(sq_a, k)
                    c(v.reciprocal(n["rstd"], n["std"]))

                scalar = lambda name, t: sc[name][:, bass.ds(t, 1)]

                def centre(t, gain):
                    return v.scalar_tensor_tensor(out=row(ACC, t), in0=row(ACC, t), scalar=scalar("mean", t), in1=RW[:, gain, :],
                                                  op0=ALU.subtract, op1=ALU.mult)

                each(0, lambda ts: [stats(t, ACC) for t in ts])
                moments(1e-6, 1)
                v.sem_inc(n1_done, 2)

                def norm1(ts):
                    for t in ts:
                        last = centre(t, 1)
                    c(last)
                    for t in ts:
                        v.scalar_tensor_tensor(out=row(ACC, t), in0=row(ACC, t), scalar=scalar("rstd", t), in1=RW[:, 2, :],
                                               op0=ALU.mult, op1=ALU.add).then_inc(n1_done, 1)
                each(1, norm1)
                v.wait_ge(n1_done, done(T - 1))

                def add_mlp(t, par):
                    v.wait_ge(m_full, done(t))
                    v.tensor_tensor(row(ACC, t), bank[2 + 3 * par][0:R, 0:D], row(ACC, t), ALU.add).then_inc(m_used, 1)
                    v.tensor_tensor(row(XN, t)[:, 0:D], row(XN, t)[:, 0:D], RW[:, 5, :], ALU.add)
                    v.wait_ge(m_used, done(t))
                    v.tensor_tensor(row(ACC, t), row(ACC, t), RW[:, 3, :], ALU.add).then_inc(loops5, 1)
                    v.wait_ge(loops5, t + 1)
                    stats(t, ACC)
                v.wait_ge(x2_in, 16)
                over_tiles(v, add_mlp)
                v.wait_ge(g_in, 16)
                v.tensor_tensor(GN, GN, wide(6), ALU.add).then_inc(gn_v, 1)
                moments(1e-6, 2)

                def norm2(ts):
                    for t in ts:
                        last = centre(t, 4)
                    c(last)
                    for t in ts:
                        last = v.scalar_tensor_tensor(out=row(XN, t)[:, 0:D], in0=row(ACC, t), scalar=scalar("rstd", t), in1=row(XN, t)[:, 0:D],
                                                      op0=ALU.mult, op1=ALU.add)
                    c(last)
                each(2, norm2)
                v.wait_ge(gn_a, 2)
                v.tensor_scalar(n["gr"], n["gr"], MIN_NORM, None, ALU.max).then_inc(gn_v, 1)
                v.wait_ge(gn_v, 2)
                c(v.reciprocal(n["gs"], n["gr"]))
                v.wait_ge(gn_a, 3)
                c(v.tensor_scalar(n["th"], n["th"], MAXN, None, ALU.min))
                c(v.tensor_tensor(n["gs"], n["gs"], n["th"], ALU.mult))

                def add_graph(ts):
                    for t in ts:
                        last = v.scalar_tensor_tensor(out=row(XN, t)[:, 0:D], in0=row(GN_, t)[:, 0:D], scalar=scalar("gs", t), in1=row(XN, t)[:, 0:D],
                                                      op0=ALU.mult, op1=ALU.add)
                    c(last)
                    for t in ts:
                        stats(t, XN)
                each(1, add_graph)
                moments(1e-5, 3)
                v.sem_inc(n3_done, 2)

                def norm3(ts):
                    for t in ts:
                        v.tensor_scalar(row(ACC, t), row(XN, t)[:, 0:D], scalar("mean", t), scalar("rstd", t), ALU.subtract, ALU.mult).then_inc(n3_done, 1)
                each(0, norm3)

                v.wait_ge(lg_done, done(T - 1))
                lg, oh = e8["lg"][:], e8["oh"][:]
                c(v.tensor_tensor(lg, bank[3][0:R, 0:T * XE].rearrange("r (t e) -> r t e", e=XE), gbr[:].unsqueeze(1).to_broadcast([R, T, XE]), ALU.add))
                c(v.tensor_reduce(n["mx"], lg, AX.X, ALU.max))
                over8 = lambda ap: ap.unsqueeze(2).to_broadcast([R, T, XE])
                v.tensor_tensor(lg, lg, over8(n["mx"]), ALU.subtract).then_inc(gn_v, 1)
                v.wait_ge(gn_v, 3)
                c(v.tensor_scalar(e8["eq"][:], lg, 0.0, None, ALU.is_equal))
                c(v.scalar_tensor_tensor(out=e8["eq"][:], in0=e8["eq"][:], scalar=-float(XE), in1=iota_f[0:R, XE:2 * XE].unsqueeze(1).to_broadcast([R, T, XE]),
                                         op0=ALU.mult, op1=ALU.add))
                c(v.tensor_reduce(n["idx"], e8["eq"][:], AX.X, ALU.min))
                v.tensor_tensor(oh, iota_f[0:R, 0:XE].unsqueeze(1).to_broadcast([R, T, XE]), over8(n["idx"]), ALU.is_equal).then_inc(oh_ready, 1)
                v.wait_ge(gn_a, 4)
                c(v.tensor_reduce(n["sm"], e8["ex"][:], AX.X, ALU.add))
                c(v.reciprocal(n["prb"], n["sm"]))
                v.wait_ge(cnt_done, 1)
                v.wait_ge(oh_ready, 1)
                c(v.tensor_copy(e8["tot"][:], bank[5][0:R, 0:T * XE].rearrange("r (t e) -> r t e", e=XE)))
                for e in range(XE):
                    last = v.tensor_tensor_scan(e8["inc"][:, :, e], one_t[:], e8["tot"][:, :, e], 0.0, ALU.mult, ALU.add)
                c(last)
                c(v.tensor_tensor(e8["inc"][:], e8["inc"][:], e8["tot"][:], ALU.subtract))
                c(v.tensor_tensor(e8["po"][:], bank[4][0:R, 0:T * XE].rearrange("r (t e) -> r t e", e=XE), e8["inc"][:], ALU.add))
                c(v.tensor_tensor(e8["po"][:], e8["po"][:], oh, ALU.mult))
                c(v.tensor_reduce(n["pos"], e8["po"][:], AX.X, ALU.add))
                c(v.tensor_scalar(n["kept"], n["pos"], CAP + 0.5, None, ALU.is_lt))
                c(v.tensor_scalar(n["pos"], n["pos"], float(CAP), -1.0, ALU.min, ALU.add))
                c(v.scalar_tensor_tensor(out=n["sf"], in0=n["idx"], scalar=float(SLOT), in1=n["pos"], op0=ALU.mult, op1=ALU.add))
                c(v.tensor_scalar(n["drop"], n["kept"], -float(XE * SLOT), float(XE * SLOT), ALU.mult, ALU.add))
                c(v.tensor_tensor(n["drop"], n["drop"], n["sf"], ALU.add))
                c(v.tensor_copy(slot[:], n["sf"]))
                c(v.tensor_copy(sidx[:], n["drop"]))
                v.tensor_tensor(wgt[:], n["prb"], n["kept"], ALU.mult).then_inc(sc_ready, 1)

        layers.close()
        w_full = [sem("w_full0"), sem("w_full1")]; wh_full = sem("wh_full"); w1l_full = sem("w1l_full"); w2l_full = sem("w2l_full"); b_in = sem("b_in")
        bt_full = sem("bt_full"); bh_full = sem("bh_full"); bT_full = sem("bT_full"); y_full = sem("y_full")
        y_out = [sem("y_out0"), sem("y_out1")]; y_free = sem("y_free")
        hp_full = sem("hp_full"); hh_full = sem("hh_full"); hhi_full = sem("hhi_full"); hl_full = sem("hl_full")
        yp_full = sem("yp_full"); yy_full = sem("yy_full")
        with ExitStack() as ctx:
            mk = lambda name, shape, dt=F32: sb(name, shape, dt, ctx=ctx)
            NF, NQ, LASTQ, COLS = FF // P, 4, CAP - 3 * P, CAP + CAP % 2
            W1e = mk("W1e", [P, 2, DT, FF]); W1h = mk("W1h", [P, 2, DT, FF]); W1l = mk("W1l", [P, 2, DT, FF])
            W2e = mk("W2e", [P, 2, NF, D]); W2h = mk("W2h", [P, 2, NF, D]); W2l = mk("W2l", [P, 2, NF, D])
            b1e = mk("b1e", [P, XE, NF]); b2e = mk("b2e", [P, XE, D])
            BE = mk("BE", [P, 2, 4, D])
            BTh = mk("BTh", [P, DT, SLOT]); BTl = mk("BTl", [P, DT, SLOT])
            H = mk("H", [P, 4, COLS])
            Hh = mk("Hh", [P, NF, COLS]); Hl = mk("Hl", [P, NF, COLS])
            Y = mk("Y", [P, 2, 4, D])
            block = ctx.enter_context(nc.Block())

            def experts(eng, body):
                with eng.Fori(0, XE // 2 - 1) as i:
                    body(2 * i, 0, i)
                    body(2 * i + 1, 1, i)
                body(XE - 2, 0, XE // 2 - 1)
                body(XE - 1, 1, XE // 2 - 1)

            more = lambda e: not (isinstance(e, int) and e == XE - 1)

            @block.sync
            def _(sp):
                def load(e, par, i):
                    one = bass.ds(e, 1)
                    sp.wait_ge(w1l_full, done(e - 2))
                    sp.wait_ge(w2l_full, done(e - 2))
                    sp.wait_ge(bt_full, done(e - 2))
                    sp.dma_start(BE[:, par], buf_dram.rearrange("(e j p) d -> e p j d", e=XE, p=P)[one].rearrange("e p j d -> (e p) j d")).then_inc(w_full[par], 16)
                    sp.dma_start(W1e[:, par], w1.rearrange("e (k p) f -> e p k f", p=P)[one].rearrange("e p k f -> (e p) k f")).then_inc(w_full[par], 16)
                    sp.dma_start(W2e[:, par], w2.rearrange("e (c p) d -> e p c d", p=P)[one].rearrange("e p c d -> (e p) c d")).then_inc(w_full[par], 16)
                with nc.allow_non_contiguous_dma("bias columns"):
                    sp.dma_start(b1e[:], b1.rearrange("e (c p) -> p e c", p=P)).then_inc(b_in, 16)
                sp.dma_start(b2e[:], bass.AP(b2.tensor, 0, [[0, P], [D, XE], [1, D]])).then_inc(b_in, 16)
                experts(sp, load)
                sp.wait_ge(y_out[0], 16 * (XE // 2))
                sp.wait_ge(y_out[1], 16 * (XE // 2))

            @block.gpsimd
            def _(pool):
                def store(e, par, i):
                    pool.wait_ge(y_full, done(e))
                    rows = y_dram.rearrange("(e j p) d -> e p j d", e=XE, p=P)[bass.ds(e, 1)].rearrange("e p j d -> (e p) j d")
                    pool.dma_start(rows, Y[:, par]).then_inc(y_out[par], 16)
                    pool.wait_ge(y_out[par], 16 * (i + 1))
                    pool.sem_inc(y_free, 1)
                pool.memset(Y[:, :, 3, :], 0.0).then_inc(y_free, 2)
                experts(pool, store)

            @block.tensor
            def _(pe):
                pe.sem_inc(bt_full, 2); pe.sem_inc(hp_full, 8); pe.sem_inc(yp_full, 4)

                def transposes(e, par, i):
                    pe.wait_ge(w_full[par], 48 * (i + 1))
                    pe.wait_ge(bT_full, done(e - 1))
                    for k in range(DT):
                        for j in range(4):
                            last = pe.transpose(bank[k][:, j * P:(j + 1) * P], BE[:, par, j, k * P:(k + 1) * P], ident[:])
                    last.then_inc(bt_full, 1)

                def expert(e, par, i):
                    pe.wait_ge(bT_full, done(e))
                    pe.wait_ge(w1l_full, done(e))
                    for f in range(NF):
                        pe.wait_ge(hh_full, NF * e + f + 8 - 3)
                        parts = [(w_, b_, k) for w_, b_ in ((W1h, BTh), (W1h, BTl), (W1l, BTh)) for k in range(DT)]
                        for n, (w_, b_, k) in enumerate(parts):
                            last = pe.matmul(bank[2 + f % 4][:, 0:COLS], one_pass(w_[:, par, k, f * P:(f + 1) * P]), one_pass(b_[:, k, 0:COLS]),
                                             start=(n == 0), stop=(n == len(parts) - 1))
                        last.then_inc(hp_full, 1)
                    if more(e):
                        transposes(e + 1, 1 - par, i + par)
                    pe.wait_ge(w2l_full, done(e))
                    for j in range(NQ):
                        m = P if j < 3 else LASTQ
                        pe.wait_ge(yy_full, NQ * e + j + 4 - 1)
                        parts = [(h_, w_, f) for f in range(NF) for h_, w_ in ((Hh, W2h), (Hh, W2l), (Hl, W2h))]
                        for n, (h_, w_, f) in enumerate(parts):
                            if j == 0 and n % 3 == 0:
                                pe.wait_ge(hl_full, NF * e + f + 9)
                            last = pe.matmul(bank[6 + j % 2][0:m, 0:D], one_pass(h_[:, f, j * P:j * P + m]), one_pass(w_[:, par, f, :]),
                                             start=(n == 0), stop=(n == len(parts) - 1))
                        last.then_inc(yp_full, 1)
                transposes(0, 0, 0)
                experts(pe, expert)

            @block.scalar
            def _(act):
                act.sem_inc(bh_full, 2); act.sem_inc(hh_full, 8); act.sem_inc(wh_full, 4)

                def tokens(e):
                    act.wait_ge(bt_full, done(e))
                    for k in range(DT):
                        last = act.activation(one_pass(BTh[:, k, :]), bank[k][:], ACT.Copy)
                    last.then_inc(bh_full, 1)

                def highs(which, par, i):
                    act.wait_ge(w_full[par], 48 * (i + 1))
                    to, from_ = ((W1h, W1e), (W2h, W2e))[which]
                    act.activation(one_pass(to[:, par]), from_[:, par], ACT.Copy).then_inc(wh_full, 1)

                def expert(e, par, i):
                    for f in range(NF):
                        act.wait_ge(hp_full, NF * e + f + 9)
                        act.wait_ge(hl_full, NF * e + f + 5)
                        act.activation(H[:, f % 4, :], bank[2 + f % 4][:, 0:COLS], ACT.Relu, bias=b1e[:, bass.ds(e, 1), f:f + 1].rearrange("p a f -> p (a f)")).then_inc(hh_full, 1)
                        if f in (3, 5) and more(e):
                            highs((f - 3) // 2, 1 - par, i + par)
                    if more(e):
                        tokens(e + 1)
                highs(0, 0, 0)
                tokens(0)
                highs(1, 0, 0)
                act.wait_ge(b_in, 32)
                experts(act, expert)

            @block.vector
            def _(v):
                v.sem_inc(y_full, 2); v.sem_inc(yy_full, 4); v.sem_inc(w1l_full, 2); v.sem_inc(w2l_full, 2); v.sem_inc(bT_full, 2)
                v.sem_inc(hhi_full, 8); v.sem_inc(hl_full, 8)

                def tokens(e):
                    v.wait_ge(bh_full, done(e))
                    for k in range(DT):
                        last = v.tensor_tensor(one_pass(BTl[:, k, :]), bank[k][:], BTh[:, k, :], ALU.subtract)
                    last.then_inc(bT_full, 1)

                def lows(which, e, par, quarters):
                    v.wait_ge(wh_full, 2 * e + 5 + which)
                    to, from_, high, count = ((W1l, W1e, W1h, w1l_full), (W2l, W2e, W2h, w2l_full))[which]
                    for q in quarters:
                        part = lambda w_: w_[:, par].rearrange("p a b -> p (a b)")[:, q * DT * FF // 4:(q + 1) * DT * FF // 4]
                        last = v.tensor_tensor(one_pass(part(to)), part(from_), part(high), ALU.subtract)
                    if quarters[-1] == 3:
                        last.then_inc(count, 1)

                def expert(e, par, i):
                    v.wait_ge(yp_full, NQ * e + 4)
                    for f in range(NF):
                        v.wait_ge(hh_full, NF * e + f + 9)
                        v.tensor_copy(one_pass(Hh[:, f, :]), H[:, f % 4, :]).then_inc(hhi_full, 1)
                        v.wait_ge(hhi_full, NF * e + f + 9)
                        v.tensor_tensor(one_pass(Hl[:, f, :]), H[:, f % 4, :], Hh[:, f, :], ALU.subtract).then_inc(hl_full, 1)
                    if more(e):
                        tokens(e + 1)
                    v.wait_ge(y_free, done(e - 2))
                    for j in range(NQ):
                        m = P if j < 3 else LASTQ
                        v.wait_ge(yp_full, NQ * e + j + 5)
                        v.tensor_tensor(Y[0:m, par, j, :], bank[6 + j % 2][0:m, 0:D], b2e[0:m, bass.ds(e, 1), :].rearrange("p a d -> p (a d)"), ALU.add).then_inc(yy_full, 1)
                        if j < 2 and more(e):
                            lows(0, e + 1, 1 - par, (2 * j, 2 * j + 1))
                            lows(1, e + 1, 1 - par, (2 * j, 2 * j + 1))
                    v.wait_ge(yy_full, NQ * e + NQ + 4)
                    v.sem_inc(y_full, 1)
                lows(0, 0, 0, range(4))
                tokens(0)
                lows(1, 0, 0, range(4))
                v.wait_ge(b_in, 32)
                experts(v, expert)

        GT = 5
        yg_in = [sem(f"yg_in{k}") for k in range(T // GT)]; yw_full = sem("yw_full"); ot_done = sem("ot_done"); ot_out = sem("ot_out")
        alt_seen = sem("alt_seen")
        with ExitStack() as ctx:
            mk = lambda name, shape, dt=F32: sb(name, shape, dt, ctx=ctx)
            YG = mk("YG", [R, T, D])
            yw = mk("yw", [R, T, D]); alt = mk("alt", [R, 2, GT, D]); neg_ = mk("neg_", [R, 2, GT, D])
            fin = mk("fin", [R, 2, GT, D], I32)
            block = ctx.enter_context(nc.Block())

            @block.gpsimd
            def _(pool):
                for t in range(T):
                    pool.indirect_dma_start(out=YG[:, t, :], out_offset=None, in_=y_dram,
                                            in_offset=bass.IndirectOffsetOnAxis(ap=slot[:, t:t + 1], axis=0)).then_inc(yg_in[t // GT], 16)

            @block.scalar
            def _(act):
                for k in range(T // GT):
                    act.wait_ge(yg_in[k], 16 * GT)
                    for t in range(GT * k, GT * (k + 1)):
                        last = act.activation(yw[:, t, :], YG[:, t, :], ACT.Copy, scale=wgt[:, t:t + 1])
                    last.then_inc(yw_full, 1)

            @block.vector
            def _(v):
                c = dve_steps.on(v)
                for k in range(T // GT):
                    v.wait_ge(yw_full, k + 1)
                    ts, par = slice(GT * k, GT * (k + 1)), k % 2
                    y = yw[:, ts, :]
                    v.tensor_scalar(fin[:, par], y, 0.0, 0.0, ALU.mult, ALU.is_equal)
                    v.tensor_scalar(alt[:, par], y, 0.0, 1.0e4, ALU.max, ALU.min)
                    c(v.tensor_scalar(neg_[:, par], y, 0.0, -1.0e4, ALU.min, ALU.max))
                    c(v.tensor_tensor(alt[:, par], alt[:, par], neg_[:, par], ALU.add))
                    v.sem_inc(alt_seen, 1)
                    c(v.copy_predicated(alt[:, par], fin[:, par], y))
                    v.tensor_tensor(XN[:, ts, 0:D], XN[:, ts, 0:D], alt[:, par], ALU.add).then_inc(ot_done, 1)

            @block.sync
            def _(sp):
                for k in range(T // GT):
                    sp.wait_ge(ot_done, k + 1)
                    sp.dma_start(out[GT * k * R:GT * (k + 1) * R, :].rearrange("(t r) d -> r t d", r=R), XN[:, GT * k:GT * (k + 1), 0:D]).then_inc(ot_out, 16)
                sp.wait_ge(ot_out, 16 * (T // GT))


_INS = ['x', 'src', 'dst', 'L0_gnn_W', 'L0_gnn_b_lin', 'L0_gnn_att', 'L0_gnn_b_conv', 'L0_mix_Wq', 'L0_mix_bq',
        'L0_mix_Wk', 'L0_mix_bk', 'L0_mix_Wv', 'L0_mix_bv', 'L0_mix_Wo', 'L0_mix_bo', 'L0_mix_proj', 'L0_mix_W1',
        'L0_mix_bias1', 'L0_mix_W2', 'L0_mix_bias2', 'L0_mix_g1', 'L0_mix_beta1', 'L0_mix_g2', 'L0_mix_beta2',
        'L0_ffn_gate_w', 'L0_ffn_gate_b', 'L0_ffn_w1', 'L0_ffn_b1', 'L0_ffn_w2', 'L0_ffn_b2']
_OUTS = [((3125, 256), 'float32')]


def kernel(**inputs):
    import numpy as _np
    import concourse.bacc as _bacc
    from concourse import mybir as _mybir
    from concourse.bass_utils import run_bass_kernel_spmd as _run

    nc = _bacc.Bacc("TRN2", target_bir_lowering=False, num_devices=1)
    arrays, args = {}, []
    for name in _INS:
        a = _np.ascontiguousarray(inputs[name])
        arrays[f"in_{name}_dram"] = a
        args.append(nc.dram_tensor(f"in_{name}_dram", a.shape, _mybir.dt.from_np(a.dtype), kind="ExternalInput").ap())
    for i, (shape, dtype) in enumerate(_OUTS):
        dt = _mybir.dt.from_np(_np.dtype(dtype))
        args.append(nc.dram_tensor(f"out_{i}_dram", shape, dt, kind="ExternalOutput").ap())
    build(nc, *args)
    r = _run(nc, [arrays], core_ids=[0])
    got = tuple(r.results[0][f"out_{i}_dram"] for i in range(len(_OUTS)))
    return got[0]
```
